# Optimizing a Trainium2 kernel written in Bass

```python
import numpy as np
import jax
import jax.numpy as jnp

def _softmax(x, axis=-1):
    return jax.nn.softmax(x, axis=axis)

def _gelu(x):
    return jax.nn.gelu(x, approximate=True)

def _silu(x):
    return jax.nn.silu(x)

def _sigmoid(x):
    return jax.nn.sigmoid(x)

def _layernorm(x, axis=-1, eps=1e-05):
    m = jnp.mean(x, axis=axis, keepdims=True)
    v = jnp.var(x, axis=axis, keepdims=True)
    return (x - m) / jnp.sqrt(v + eps)

def _scatter_add(tgt, idx, src, axis=0):
    return tgt.at[idx].add(src)

def _segment_sum(src, seg, n):
    return jax.ops.segment_sum(src, seg, n)
kernel_name = 'mk_adj_ffn_d1_adj_r2_e92dcb'

def setup_inputs(seed: int=0):
    np.random.seed(seed)
    _w = jnp.asarray

    def _rec_inputs():
        import jax
        import jax.numpy as jnp
        _gk = jax.random.key(seed)
        x = -1.394e-06 + 0.9999 * jax.random.normal(jax.random.fold_in(_gk, 1), (4096, 256), jnp.float32)
        _w = (1.0 + jnp.arange(4096, dtype=jnp.float32)) ** (-0.5)
        _w = _w / _w.mean()
        _pij = jnp.clip(0.000976562 * _w[:, None] * _w[None, :], 0.0, 1.0)
        _a = jax.random.uniform(jax.random.fold_in(_gk, 2), (4096, 4096)) < _pij
        _a = jnp.logical_or(_a, jnp.eye(4096, dtype=bool))
        adj = _a
        return (x, adj)
    x, adj = _rec_inputs()

    def _L0_gnn_setup():
        import jax, jax.numpy as jnp
        import numpy as np
        import math
        N = 4096
        D_IN = 256
        LOCAL_D = 256
        GLOBAL_D = 256
        key = jax.random.key(seed)
        ks = jax.random.split(key, 16)
        s = 1.0 / math.sqrt(D_IN)
        adj = jax.random.bernoulli(ks[0], 0.01, (N, N))
        adj = adj | jnp.eye(N, dtype=bool)
        return {'adj_matrix': adj, 'x': jax.random.normal(ks[1], (N, D_IN), jnp.float32), 'masked_x': jax.random.normal(ks[2], (N, D_IN), jnp.float32), 'Wlq': jax.random.normal(ks[3], (D_IN, LOCAL_D), jnp.float32) * s, 'Wlk': jax.random.normal(ks[4], (D_IN, LOCAL_D), jnp.float32) * s, 'Wlv': jax.random.normal(ks[5], (D_IN, D_IN), jnp.float32) * s, 'blv': jax.random.normal(ks[6], (D_IN,), jnp.float32) * 0.01, 'Wgq': jax.random.normal(ks[7], (D_IN, GLOBAL_D), jnp.float32) * s, 'Wgk': jax.random.normal(ks[8], (D_IN, GLOBAL_D), jnp.float32) * s, 'Wgv': jax.random.normal(ks[9], (D_IN, D_IN), jnp.float32) * s, 'bgv': jax.random.normal(ks[10], (D_IN,), jnp.float32) * 0.01, 'Wes': jax.random.normal(ks[11], (D_IN, 1), jnp.float32) * s, 'Wev': jax.random.normal(ks[12], (D_IN, D_IN), jnp.float32) * s, 'bev': jax.random.normal(ks[13], (D_IN,), jnp.float32) * 0.01}
    _L0_gnn_all = _L0_gnn_setup()
    _L0_gnn_in = {k: v for k, v in _L0_gnn_all.items() if k in ('masked_x', 'Wlq', 'Wlk', 'Wlv', 'blv', 'Wgq', 'Wgk', 'Wgv', 'bgv', 'Wes', 'Wev', 'bev')}
    del _L0_gnn_all

    def _L0_ffn_setup():
        import jax, jax.numpy as jnp
        import numpy as np
        MICRO_BATCHES = 2
        TOP_K = 2
        D = 256
        E = 8
        B, S = (8, 4096)
        key = jax.random.key(seed)
        ks = jax.random.split(key, 12)
        s = 0.02
        return {'x': jax.random.normal(ks[0], (B, S, D), dtype=jnp.float32), 'ln_g': jnp.ones((D,), jnp.float32), 'ln_b': jnp.zeros((D,), jnp.float32), 'attn_w': jax.random.normal(ks[1], (D, D), jnp.float32) * s, 'attn_b': jnp.zeros((D,), jnp.float32), 'gate_w': jax.random.normal(ks[2], (E, D), jnp.float32) * s, 'fc1_w': jax.random.normal(ks[3], (E, 4 * D, D), jnp.float32) * s, 'fc1_b': jnp.zeros((E, 4 * D), jnp.float32), 'fc2_w': jax.random.normal(ks[4], (E, D, 4 * D), jnp.float32) * s, 'fc2_b': jnp.zeros((E, D), jnp.float32), 'next_w': jax.random.normal(ks[5], (D, D), jnp.float32) * s, 'next_b': jnp.zeros((D,), jnp.float32)}
    _L0_ffn_all = _L0_ffn_setup()
    _L0_ffn_in = {k: v for k, v in _L0_ffn_all.items() if k in ('ln_g', 'ln_b', 'attn_w', 'attn_b', 'gate_w', 'fc1_w', 'fc1_b', 'fc2_w', 'fc2_b', 'next_w', 'next_b')}
    del _L0_ffn_all
    return {'x': x, 'adj': adj, 'L0_gnn_masked_x': _L0_gnn_in['masked_x'], 'L0_gnn_Wlq': _L0_gnn_in['Wlq'], 'L0_gnn_Wlk': _L0_gnn_in['Wlk'], 'L0_gnn_Wlv': _L0_gnn_in['Wlv'], 'L0_gnn_blv': _L0_gnn_in['blv'], 'L0_gnn_Wgq': _L0_gnn_in['Wgq'], 'L0_gnn_Wgk': _L0_gnn_in['Wgk'], 'L0_gnn_Wgv': _L0_gnn_in['Wgv'], 'L0_gnn_bgv': _L0_gnn_in['bgv'], 'L0_gnn_Wes': _L0_gnn_in['Wes'], 'L0_gnn_Wev': _L0_gnn_in['Wev'], 'L0_gnn_bev': _L0_gnn_in['bev'], 'L0_ffn_ln_g': _L0_ffn_in['ln_g'], 'L0_ffn_ln_b': _L0_ffn_in['ln_b'], 'L0_ffn_attn_w': _L0_ffn_in['attn_w'], 'L0_ffn_attn_b': _L0_ffn_in['attn_b'], 'L0_ffn_gate_w': _L0_ffn_in['gate_w'], 'L0_ffn_fc1_w': _L0_ffn_in['fc1_w'], 'L0_ffn_fc1_b': _L0_ffn_in['fc1_b'], 'L0_ffn_fc2_w': _L0_ffn_in['fc2_w'], 'L0_ffn_fc2_b': _L0_ffn_in['fc2_b'], 'L0_ffn_next_w': _L0_ffn_in['next_w'], 'L0_ffn_next_b': _L0_ffn_in['next_b']}

def reference(x, adj, L0_gnn_masked_x, L0_gnn_Wlq, L0_gnn_Wlk, L0_gnn_Wlv, L0_gnn_blv, L0_gnn_Wgq, L0_gnn_Wgk, L0_gnn_Wgv, L0_gnn_bgv, L0_gnn_Wes, L0_gnn_Wev, L0_gnn_bev, L0_ffn_ln_g, L0_ffn_ln_b, L0_ffn_attn_w, L0_ffn_attn_b, L0_ffn_gate_w, L0_ffn_fc1_w, L0_ffn_fc1_b, L0_ffn_fc2_w, L0_ffn_fc2_b, L0_ffn_next_w, L0_ffn_next_b):
    import jax
    import jax.numpy as jnp

    def _L0_gnn_ref(adj_matrix, x, masked_x, Wlq, Wlk, Wlv, blv, Wgq, Wgk, Wgv, bgv, Wes, Wev, bev):
        import jax, jax.numpy as jnp
        import numpy as np
        import math
        N = 4096
        D_IN = 256
        LOCAL_D = 256
        GLOBAL_D = 256
        scale = 1.0 / math.sqrt(D_IN)
        x_bar = jnp.mean(x, axis=0, keepdims=True)
        lQ = masked_x @ Wlq
        lK = x @ Wlk
        lV = x @ Wlv + blv
        gQ = masked_x @ Wgq
        gK = x_bar @ Wgk
        gV = x_bar @ Wgv + bgv
        es = masked_x @ Wes
        eV = masked_x @ Wev + bev
        local_scores = lQ @ lK.T * scale
        local_scores = jnp.where(adj_matrix, local_scores, jnp.float32(-1000000000.0))
        global_scores = gQ @ gK.T * scale
        max_score = jnp.maximum(jnp.max(local_scores, axis=1, keepdims=True), jnp.maximum(global_scores, es))
        le = jnp.exp(local_scores - max_score)
        ge = jnp.exp(global_scores - max_score)
        ee = jnp.exp(es - max_score)
        denom = jnp.sum(le, axis=-1, keepdims=True) + ge + ee
        res = le / denom @ lV + ge / denom * gV + ee / denom * eV
        x_recon = jnp.maximum(res, masked_x)
        return x_recon

    def _L0_ffn_ref(x, ln_g, ln_b, attn_w, attn_b, gate_w, fc1_w, fc1_b, fc2_w, fc2_b, next_w, next_b):
        import jax, jax.numpy as jnp
        import numpy as np
        MICRO_BATCHES = 2
        TOP_K = 2
        D = 256
        E = 8
        B, S = (8, 4096)
        b, s, d = x.shape
        xf = x.reshape(b * s, d)
        mu = jnp.mean(xf, axis=-1, keepdims=True)
        var = jnp.var(xf, axis=-1, keepdims=True)
        normed = (xf - mu) / jnp.sqrt(var + 1e-05) * ln_g + ln_b
        x_attn = normed @ attn_w.T + attn_b + xf
        logits = x_attn @ gate_w.T
        _scores, _indices = jax.lax.top_k(logits, TOP_K)
        e = fc1_w.shape[0]
        t = b * s // (MICRO_BATCHES * e)
        tok = x_attn.reshape(MICRO_BATCHES, e, t, d)
        h = jnp.einsum('meti,ehi->meth', tok, fc1_w) + fc1_b[None, :, None, :]
        h = jax.nn.gelu(h, approximate=False)
        y = jnp.einsum('meth,edh->metd', h, fc2_w) + fc2_b[None, :, None, :]
        yf = y.reshape(b * s, d)
        out = jax.nn.gelu(yf @ next_w.T + next_b, approximate=False)
        return out.reshape(b, s, d)
    x = x + _L0_gnn_ref(adj, _layernorm(x, axis=-1), L0_gnn_masked_x, L0_gnn_Wlq, L0_gnn_Wlk, L0_gnn_Wlv, L0_gnn_blv, L0_gnn_Wgq, L0_gnn_Wgk, L0_gnn_Wgv, L0_gnn_bgv, L0_gnn_Wes, L0_gnn_Wev, L0_gnn_bev)
    x = x + _L0_ffn_ref(_layernorm(x, axis=-1)[None], L0_ffn_ln_g, L0_ffn_ln_b, L0_ffn_attn_w, L0_ffn_attn_b, L0_ffn_gate_w, L0_ffn_fc1_w, L0_ffn_fc1_b, L0_ffn_fc2_w, L0_ffn_fc2_b, L0_ffn_next_w, L0_ffn_next_b)[0]
    return x

_drawn_inputs = setup_inputs


def setup_inputs(seed=0):
    import zlib

    import numpy as np

    out = dict(_drawn_inputs(seed))
    spreads = {'L0_ffn_ln_g': (1.0, 0.6),
     'L0_ffn_ln_b': (0.0, 0.8),
     'L0_ffn_attn_b': (0.0, 0.8),
     'L0_ffn_fc1_b': (0.0, 0.8),
     'L0_ffn_fc2_b': (0.0, 0.639),
     'L0_ffn_next_b': (0.0, 0.665)}
    factors = {'L0_gnn_blv': 8.0,
     'L0_gnn_Wgq': 8.0,
     'L0_gnn_Wgk': 8.0,
     'L0_gnn_Wgv': 32.986,
     'L0_gnn_bgv': 50.249,
     'L0_gnn_bev': 50.219,
     'L0_ffn_attn_w': 8.0,
     'L0_ffn_fc1_w': 3.826,
     'L0_ffn_fc2_w': 3.6,
     'L0_ffn_next_w': 2.821}
    for name, (base, spread) in spreads.items():
        noise = np.random.default_rng([zlib.crc32(name.encode()), seed]).standard_normal(out[name].shape)
        drawn = base * np.exp(spread * noise) if base else spread * noise
        out[name] = jnp.asarray(drawn.astype(out[name].dtype))
    for name, factor in factors.items():
        out[name] = (out[name] * factor).astype(out[name].dtype)
    return out
```

```python
import concourse.bass as bass
from concourse import mybir
from contextlib import ExitStack

fp32 = mybir.dt.float32
fp32r = mybir.dt.float32r
uint8 = mybir.dt.uint8
ALU = mybir.AluOpType
ACT = mybir.ActivationFunctionType
AX = mybir.AxisListType

N, D, E, HID = 4096, 256, 8, 1024
P = 128
KD = D // P
NT = N // P
CH = 512
NC = N // CH
TG = CH // P
NG = N // CH
HB = HID // P
ROWU = D + 4
SCALE = 1.0 / 16.0
MASKED = -1.0e9 / SCALE
EPS = 1e-5
WLV, WEV, WATT, WNEXT = range(4)


def wait(engine, semaphore, value):
    if isinstance(value, int) and value <= 0:
        return
    engine.wait_ge(semaphore, value)


def split_product(nc, out, lhs, rhs, start=True, stop=True):
    pairs = [(lh, rh, k, len(lhs)) for k, (lh, rh) in enumerate(zip(lhs, rhs))]
    for (l_hi, l_lo), (r_hi, r_lo), k, n in pairs:
        nc.tensor.matmul(out, l_hi, r_hi, start=start and k == 0, stop=False)
        nc.tensor.matmul(out, l_hi, r_lo, start=False, stop=False)
        last = nc.tensor.matmul(out, l_lo, r_hi, start=False, stop=stop and k == n - 1)
    return last


def gnn_moe_kernel(nc, x, mx, mxT, adj, wlqT, wlkT, wgk, wgqT, wgv, bgv, wes, wlv, blv, wev, bev,
                   ln_g, ln_b, attn_wT, attn_b, next_wT, next_b, b1, b2, wffn, out):
    u_dram = nc.dram_tensor("u_scratch", (NT, P, ROWU), fp32, kind="Internal").ap()
    q_dram = nc.dram_tensor("q_scratch", (NT, P, KD, P), fp32, kind="Internal").ap()

    ctx = ExitStack()
    with ctx:
        def sb(stack, name, shape, dt=fp32):
            return stack.enter_context(nc.sbuf_tensor(name, shape, dt))

        def ps(stack, name, shape=(P, CH)):
            return stack.enter_context(nc.psum_tensor(name, list(shape), fp32))

        def sem(name):
            return ctx.enter_context(nc.semaphore(name))

        ident = sb(ctx, "ident", [P, P])
        w_hi = sb(ctx, "w_hi", [P, 4, KD, D], fp32r)
        w_lo = sb(ctx, "w_lo", [P, 4, KD, D], fp32r)
        blv_b = sb(ctx, "blv_b", [P, D])
        bev_b = sb(ctx, "bev_b", [P, D])
        gv_b = sb(ctx, "gv_b", [P, D])
        attc_b = sb(ctx, "attc_b", [P, D])
        nextb_b = sb(ctx, "nextb_b", [P, D])
        wes_b = sb(ctx, "wes_b", [P, D])
        wg_b = sb(ctx, "wg_b", [P, D])

        ab = ctx.enter_context(ExitStack())
        lnT_hi = sb(ab, "lnT_hi", [P, KD, N], fp32r)
        lnT_lo = sb(ab, "lnT_lo", [P, KD, N], fp32r)
        v_sp = sb(ab, "v_sp", [P, NT, 2 * D], fp32r)

        a = ab.enter_context(ExitStack())
        xg = sb(a, "xg", [P, 2, TG, D])
        lnf = sb(a, "lnf", [P, 2, TG, D])
        st6 = sb(a, "st6", [P, TG, 6])
        mv = sb(a, "mv", [P, 2, TG, 2])
        veps = sb(a, "veps", [P, TG])
        mhalf = sb(a, "mhalf", [P, TG])
        rstd = sb(a, "rstd", [P, 2, TG])
        mg = sb(a, "mg", [P, KD, CH])
        mg_hi = sb(a, "mg_hi", [P, KD, CH], fp32r)
        mg_lo = sb(a, "mg_lo", [P, KD, CH], fp32r)
        q_out = sb(a, "q_out", [P, KD, CH])
        qw_hi = sb(a, "qw_hi", [P, KD, D], fp32r)
        qw_lo = sb(a, "qw_lo", [P, KD, D], fp32r)
        qw_f = sb(a, "qw_f", [P, KD, D])
        wq_in = sb(a, "wq_in", [P, 2, KD, D])
        wgv_in = sb(a, "wgv_in", [P, KD, D])
        w_in = sb(a, "w_in", [P, 4, KD, D])
        lng = sb(a, "lng", [P, KD])
        lnb = sb(a, "lnb", [P, KD])
        xsum = sb(a, "xsum", [P, KD, NG])
        xbar = sb(a, "xbar", [P, KD])
        gk = sb(a, "gk", [P, KD])
        cols_b = sb(a, "cols_b", [P, 3, KD, P])
        ones = sb(a, "ones", [P, P])

        pa = ExitStack()
        tr_ps = [ps(pa, f"tr_ps{k}") for k in range(KD)]
        q_ps = [ps(pa, f"q_ps{k}") for k in range(KD)]
        qw_ps = ps(pa, "qw_ps", (P, CH))
        gk_ps = ps(pa, "gk_ps", (P, CH))
        row_ps = ps(pa, "row_ps", (P, CH))
        attc_ps = ps(pa, "attc_ps", (P, CH))

        x_in = [sem(f"x_in{i}") for i in range(2)]
        mg_in = sem("mg_in")
        wq_loaded, wg_loaded, w_loaded, rows_loaded = (sem(n) for n in ("wq_loaded", "wg_loaded", "w_loaded", "rows_loaded"))
        ident_ready, half_ready = sem("ident_ready"), sem("half_ready")
        stats_done, mv_ready, veps_ready, rstd_ready, ln_ready = (
            sem(n) for n in ("stats_done", "mv_ready", "veps_ready", "rstd_ready", "ln_ready"))
        vhi_ready, vlo_ready, tr_done, thi_ready, tlo_ready = (
            sem(n) for n in ("vhi_ready", "vlo_ready", "tr_done", "thi_ready", "tlo_ready"))
        mhi_ready, mlo_ready, q_done, q_copied, q_stored = (
            sem(n) for n in ("mhi_ready", "mlo_ready", "q_done", "q_copied", "q_stored"))
        qw_done, qwf_ready, qwhi_ready, qwlo_ready = (sem(n) for n in ("qw_done", "qwf_ready", "qwhi_ready", "qwlo_ready"))
        xs_ready, xbar_ready, gk_done, gk_ready, cols_ready, attcols_ready, rows_done, attc_done = (
            sem(n) for n in ("xs_ready", "xbar_ready", "gk_done", "gk_ready", "cols_ready", "attcols_ready", "rows_done", "attc_done"))
        attg_ready, whi_ready = sem("attg_ready"), sem("whi_ready")

        settled = {}

        def settle(engine):
            if engine.engine not in settled:
                settled[engine.engine] = sem(f"settled_{len(settled)}")
            engine.sem_inc(settled[engine.engine], 1)

        def kblocks(ap):
            return ap.rearrange("(k p) n -> p k n", p=P)

        def groups(eng, group):
            for pp in range(2):
                group(0, pp)
            with eng.Fori(1, NG // 2) as h:
                for pp in range(2):
                    group(h, pp)

        with nc.Block() as block:
            @block.sync
            def _(sp):
                sp.dma_start(xg[:, 0], x[0:CH].rearrange("(t p) d -> p t d", p=P)).then_inc(x_in[0], 16)
                for n, w in enumerate((wlqT, wlkT)):
                    sp.dma_start(wq_in[:, n], kblocks(w)).then_inc(wq_loaded, 16)
                sp.dma_start(xg[:, 1], x[CH:2 * CH].rearrange("(t p) d -> p t d", p=P)).then_inc(x_in[1], 16)
                sp.dma_start(mg[:, :, :], mxT[:, 0:CH].rearrange("(k p) q -> p k q", p=P)).then_inc(mg_in, 16)
                sp.dma_start(lng[:, :], ln_g).then_inc(rows_loaded, 16)
                sp.dma_start(lnb[:, :], ln_b).then_inc(rows_loaded, 16)
                for n, w in enumerate((wlv, wev, attn_wT, next_wT)):
                    sp.dma_start(w_in[:, n], kblocks(w)).then_inc(w_loaded, 16)
                sp.dma_start(wgv_in[:, :, :], kblocks(wgv)).then_inc(wg_loaded, 16)
                for dst, row in ((blv_b, blv), (bev_b, bev), (gv_b, bgv), (attc_b, attn_b), (nextb_b, next_b), (wes_b, wes)):
                    sp.dma_start(dst[:, :], row.partition_broadcast(P)).then_inc(rows_loaded, 16)

                sp.wait_ge(qw_done, 1)
                for n, w in enumerate((wgk, wgqT)):
                    sp.dma_start(wq_in[:, n], kblocks(w)).then_inc(wg_loaded, 16)

                def group(g, pp, more_x, more_m):
                    if more_x:
                        sp.wait_ge(ln_ready, g + 1)
                        settle(sp)
                        sp.dma_start(xg[:, pp], x[bass.ds((g + 2) * CH, CH)].rearrange("(t p) d -> p t d", p=P)).then_inc(x_in[pp], 16)
                    if more_m:
                        sp.wait_ge(mlo_ready, g + 1)
                        settle(sp)
                        sp.dma_start(mg[:, :, :], mxT[:, bass.ds((g + 1) * CH, CH)].rearrange("(k p) q -> p k q", p=P)).then_inc(mg_in, 16)
                    sp.wait_ge(q_copied, 2 * g + 2)
                    settle(sp)
                    for k in range(KD):
                        sp.dma_start(q_dram[bass.ds(g * TG, TG), :, k, :].rearrange("t p q -> p t q"),
                                     q_out[:, k, :].rearrange("p (t q) -> p t q", q=P)).then_inc(q_stored, 16)

                with sp.Fori(0, NG // 2 - 1) as h:
                    for pp in range(2):
                        group(2 * h + pp, pp, True, True)
                group(NG - 2, 0, False, True)
                group(NG - 1, 1, False, False)
                sp.wait_ge(q_stored, 32 * NG)

            @block.gpsimd
            def _(pool):
                nc.gpsimd.memset(ident[:, :], 0.0).then_inc(ident_ready, 1)
                nc.gpsimd.memset(mhalf[:, :], -0.5).then_inc(half_ready, 1)
                nc.gpsimd.memset(ones[:, :], 1.0).then_inc(half_ready, 1)
                pool.wait_ge(ident_ready, 1)
                nc.gpsimd.affine_select(out=ident[:, :], in_=ident[:, :], compare_op=ALU.not_equal, fill=1.0, base=0,
                                        pattern=[[-1, P]], channel_multiplier=1).then_inc(ident_ready, 1)
                pool.wait_ge(half_ready, 2)

                def group(h, pp):
                    g = 2 * h + pp
                    pool.wait_ge(mv_ready, 4 * g + 4)
                    settle(pool)
                    nc.gpsimd.tensor_scalar(veps[:, :], mv[:, pp, :, 1], EPS, 0.0, ALU.add, ALU.add).then_inc(veps_ready, 1)
                    pool.wait_ge(veps_ready, g + 1)
                    nc.gpsimd.tensor_tensor(out=rstd[:, pp, :], in0=veps[:, :], in1=mhalf[:, :], op=ALU.pow).then_inc(rstd_ready, 1)
                    pool.wait_ge(vhi_ready, g + 1)
                    nc.gpsimd.tensor_tensor(out=v_sp[:, bass.ds(g * TG, TG), D:2 * D], in0=lnf[:, pp],
                                            in1=v_sp[:, bass.ds(g * TG, TG), 0:D].bitcast(fp32), op=ALU.subtract).then_inc(vlo_ready, 1)
                groups(pool, group)

            @block.vector
            def _(dve):
                dve.wait_ge(qwhi_ready, 1)
                nc.vector.tensor_tensor(qw_lo[:, :, :], qw_f[:, :, :], qw_hi[:, :, :].bitcast(fp32), ALU.subtract).then_inc(qwlo_ready, 1)
                def group(h, pp):
                    g = 2 * h + pp
                    dve.wait_ge(x_in[pp], 16 * h + 16)
                    for j in range(TG):
                        nc.vector.bn_stats(st6[:, j], xg[:, pp, j]).then_inc(stats_done, 1)
                    dve.wait_ge(stats_done, 4 * g + 4)
                    settle(dve)
                    for j in range(TG):
                        nc.vector.bn_aggr(mv[:, pp, j], st6[:, j]).then_inc(mv_ready, 1)
                    dve.wait_ge(mhi_ready, g + 1)
                    nc.vector.tensor_tensor(mg_lo[:, :, :], mg[:, :, :], mg_hi[:, :, :].bitcast(fp32), ALU.subtract).then_inc(mlo_ready, 1)
                    dve.wait_ge(rstd_ready, g + 1)
                    for j in range(TG):
                        last = nc.vector.tensor_scalar(lnf[:, pp, j], xg[:, pp, j], mv[:, pp, j, 0:1], rstd[:, pp, j:j + 1],
                                                       ALU.subtract, ALU.mult)
                    last.then_inc(ln_ready, 1)
                    for k in range(KD):
                        dve.wait_ge(thi_ready, 2 * g + k + 1)
                        nc.vector.tensor_tensor(lnT_lo[:, k, bass.ds(g * CH, CH)], tr_ps[k][:, :],
                                                lnT_hi[:, k, bass.ds(g * CH, CH)].bitcast(fp32), ALU.subtract).then_inc(tlo_ready, 1)
                groups(dve, group)

                dve.wait_ge(thi_ready, 2 * NG)
                nc.vector.tensor_reduce(xbar[:, :], xsum[:, :, :], AX.X, ALU.add).then_inc(xs_ready, 1)
                dve.wait_ge(xs_ready, 1)
                nc.vector.tensor_scalar(xbar[:, :], xbar[:, :], 1.0 / N, None, ALU.mult).then_inc(xbar_ready, 1)
                dve.wait_ge(xbar_ready, 1)
                dve.wait_ge(half_ready, 2)
                for k in range(KD):
                    nc.vector.tensor_scalar(cols_b[:, 0, k], ones[:, :], xbar[:, k:k + 1], None, ALU.mult).then_inc(cols_ready, 1)
                dve.wait_ge(gk_done, 1)
                nc.vector.tensor_copy(gk[:, :], gk_ps[:, 0:KD]).then_inc(gk_ready, 1)
                dve.wait_ge(gk_ready, 1)
                for k in range(KD):
                    nc.vector.tensor_scalar(cols_b[:, 1, k], ones[:, :], gk[:, k:k + 1], None, ALU.mult).then_inc(cols_ready, 1)
                dve.wait_ge(rows_loaded, 16 * 8)
                dve.wait_ge(rows_done, 1)
                nc.vector.tensor_tensor(gv_b[:, :], row_ps[:, 0:D], gv_b[:, :], ALU.add)
                nc.vector.tensor_copy(wg_b[:, :], row_ps[:, D:2 * D])
                dve.wait_ge(attc_done, 1)
                nc.vector.tensor_tensor(attc_b[:, :], attc_ps[:, 0:D], attc_b[:, :], ALU.add)
                dve.wait_ge(whi_ready, 1)
                nc.vector.tensor_tensor(w_lo[:, :, :, :], w_in[:, :, :, :], w_hi[:, :, :, :].bitcast(fp32), ALU.subtract)

            @block.scalar
            def _(act):
                act.wait_ge(qw_done, 1)
                nc.scalar.activation(qw_f[:, :, :], qw_ps[:, :].rearrange("p (k n) -> p k n", k=KD), ACT.Copy).then_inc(qwf_ready, 1)
                act.wait_ge(qwf_ready, 1)
                nc.scalar.activation(qw_hi[:, :, :], qw_f[:, :, :], ACT.Copy).then_inc(qwhi_ready, 1)
                act.wait_ge(qwhi_ready, 1)
                act.wait_ge(rows_loaded, 16 * 8)
                act.wait_ge(w_loaded, 64)
                act.wait_ge(half_ready, 2)
                for k in range(KD):
                    nc.scalar.activation(cols_b[:, 2, k], ones[:, :], ACT.Copy, scale=lnb[:, k:k + 1]).then_inc(attcols_ready, 1)
                act.wait_ge(attc_done, 1)
                for k in range(KD):
                    nc.scalar.activation(w_in[:, WATT, k], w_in[:, WATT, k], ACT.Copy, scale=lng[:, k:k + 1]).then_inc(attg_ready, 1)
                act.wait_ge(attg_ready, 2)
                nc.scalar.activation(w_hi[:, :, :, :], w_in[:, :, :, :], ACT.Copy).then_inc(whi_ready, 1)

                def group(h, pp):
                    g = 2 * h + pp

                    act.wait_ge(mg_in, 16 * g + 16)
                    wait(act, q_done, 2 * g)
                    nc.scalar.activation(mg_hi[:, :, :], mg[:, :, :], ACT.Copy).then_inc(mhi_ready, 1)
                    act.wait_ge(ln_ready, g + 1)
                    nc.scalar.activation(v_sp[:, bass.ds(g * TG, TG), 0:D], lnf[:, pp], ACT.Copy).then_inc(vhi_ready, 1)
                    for k in range(KD):
                        act.wait_ge(tr_done, 2 * g + k + 1)
                        nc.scalar.activation(lnT_hi[:, k, bass.ds(g * CH, CH)], tr_ps[k][:, :], ACT.Copy,
                                             accum_out=xsum[:, k, bass.ds(g, 1)]).then_inc(thi_ready, 1)
                    wait(act, q_stored, 32 * g)
                    for k in range(KD):
                        act.wait_ge(q_done, 2 * g + k + 1)
                        nc.scalar.activation(q_out[:, k, :], q_ps[k][:, :], ACT.Copy).then_inc(q_copied, 1)
                groups(act, group)

            @block.tensor
            def _(pe):
                pe.wait_ge(wq_loaded, 32)
                for m in range(KD):
                    for k in range(KD):
                        last = nc.tensor.matmul(qw_ps[:, m * D:(m + 1) * D], wq_in[:, 0, k, m * P:(m + 1) * P], wq_in[:, 1, k, :],
                                                start=k == 0, stop=k == KD - 1)
                last.then_inc(qw_done, 1)
                pe.wait_ge(attcols_ready, 2)
                for k in range(KD):
                    last = nc.tensor.matmul(attc_ps[:, 0:D], cols_b[:, 2, k], w_in[:, WATT, k], start=k == 0, stop=k == KD - 1)
                last.then_inc(attc_done, 1)
                pe.wait_ge(qwlo_ready, 1)
                pe.wait_ge(ident_ready, 2)

                def group(h, pp):
                    g = 2 * h + pp
                    pe.wait_ge(ln_ready, g + 1)
                    wait(pe, tlo_ready, 2 * g)
                    for k in range(KD):
                        for j in range(TG):
                            last = nc.tensor.transpose(tr_ps[k][:, j * P:(j + 1) * P], lnf[:, pp, j, k * P:(k + 1) * P], ident[:, :])
                        last.then_inc(tr_done, 1)
                    pe.wait_ge(mlo_ready, g + 1)
                    wait(pe, q_copied, 2 * g)
                    for m in range(KD):
                        ms = slice(m * P, (m + 1) * P)
                        split_product(nc, q_ps[m][:, :],
                                      [(qw_hi[:, k, ms], qw_lo[:, k, ms]) for k in range(KD)],
                                      [(mg_hi[:, k], mg_lo[:, k]) for k in range(KD)]).then_inc(q_done, 1)
                groups(pe, group)

                pe.wait_ge(wg_loaded, 48)
                pe.wait_ge(xbar_ready, 1)
                for m in range(KD):
                    for k in range(KD):
                        last = nc.tensor.matmul(gk_ps[:, m:m + 1], wq_in[:, 0, k, m * P:(m + 1) * P], xbar[:, k:k + 1],
                                                start=k == 0, stop=k == KD - 1)
                last.then_inc(gk_done, 1)
                pe.wait_ge(cols_ready, 4)
                for n, w in enumerate((wgv_in, wq_in[:, 1])):
                    for k in range(KD):
                        last = nc.tensor.matmul(row_ps[:, n * D:(n + 1) * D], cols_b[:, n, k], w[:, k, :],
                                                start=k == 0, stop=k == KD - 1)
                last.then_inc(rows_done, 1)
        pa.close()
        a.close()

        b = ab.enter_context(ExitStack())
        scores = sb(b, "scores", [P, N])
        adj8 = sb(b, "adj8", [P, N], uint8)
        bias = sb(b, "bias", [P, 2, 2 * CH])
        q_in = sb(b, "q_in", [P, KD, P])
        q_hi = sb(b, "q_hi", [P, KD, P], fp32r)
        q_lo = sb(b, "q_lo", [P, KD, P], fp32r)
        mxt = sb(b, "mxt", [P, D])
        dotted = sb(b, "dotted", [P, 2, D])
        p_hi = sb(b, "p_hi", [P, 2, CH], fp32r)
        p_lo = sb(b, "p_lo", [P, 2, CH], fp32r)
        tops = sb(b, "tops", [P, NC + 2])
        neg_top = sb(b, "neg_top", [P, 1])
        sums = sb(b, "sums", [P, 6])
        den = sb(b, "den", [P, 1])
        local_sum = sb(b, "local_sum", [P, 1])
        rden = sb(b, "rden", [P, 1])
        u_part = sb(b, "u_part", [P, D])
        u_out = sb(b, "u_out", [P, ROWU])

        pb = ExitStack()
        s_ps = [ps(pb, f"s_ps{i}") for i in range(2)]
        pt_ps = [ps(pb, f"pt_ps{i}") for i in range(2)]
        u_ps = ps(pb, "u_ps")

        adj_in = [sem(f"adj_in{i}") for i in range(2)]
        q_loaded, mx_loaded, u_stored = sem("q_loaded"), sem("mx_loaded"), sem("u_stored")
        bias_ready, qhi_ready, qlo_ready = sem("bias_ready"), sem("qhi_ready"), sem("qlo_ready")
        score_done, score_masked, extra_dotted, extra_ready, top_ready = (
            sem(n) for n in ("score_done", "score_masked", "extra_dotted", "extra_ready", "top_ready"))
        exp_done, extra_exp, den_ready, rden_ready, coef_ready = (
            sem(n) for n in ("exp_done", "extra_exp", "den_ready", "rden_ready", "coef_ready"))
        pt_done, phi_ready, plo_ready, pv_done, upart_ready, u_ready = (
            sem(n) for n in ("pt_done", "phi_ready", "plo_ready", "pv_done", "upart_ready", "u_ready"))

        def steps(eng, step):
            step(-1, here=False)
            step(0)
            with eng.Fori(1, NT - 2) as t:
                step(t)
            step(NT - 2, after=False)
            step(NT - 1, ahead=False, after=False)

        with nc.Block() as block:
            @block.sync
            def _(sp):
                def load_queries(n):
                    wait(sp, qlo_ready, n)
                    settle(sp)
                    sp.dma_start(q_in[:, :, :], q_dram[n]).then_inc(q_loaded, 16)

                def step(t, here=True, ahead=True, after=True):
                    if ahead:
                        for h in range(2):
                            wait(sp, bias_ready, 4 * t + 2 * h + 2)
                            settle(sp)
                            sp.dma_start(adj8[:, h * (N // 2):(h + 1) * (N // 2)],
                                         adj[bass.ds((t + 1) * P, P), h * (N // 2):(h + 1) * (N // 2)]).then_inc(adj_in[h], 16)
                        wait(sp, extra_dotted, 2 * t + 2)
                        settle(sp)
                        sp.dma_start(mxt[:, :], mx[bass.ds((t + 1) * P, P)]).then_inc(mx_loaded, 16)
                    if after:
                        load_queries(t + 2)
                    if here:
                        sp.wait_ge(u_ready, t + 1)
                        sp.wait_ge(coef_ready, 2 * t + 2)
                        settle(sp)
                        sp.dma_start(u_dram[t], u_out[:, :]).then_inc(u_stored, 16)

                load_queries(0)
                steps(sp, step)
                sp.wait_ge(u_stored, 16 * NT)

            @block.gpsimd
            def _(pool):
                def step(t, here=True, ahead=True, after=True):
                    if ahead:
                        n = t + 1
                        for c in range(4):
                            if c % 2 == 0:
                                pool.wait_ge(adj_in[c // 2], 16 * n + 16)
                            wait(pool, score_masked, 8 * n + 2 * c - 2)
                            settle(pool)
                            nc.gpsimd.tensor_scalar(bias[:, c % 2], adj8[:, c * 2 * CH:(c + 1) * 2 * CH], -MASKED, MASKED,
                                                    ALU.mult, ALU.add).then_inc(bias_ready, 1)
                steps(pool, step)

            @block.vector
            def _(dve):
                def q_low(n):
                    dve.wait_ge(qhi_ready, n + 1)
                    nc.vector.tensor_tensor(q_lo[:, :, :], q_in[:, :, :], q_hi[:, :, :].bitcast(fp32), ALU.subtract).then_inc(qlo_ready, 1)

                def step(t, here=True, ahead=True, after=True):
                    n = t + 1
                    for c in range(NC):
                        if here:
                            dve.wait_ge(phi_ready, 8 * t + c + 1)
                            wait(dve, pv_done, 8 * t + c - 1)
                            nc.vector.tensor_tensor(p_lo[:, c % 2], pt_ps[c % 2][:, :], p_hi[:, c % 2].bitcast(fp32),
                                                    ALU.subtract).then_inc(plo_ready, 1)
                        if ahead:
                            dve.wait_ge(score_done, 8 * n + c + 1)
                            dve.wait_ge(bias_ready, 4 * n + c // 2 + 1)
                            settle(dve)
                            nc.vector.tensor_tensor_reduce(out=scores[:, c * CH:(c + 1) * CH], in0=s_ps[c % 2][:, :],
                                                           in1=bias[:, c // 2 % 2, c % 2 * CH:(c % 2 + 1) * CH],
                                                           scale=SCALE, scalar=-3.0e38, op0=ALU.add, op1=ALU.max,
                                                           accum_out=tops[:, c:c + 1]).then_inc(score_masked, 1)
                        if here and c == 3:
                            dve.wait_ge(exp_done, 4 * t + 4)
                            dve.wait_ge(extra_exp, t + 1)
                            nc.vector.tensor_reduce(den[:, :], sums[:, 0:6], AX.X, ALU.add).then_inc(den_ready, 1)
                            nc.vector.tensor_reduce(local_sum[:, :], sums[:, 0:4], AX.X, ALU.add).then_inc(den_ready, 1)
                            dve.wait_ge(den_ready, 2 * t + 2)
                            nc.vector.reciprocal(rden[:, :], den[:, :]).then_inc(rden_ready, 1)
                            dve.wait_ge(rden_ready, t + 1)
                            wait(dve, u_stored, 16 * t)
                            nc.vector.tensor_scalar(u_out[:, D:D + 1], local_sum[:, :], rden[:, :], None, ALU.mult).then_inc(coef_ready, 1)
                            nc.vector.tensor_scalar(u_out[:, D + 1:D + 3], sums[:, 4:6], rden[:, :], None, ALU.mult).then_inc(coef_ready, 1)
                            if isinstance(t, int) and t == 0:
                                nc.vector.memset(u_out[:, D + 3:D + 4], 0.0)
                        if ahead and c == 5:
                            dve.wait_ge(mx_loaded, 16 * n + 16)
                            wait(dve, extra_exp, n)
                            nc.vector.tensor_tensor_reduce(out=dotted[:, 0], in0=mxt[:, :], in1=wg_b[:, :], scale=SCALE, scalar=0.0,
                                                           op0=ALU.mult, op1=ALU.add, accum_out=tops[:, NC:NC + 1]).then_inc(extra_dotted, 1)
                            nc.vector.tensor_tensor_reduce(out=dotted[:, 1], in0=mxt[:, :], in1=wes_b[:, :], scale=1.0, scalar=0.0,
                                                           op0=ALU.mult, op1=ALU.add, accum_out=tops[:, NC + 1:NC + 2]).then_inc(extra_dotted, 1)
                    if ahead:
                        dve.wait_ge(score_masked, 8 * n + 8)
                        dve.wait_ge(extra_dotted, 2 * n + 2)
                        nc.vector.tensor_reduce(neg_top[:, :], tops[:, :], AX.X, ALU.max, negate=True).then_inc(top_ready, 1)
                    if after:
                        q_low(t + 2)
                    if here:
                        dve.wait_ge(upart_ready, t + 1)
                        nc.vector.scalar_tensor_tensor(out=u_out[:, 0:D], in0=u_ps[:, 0:D], scalar=rden[:, :], in1=u_part[:, :],
                                                       op0=ALU.mult, op1=ALU.add).then_inc(u_ready, 1)
                q_low(0)
                steps(dve, step)

            @block.scalar
            def _(act):
                def q_high(n):
                    act.wait_ge(q_loaded, 16 * n + 16)
                    wait(act, score_done, 8 * n)
                    nc.scalar.activation(q_hi[:, :, :], q_in[:, :, :], ACT.Copy).then_inc(qhi_ready, 1)

                def exponentials(part):
                    span = slice(part * 2 * CH, (part + 1) * 2 * CH)
                    nc.scalar.activation(scores[:, span], scores[:, span], ACT.Exp, bias=neg_top[:, :],
                                         accum_out=sums[:, part:part + 1]).then_inc(exp_done, 1)

                def step(t, here=True, ahead=True, after=True):
                    n = t + 1
                    if here:
                        for c in range(NC):
                            act.wait_ge(pt_done, 8 * t + c + 1)
                            wait(act, pv_done, 8 * t + c - 1)
                            nc.scalar.activation(p_hi[:, c % 2], pt_ps[c % 2][:, :], ACT.Copy).then_inc(phi_ready, 1)
                            if c < 2:
                                exponentials(2 + c)
                            if c == 1:
                                nc.scalar.activation(sums[:, 4:6], tops[:, NC:NC + 2], ACT.Exp, bias=neg_top[:, :]).then_inc(extra_exp, 1)
                    if after:
                        q_high(t + 2)
                    if ahead:
                        act.wait_ge(top_ready, n + 1)
                        exponentials(0)
                    if here:
                        act.wait_ge(pv_done, 8 * t + 8)
                        act.wait_ge(rden_ready, t + 1)
                        nc.scalar.activation(u_part[:, :], u_ps[:, D:2 * D], ACT.Copy, scale=rden[:, :]).then_inc(upart_ready, 1)
                    if ahead:
                        exponentials(1)
                q_high(0)
                steps(act, step)

            @block.tensor
            def _(pe):
                def weigh(t, c):
                    pe.wait_ge(plo_ready, 8 * t + c + 1)
                    if c == 0:
                        wait(pe, u_ready, t)
                    for j in range(TG):
                        js = slice(j * P, (j + 1) * P)
                        nc.tensor.matmul(u_ps[:, :], p_hi[:, c % 2, js], v_sp[:, c * TG + j, :], start=c + j == 0, stop=False)
                        last = nc.tensor.matmul(u_ps[:, 0:D], p_lo[:, c % 2, js], v_sp[:, c * TG + j, 0:D],
                                                start=False, stop=c * TG + j == NT - 1)
                    last.then_inc(pv_done, 1)

                def step(t, here=True, ahead=True, after=True):
                    n = t + 1
                    for c in range(NC):
                        if here:
                            if c % 2 == 0:
                                pe.wait_ge(exp_done, 4 * t + c // 2 + 1)
                            wait(pe, plo_ready, 8 * t + c - 1)
                            for j in range(TG):
                                last = nc.tensor.transpose(pt_ps[c % 2][:, j * P:(j + 1) * P],
                                                           scores[:, (c * TG + j) * P:(c * TG + j + 1) * P], ident[:, :])
                            last.then_inc(pt_done, 1)
                        if ahead:
                            if c == 0:
                                pe.wait_ge(qlo_ready, n + 1)
                            wait(pe, score_masked, 8 * n + c - 1)
                            cs = slice(c * CH, (c + 1) * CH)
                            split_product(nc, s_ps[c % 2][:, :], [(q_hi[:, k], q_lo[:, k]) for k in range(KD)],
                                          [(lnT_hi[:, k, cs], lnT_lo[:, k, cs]) for k in range(KD)]).then_inc(score_done, 1)
                        if here and c > 0:
                            weigh(t, c - 1)
                    if here:
                        weigh(t, NC - 1)
                steps(pe, step)
        pb.close()
        ab.close()

        raw = sb(ctx, "raw", [P, HB, 2 * D])
        e_hi = sb(ctx, "e_hi", [P, HB, 2 * D], fp32r)
        e_lo = sb(ctx, "e_lo", [P, HB, 2 * D], fp32r)
        b1_c = sb(ctx, "b1_c", [P, E * HB])
        b2_c = sb(ctx, "b2_c", [P, E * KD])
        mhalf2 = sb(ctx, "mhalf2", [P, 2])
        u4 = sb(ctx, "u4", [P, TG, ROWU])
        mx4 = sb(ctx, "mx4", [P, TG, D])
        x4 = sb(ctx, "x4", [P, TG, D])
        mT = sb(ctx, "mT", [P, KD, CH])
        mT_hi = sb(ctx, "mT_hi", [P, KD, CH], fp32r)
        mT_lo = sb(ctx, "mT_lo", [P, KD, CH], fp32r)
        uT_hi = sb(ctx, "uT_hi", [P, 2, KD, P], fp32r)
        uT_lo = sb(ctx, "uT_lo", [P, 2, KD, P], fp32r)
        kt = sb(ctx, "kt", [P, TG, D])
        kt_b = sb(ctx, "kt_b", [P, 3, D])
        comb = sb(ctx, "comb", [P, D])
        res = sb(ctx, "res", [P, 2, D])
        resm = sb(ctx, "resm", [P, 2, D])
        x1_next = sb(ctx, "x1_next", [P, TG, D])
        x1_here = sb(ctx, "x1_here", [P, TG, D])
        cst6 = sb(ctx, "cst6", [P, 2, 6])
        cmv = sb(ctx, "cmv", [P, 2, 2])
        cve = sb(ctx, "cve", [P, 2])
        crstd = sb(ctx, "crstd", [P, 2])
        xf = sb(ctx, "xf", [P, 2, D])
        xn = sb(ctx, "xn", [P, 2, D])
        xfa = sb(ctx, "xfa", [P, 2, D])
        nT_hi = sb(ctx, "nT_hi", [P, 2, KD, P], fp32r)
        nT_lo = sb(ctx, "nT_lo", [P, 2, KD, P], fp32r)
        xa = sb(ctx, "xa", [P, TG, D])
        xT_hi = sb(ctx, "xT_hi", [P, KD, CH], fp32r)
        xT_lo = sb(ctx, "xT_lo", [P, KD, CH], fp32r)
        hf = sb(ctx, "hf", [P, 2, CH])
        h_hi = sb(ctx, "h_hi", [P, 2, CH], fp32r)
        h_lo = sb(ctx, "h_lo", [P, 2, CH], fp32r)
        yf = sb(ctx, "yf", [P, KD, CH])
        y_hi = sb(ctx, "y_hi", [P, KD, CH], fp32r)
        y_lo = sb(ctx, "y_lo", [P, KD, CH], fp32r)
        zt = sb(ctx, "zt", [P, 2, 2, D])
        zg = sb(ctx, "zg", [P, 2, 2, D])
        o4 = sb(ctx, "o4", [P, 2, 2, D])

        h_ps = [ps(ctx, f"h_ps{i}") for i in range(2)]
        y_ps = [ps(ctx, f"y_ps{i}") for i in range(KD)]
        xt_ps = ps(ctx, "xt_ps")
        vp_ps = ps(ctx, "vp_ps")
        ap_ps = ps(ctx, "ap_ps")
        zp_ps = ps(ctx, "zp_ps")

        x_loaded, b_loaded = sem("x_loaded"), sem("b_loaded")
        raw_in = [sem(f"raw_in{i}") for i in range(4)]
        out_stored = [sem(f"out_stored{i}") for i in range(2)]
        (ehi_ready, elo_ready, mthi_ready, mtlo_ready, kpart_ready, ksum_ready, kt_ready, ut_done, uthi_ready, utlo_ready,
         proj_done, comb_ready, vp_taken, resm_ready, x1_ready) = (sem(n) for n in (
             "ehi_ready", "elo_ready", "mthi_ready", "mtlo_ready", "kpart_ready", "ksum_ready", "kt_ready", "ut_done", "uthi_ready",
             "utlo_ready", "proj_done", "comb_ready", "vp_taken", "resm_ready", "x1_ready"))
        (half2_ready, cst_done, cmv_ready, cve_ready, crstd_ready, xf_ready, xn_ready, xfa_ready, nt_done, nthi_ready, ntlo_ready,
         att_done, xa_ready, xt_done, xthi_ready, xtlo_ready) = (sem(n) for n in (
             "half2_ready", "cst_done", "cmv_ready", "cve_ready", "crstd_ready", "xf_ready", "xn_ready", "xfa_ready", "nt_done",
             "nthi_ready", "ntlo_ready", "att_done", "xa_ready", "xt_done", "xthi_ready", "xtlo_ready"))
        (fc1_done, gelu_done, hhi_ready, hlo_ready, fc2_done, y_ready, yhi_ready, ylo_ready, z_done, zt_ready, zg_ready, o_ready,
         x1_moved) = (sem(n) for n in (
             "fc1_done", "gelu_done", "hhi_ready", "hlo_ready", "fc2_done", "y_ready", "yhi_ready", "ylo_ready", "z_done",
             "zt_ready", "zg_ready", "o_ready", "x1_moved"))

        def bodies(eng, body):
            body(-1, here=False)
            body(0)
            with eng.Fori(1, E - 1) as e:
                body(e)
            body(E - 1, ahead=False)

        RUN = 2 * P

        with nc.Block() as block:
            @block.sync
            def _(sp):
                def load_weights(e, i):
                    wait(sp, elo_ready, 8 * e - 6 + 2 * i)
                    settle(sp)
                    sp.dma_start(raw[:, 2 * i:2 * i + 2], wffn[e, :, 2 * i:2 * i + 2]).then_inc(raw_in[i], 16)

                def load_tokens(n):
                    wait(sp, x1_ready, 2 * n)
                    settle(sp)
                    for m in range(2):
                        row = m * (N // 2) + n * RUN
                        tiles = slice(2 * m, 2 * m + 2)
                        sp.dma_start(u4[:, tiles], u_dram[bass.ds(m * (NT // 2) + 2 * n, 2)].rearrange("t p c -> p t c")).then_inc(x_loaded, 16)
                        sp.dma_start(mT[:, :, m * RUN:(m + 1) * RUN], mxT[:, bass.ds(row, RUN)].rearrange("(k p) q -> p k q", p=P)).then_inc(x_loaded, 16)
                        sp.dma_start(mx4[:, tiles], mx[bass.ds(row, RUN)].rearrange("(t p) d -> p t d", p=P)).then_inc(x_loaded, 16)
                        sp.dma_start(x4[:, tiles], x[bass.ds(row, RUN)].rearrange("(t p) d -> p t d", p=P)).then_inc(x_loaded, 16)

                def body(e, here=True, ahead=True):
                    if ahead:
                        if not here:
                            load_tokens(0)
                            for i in range(4):
                                load_weights(0, i)
                            sp.dma_start(b1_c[:, :], b1).then_inc(b_loaded, 16)
                            sp.dma_start(b2_c[:, :], b2).then_inc(b_loaded, 16)
                        if here:
                            load_tokens(e + 1)
                            for i in range(4):
                                load_weights(e + 1, i)
                    if here:
                        for m in range(2):
                            sp.wait_ge(o_ready, 2 * e + m + 1)
                            settle(sp)
                            sp.dma_start(out[bass.ds(m * (N // 2) + e * RUN, RUN)].rearrange("(t p) d -> p t d", p=P),
                                         o4[:, m]).then_inc(out_stored[m], 16)
                bodies(sp, body)
                for m in range(2):
                    sp.wait_ge(out_stored[m], 16 * E)

            @block.gpsimd
            def _(pool):
                nc.gpsimd.memset(mhalf2[:, :], -0.5).then_inc(half2_ready, 1)
                pool.wait_ge(half2_ready, 1)

                def rank_one(n, tt):
                    i = 4 * n + tt
                    wait(pool, kt_ready, i)
                    settle(pool)
                    for r, row in enumerate((blv_b, gv_b, bev_b)):
                        nc.gpsimd.tensor_scalar(kt_b[:, r], row[:, :], u4[:, tt, D + r:D + r + 1], 0.0, ALU.mult, ALU.add).then_inc(kpart_ready, 1)
                    wait(pool, vp_taken, 4 * n + tt - 3)
                    pool.wait_ge(kpart_ready, 3 * i + 3)
                    nc.gpsimd.tensor_tensor(out=kt[:, tt], in0=kt_b[:, 0], in1=kt_b[:, 1], op=ALU.add).then_inc(ksum_ready, 1)
                    pool.wait_ge(ksum_ready, i + 1)
                    nc.gpsimd.tensor_tensor(out=kt[:, tt], in0=kt[:, tt], in1=kt_b[:, 2], op=ALU.add).then_inc(kt_ready, 1)

                def reciprocal_deviation(i):
                    pool.wait_ge(cmv_ready, 2 * i + 2)
                    settle(pool)
                    nc.gpsimd.tensor_scalar(cve[:, :], cmv[:, :, 1], EPS, 0.0, ALU.add, ALU.add).then_inc(cve_ready, 1)
                    pool.wait_ge(cve_ready, i + 1)
                    nc.gpsimd.tensor_tensor(out=crstd[:, :], in0=cve[:, :], in1=mhalf2[:, :], op=ALU.pow).then_inc(crstd_ready, 1)

                def low_weights(e, j):
                    pool.wait_ge(ehi_ready, 8 * e + j + 1)
                    nc.gpsimd.tensor_tensor(out=e_lo[:, j], in0=raw[:, j], in1=e_hi[:, j].bitcast(fp32), op=ALU.subtract).then_inc(elo_ready, 1)

                def body(e, here=True, ahead=True):
                    if ahead:
                        n = e + 1
                        pool.wait_ge(x_loaded, 128 * n + 128)
                        for tt in range(TG):
                            rank_one(n, tt)
                        reciprocal_deviation(4 * n)
                        low_weights(n, 0)
                        reciprocal_deviation(4 * n + 1)
                        low_weights(n, 1)
                        low_weights(n, 2)
                        reciprocal_deviation(4 * n + 2)
                        low_weights(n, 3)
                        reciprocal_deviation(4 * n + 3)
                        for j in range(4, HB):
                            low_weights(n, j)
                bodies(pool, body)

            @block.vector
            def _(dve):
                def combine(n, tt):
                    dve.wait_ge(proj_done, 4 * n + tt + 1)
                    dve.wait_ge(kt_ready, 4 * n + tt + 1)
                    nc.vector.scalar_tensor_tensor(out=comb[:, :], in0=vp_ps[:, D:2 * D], scalar=u4[:, tt, D + 2:D + 3], in1=kt[:, tt],
                                                   op0=ALU.mult, op1=ALU.add).then_inc(comb_ready, 1)
                    dve.wait_ge(comb_ready, 4 * n + tt + 1)
                    nc.vector.tensor_tensor(res[:, tt % 2], vp_ps[:, 0:D], comb[:, :], ALU.add).then_inc(vp_taken, 1)

                def residual(n, q):
                    tiles = slice(2 * q, 2 * q + 2)
                    dve.wait_ge(vp_taken, 4 * n + 2 * q + 2)
                    nc.vector.tensor_tensor(resm[:, :, :], res[:, :, :], mx4[:, tiles], ALU.max).then_inc(resm_ready, 1)
                    dve.wait_ge(resm_ready, 2 * n + q + 1)
                    nc.vector.tensor_tensor(x1_next[:, tiles], resm[:, :, :], x4[:, tiles], ALU.add).then_inc(x1_ready, 1)

                def moments(i, tiles):
                    for s in range(2):
                        nc.vector.bn_stats(cst6[:, s], tiles[s]).then_inc(cst_done, 1)
                    dve.wait_ge(cst_done, 2 * i + 2)
                    settle(dve)
                    for s in range(2):
                        nc.vector.bn_aggr(cmv[:, s], cst6[:, s]).then_inc(cmv_ready, 1)

                def first_moments(n, q):
                    dve.wait_ge(x1_ready, 2 * n + q + 1)
                    moments(4 * n + 2 * q, [x1_next[:, 2 * q + s] for s in range(2)])

                def first_norm(n, q):
                    i = 4 * n + 2 * q
                    dve.wait_ge(crstd_ready, i + 1)
                    for s in range(2):
                        nc.vector.tensor_scalar(xf[:, s], x1_next[:, 2 * q + s], cmv[:, s, 0:1], crstd[:, s:s + 1],
                                                ALU.subtract, ALU.mult).then_inc(xf_ready, 1)
                    dve.wait_ge(xf_ready, 4 * n + 2 * q + 2)
                    moments(i + 1, [xf[:, s] for s in range(2)])

                def second_norm(n, q):
                    i = 4 * n + 2 * q + 1
                    dve.wait_ge(crstd_ready, i + 1)
                    for s in range(2):
                        nc.vector.tensor_scalar(xn[:, s], xf[:, s], cmv[:, s, 0:1], crstd[:, s:s + 1],
                                                ALU.subtract, ALU.mult).then_inc(xn_ready, 1)
                    for s in range(2):
                        nc.vector.tensor_tensor(xfa[:, s], xf[:, s], attc_b[:, :], ALU.add).then_inc(xfa_ready, 1)

                def low(out, whole, high, done):
                    nc.vector.tensor_tensor(out, whole, high.bitcast(fp32), ALU.subtract).then_inc(done, 1)

                def attended(n, q):
                    dve.wait_ge(att_done, 2 * n + q + 1)
                    dve.wait_ge(xfa_ready, 4 * n + 2 * q + 2)
                    nc.vector.tensor_tensor(xa[:, 2 * q:2 * q + 2], ap_ps[:, :].rearrange("p (t d) -> p t d", t=2), xfa[:, :, :],
                                            ALU.add).then_inc(xa_ready, 1)

                def low_attended(n, q):
                    dve.wait_ge(nthi_ready, 2 * n + q + 1)
                    low(nT_lo[:, :, :, :], xt_ps[:, :].rearrange("p (t k c) -> p t k c", t=2, k=KD), nT_hi[:, :, :, :], ntlo_ready)

                def low_result(n, q):
                    dve.wait_ge(uthi_ready, 2 * n + q + 1)
                    low(uT_lo[:, :, :, :], xt_ps[:, :].rearrange("p (t k c) -> p t k c", t=2, k=KD), uT_hi[:, :, :, :], utlo_ready)

                def body(e, here=True, ahead=True):
                    n = e + 1
                    for j in range(HB):
                        if here:
                            dve.wait_ge(hhi_ready, 8 * e + j + 1)
                            low(h_lo[:, j % 2], hf[:, j % 2], h_hi[:, j % 2], hlo_ready)
                        if ahead:
                            if j == 0:
                                dve.wait_ge(mthi_ready, n + 1)
                                low(mT_lo[:, :, :], mT[:, :, :], mT_hi[:, :, :], mtlo_ready)
                                low_result(n, 0)
                            if j == 1:
                                combine(n, 0)
                            if j == 2:
                                combine(n, 1)
                                low_result(n, 1)
                                residual(n, 0)
                                first_moments(n, 0)
                            if j == 3:
                                combine(n, 2)
                                first_norm(n, 0)
                            if j == 4:
                                combine(n, 3)
                                second_norm(n, 0)
                                residual(n, 1)
                            if j == 5:
                                low_attended(n, 0)
                                first_moments(n, 1)
                            if j == 6:
                                attended(n, 0)
                                first_norm(n, 1)
                                second_norm(n, 1)
                            if j == 7:
                                low_attended(n, 1)
                    if ahead:
                        attended(n, 1)
                    if here:
                        dve.wait_ge(yhi_ready, e + 1)
                        low(y_lo[:, :, :], yf[:, :, :], y_hi[:, :, :], ylo_ready)
                    if ahead:
                        for q, bank in enumerate((xt_ps, vp_ps)):
                            dve.wait_ge(xthi_ready, 2 * n + q + 1)
                            low(xT_lo[:, :, q * RUN:(q + 1) * RUN].rearrange("p k (t c) -> p k t c", t=2),
                                bank[:, :].rearrange("p (t k c) -> p k t c", t=2, k=KD),
                                xT_hi[:, :, q * RUN:(q + 1) * RUN].rearrange("p k (t c) -> p k t c", t=2), xtlo_ready)
                    if here:
                        for m, bank in enumerate((zp_ps, ap_ps)):
                            dve.wait_ge(z_done, 2 * e + m + 1)
                            wait(dve, zg_ready, 2 * e + m - 1)
                            for s in range(2):
                                nc.vector.tensor_tensor(zt[:, m, s], bank[:, s * D:(s + 1) * D], nextb_b[:, :], ALU.add).then_inc(zt_ready, 1)
                        for m in range(2):
                            dve.wait_ge(zg_ready, 2 * e + m + 1)
                            wait(dve, out_stored[m], 16 * e)
                            wait(dve, x1_moved, e + 1)
                            nc.vector.tensor_tensor(o4[:, m], zg[:, m], x1_here[:, 2 * m:2 * m + 2], ALU.add).then_inc(o_ready, 1)
                    if ahead:
                        dve.wait_ge(x1_ready, 2 * n + 2)
                        wait(dve, o_ready, 2 * e + 2)
                        nc.vector.tensor_copy(x1_here[:, :, :], x1_next[:, :, :]).then_inc(x1_moved, 1)
                bodies(dve, body)

            @block.scalar
            def _(act):
                def high(out, whole, done):
                    nc.scalar.activation(out, whole, ACT.Copy).then_inc(done, 1)

                def high_weights(e, j):
                    act.wait_ge(raw_in[j // 2], 16 * e + 16)
                    wait(act, fc2_done, 8 * e + j - 7)
                    high(e_hi[:, j], raw[:, j], ehi_ready)

                def high_result(n, q):
                    act.wait_ge(ut_done, 2 * n + q + 1)
                    wait(act, proj_done, 4 * n + 2 * q)
                    high(uT_hi[:, :, :, :], xt_ps[:, :].rearrange("p (t k c) -> p t k c", t=2, k=KD), uthi_ready)

                def high_attended(n, q):
                    act.wait_ge(nt_done, 2 * n + q + 1)
                    wait(act, att_done, 2 * n + q)
                    high(nT_hi[:, :, :, :], xt_ps[:, :].rearrange("p (t k c) -> p t k c", t=2, k=KD), nthi_ready)

                def body(e, here=True, ahead=True):
                    n = e + 1
                    for j in range(HB):
                        if here:
                            act.wait_ge(fc1_done, 8 * e + j + 1)
                            wait(act, fc2_done, 8 * e + j - 1)
                            nc.scalar.activation(hf[:, j % 2], h_ps[j % 2][:, :], ACT.Gelu,
                                                 bias=b1_c[:, bass.ds(8 * e + j, 1)]).then_inc(gelu_done, 1)
                            act.wait_ge(gelu_done, 8 * e + j + 1)
                            high(h_hi[:, j % 2], hf[:, j % 2], hhi_ready)
                        if ahead:
                            if j == 0:
                                act.wait_ge(x_loaded, 128 * n + 128)
                                wait(act, proj_done, 4 * n)
                                high(mT_hi[:, :, :], mT[:, :, :], mthi_ready)
                                high_result(n, 0)
                            if j == 2:
                                high_result(n, 1)
                            if j == 5:
                                high_attended(n, 0)
                            if j == 7:
                                high_attended(n, 1)
                            if j >= 2:
                                high_weights(n, j - 2)
                    if here:
                        act.wait_ge(fc2_done, 8 * e + 8)
                        for k in range(KD):
                            nc.scalar.activation(yf[:, k], y_ps[k][:, :], ACT.Identity, bias=b2_c[:, bass.ds(2 * e + k, 1)]).then_inc(y_ready, 1)
                        act.wait_ge(y_ready, 2 * e + 2)
                        wait(act, z_done, 2 * e)
                        high(y_hi[:, :, :], yf[:, :, :], yhi_ready)
                    if ahead:
                        for q, bank in enumerate((xt_ps, vp_ps)):
                            act.wait_ge(xt_done, 2 * n + q + 1)
                            wait(act, fc1_done, 8 * n)
                            high(xT_hi[:, :, q * RUN:(q + 1) * RUN].rearrange("p k (t c) -> p k t c", t=2),
                                 bank[:, :].rearrange("p (t k c) -> p k t c", t=2, k=KD), xthi_ready)
                        high_weights(n, 6)
                        high_weights(n, 7)
                    if here:
                        for m in range(2):
                            act.wait_ge(zt_ready, 4 * e + 2 * m + 2)
                            wait(act, o_ready, 2 * e + m - 1)
                            nc.scalar.activation(zg[:, m], zt[:, m], ACT.Gelu).then_inc(zg_ready, 1)
                act.wait_ge(b_loaded, 32)
                bodies(act, body)

            @block.tensor
            def _(pe):
                def parts(hi, lo, index, what):
                    return [(hi[(slice(None), index, k, what)], lo[(slice(None), index, k, what)]) for k in range(KD)]

                def turn(bank, tile, s):
                    for k in range(KD):
                        last = nc.tensor.transpose(bank[:, (KD * s + k) * P:(KD * s + k + 1) * P], tile[:, k * P:(k + 1) * P], ident[:, :])
                    return last

                def turn_results(n, q):
                    pe.wait_ge(x_loaded, 128 * n + 128)
                    if q == 0:
                        wait(pe, xtlo_ready, 2 * n - 1)
                    else:
                        pe.wait_ge(utlo_ready, 2 * n + 1)
                    for s in range(2):
                        last = turn(xt_ps, u4[:, 2 * q + s], s)
                    last.then_inc(ut_done, 1)

                def project(n, tt):
                    if tt % 2 == 0:
                        pe.wait_ge(utlo_ready, 2 * n + tt // 2 + 1)
                    if tt == 0:
                        pe.wait_ge(mtlo_ready, n + 1)
                        wait(pe, xtlo_ready, 2 * n)
                    else:
                        pe.wait_ge(vp_taken, 4 * n + tt)
                    ts = slice(tt * P, (tt + 1) * P)
                    split_product(nc, vp_ps[:, 0:D], parts(uT_hi, uT_lo, tt % 2, slice(None)), parts(w_hi, w_lo, WLV, slice(None)))
                    split_product(nc, vp_ps[:, D:2 * D], [(mT_hi[:, k, ts], mT_lo[:, k, ts]) for k in range(KD)],
                                  parts(w_hi, w_lo, WEV, slice(None))).then_inc(proj_done, 1)

                def turn_normed(n, q):
                    pe.wait_ge(xn_ready, 4 * n + 2 * q + 2)
                    if q == 0:
                        pe.wait_ge(utlo_ready, 2 * n + 2)
                    else:
                        pe.wait_ge(ntlo_ready, 2 * n + 1)
                    for s in range(2):
                        last = turn(xt_ps, xn[:, s], s)
                    last.then_inc(nt_done, 1)

                def attend(n, q):
                    pe.wait_ge(ntlo_ready, 2 * n + q + 1)
                    if q == 0:
                        wait(pe, zt_ready, 4 * n - 4)
                    else:
                        pe.wait_ge(xa_ready, 2 * n + 1)
                    for s in range(2):
                        last = split_product(nc, ap_ps[:, s * D:(s + 1) * D], parts(nT_hi, nT_lo, s, slice(None)),
                                             parts(w_hi, w_lo, WATT, slice(None)))
                    last.then_inc(att_done, 1)

                def turn_attended(n, q):
                    pe.wait_ge(xa_ready, 2 * n + q + 1)
                    if q == 0:
                        pe.wait_ge(ntlo_ready, 2 * n + 2)
                    else:
                        pe.wait_ge(vp_taken, 4 * n + 4)
                    for s in range(2):
                        last = turn((xt_ps, vp_ps)[q], xa[:, 2 * q + s], s)
                    last.then_inc(xt_done, 1)

                def first_layer(e, j):
                    pe.wait_ge(elo_ready, 8 * e + j + 1)
                    if j == 0:
                        pe.wait_ge(xtlo_ready, 2 * e + 2)
                    wait(pe, gelu_done, 8 * e + j - 1)
                    split_product(nc, h_ps[j % 2][:, :],
                                  [(e_hi[:, j, k * P:(k + 1) * P], e_lo[:, j, k * P:(k + 1) * P]) for k in range(KD)],
                                  [(xT_hi[:, k], xT_lo[:, k]) for k in range(KD)]).then_inc(fc1_done, 1)

                def second_layer(e, j):
                    pe.wait_ge(hlo_ready, 8 * e + j + 1)
                    if j == 0:
                        wait(pe, y_ready, 2 * e)
                    for k in range(KD):
                        ks = slice(D + k * P, D + (k + 1) * P)
                        last = split_product(nc, y_ps[k][:, :], [(e_hi[:, j, ks], e_lo[:, j, ks])],
                                             [(h_hi[:, j % 2], h_lo[:, j % 2])], start=j == 0, stop=j == HB - 1)
                    last.then_inc(fc2_done, 1)

                def last_layer(e, m):
                    if m == 0:
                        pe.wait_ge(ylo_ready, e + 1)
                        wait(pe, zt_ready, 4 * e - 2)
                    else:
                        wait(pe, xa_ready, 2 * e + 4 if not isinstance(e, int) or e < E - 1 else 2 * E)
                        wait(pe, zt_ready, 4 * e)
                    for s in range(2):
                        ts = slice((2 * m + s) * P, (2 * m + s + 1) * P)
                        last = split_product(nc, (zp_ps, ap_ps)[m][:, s * D:(s + 1) * D],
                                             [(y_hi[:, k, ts], y_lo[:, k, ts]) for k in range(KD)],
                                             parts(w_hi, w_lo, WNEXT, slice(None)))
                    last.then_inc(z_done, 1)

                def body(e, here=True, ahead=True):
                    n = e + 1
                    for j in range(HB):
                        if here:
                            first_layer(e, j)
                            if j > 0:
                                second_layer(e, j - 1)
                        if ahead:
                            if j == 0:
                                turn_results(n, 0)
                            if j == 1:
                                project(n, 0)
                            if j == 2:
                                project(n, 1)
                                turn_results(n, 1)
                            if j == 3:
                                project(n, 2)
                            if j == 4:
                                project(n, 3)
                            if j == 5:
                                turn_normed(n, 0)
                            if j == 6:
                                attend(n, 0)
                            if j == 7:
                                turn_normed(n, 1)
                    if here:
                        second_layer(e, HB - 1)
                    if ahead:
                        attend(n, 1)
                        turn_attended(n, 0)
                        turn_attended(n, 1)
                    if here:
                        last_layer(e, 0)
                        last_layer(e, 1)
                bodies(pe, body)


def kernel(**inputs):
    import numpy as np
    import concourse.bacc as bacc
    from concourse.bass_utils import run_bass_kernel_spmd

    def g(name):
        return np.asarray(inputs[name])

    def rows_to_columns(a, blocks):
        return a.reshape(-1, blocks, P).transpose(2, 0, 1).reshape(P, -1)

    fc1 = g("L0_ffn_fc1_w").reshape(E, HB, P, KD, P).transpose(0, 4, 1, 3, 2).reshape(E, P, HB, D)
    fc2 = g("L0_ffn_fc2_w").reshape(E, D, HB, P).transpose(0, 3, 2, 1)
    arrays = {
        "x": g("x"), "mx": g("L0_gnn_masked_x"), "mxT": g("L0_gnn_masked_x").T, "adj": g("adj"),
        "wlqT": g("L0_gnn_Wlq").T, "wlkT": g("L0_gnn_Wlk").T, "wgk": g("L0_gnn_Wgk"), "wgqT": g("L0_gnn_Wgq").T,
        "wgv": g("L0_gnn_Wgv"), "bgv": g("L0_gnn_bgv"), "wes": g("L0_gnn_Wes").reshape(D), "wlv": g("L0_gnn_Wlv"),
        "blv": g("L0_gnn_blv"), "wev": g("L0_gnn_Wev"), "bev": g("L0_gnn_bev"),
        "ln_g": rows_to_columns(g("L0_ffn_ln_g")[None], KD), "ln_b": rows_to_columns(g("L0_ffn_ln_b")[None], KD),
        "attn_wT": g("L0_ffn_attn_w").T, "attn_b": g("L0_ffn_attn_b"), "next_wT": g("L0_ffn_next_w").T, "next_b": g("L0_ffn_next_b"),
        "b1": rows_to_columns(g("L0_ffn_fc1_b"), HB), "b2": rows_to_columns(g("L0_ffn_fc2_b"), KD),
        "wffn": np.concatenate([fc1, fc2], axis=3),
    }
    nc = bacc.Bacc("TRN2", target_bir_lowering=False, num_devices=1)
    fed, args = {}, []
    for name, a in arrays.items():
        fed[f"in_{name}"] = np.ascontiguousarray(a)
        args.append(nc.dram_tensor(f"in_{name}", a.shape, mybir.dt.from_np(a.dtype), kind="ExternalInput").ap())
    args.append(nc.dram_tensor("result", (N, D), fp32, kind="ExternalOutput").ap())
    gnn_moe_kernel(nc, *args)
    r = run_bass_kernel_spmd(nc, [fed], core_ids=[0])
    return r.results[0]["result"]
```

```python
import concourse.bass as bass
from concourse import mybir
from contextlib import ExitStack

fp32 = mybir.dt.float32
fp32r = mybir.dt.float32r
uint8 = mybir.dt.uint8
ALU = mybir.AluOpType
ACT = mybir.ActivationFunctionType
AX = mybir.AxisListType

N, D, E, HID = 4096, 256, 8, 1024
P = 128
KD = D // P
NT = N // P
CH = 512
NC = N // CH
TG = CH // P
NG = N // CH
HB = HID // P
ROWU = 2 * D + 4
W_LOC, W_GLOB, W_EXT = 2 * D, 2 * D + 1, 2 * D + 2
SCALE = 1.0 / 16.0
MASKED = -1.0e9 / SCALE
EPS = 1e-5
WLV, WEV, WATT, WNEXT = range(4)


def wait(engine, semaphore, value):
    if isinstance(value, int) and value <= 0:
        return
    engine.wait_ge(semaphore, value)


def split_product(nc, out, lhs, rhs, start=True, stop=True):
    pairs = [(lh, rh, k, len(lhs)) for k, (lh, rh) in enumerate(zip(lhs, rhs))]
    for (l_hi, l_lo), (r_hi, r_lo), k, n in pairs:
        nc.tensor.matmul(out, l_hi, r_hi, start=start and k == 0, stop=False)
        nc.tensor.matmul(out, l_hi, r_lo, start=False, stop=False)
        last = nc.tensor.matmul(out, l_lo, r_hi, start=False, stop=stop and k == n - 1)
    return last


def gnn_moe_kernel(nc, x, mx, mxT, adj, wlqT, wlkT, wgk, wgqT, wgv, bgv, wes, wlv, blv, wev, bev,
                   ln_g, ln_b, attn_wT, attn_b, next_wT, next_b, b1, b2, wffn, out):
    u_dram = nc.dram_tensor("u_scratch", (NT, P, ROWU), fp32, kind="Internal").ap()
    q_dram = nc.dram_tensor("q_scratch", (NT, P, KD, P), fp32, kind="Internal").ap()

    ctx = ExitStack()
    with ctx:
        def sb(stack, name, shape, dt=fp32):
            return stack.enter_context(nc.sbuf_tensor(name, shape, dt))

        def ps(stack, name, shape=(P, CH)):
            return stack.enter_context(nc.psum_tensor(name, list(shape), fp32))

        def sem(name):
            return ctx.enter_context(nc.semaphore(name))

        ident = sb(ctx, "ident", [P, P])
        w_hi = sb(ctx, "w_hi", [P, 4, KD, D], fp32r)
        w_lo = sb(ctx, "w_lo", [P, 4, KD, D], fp32r)
        blv_b = sb(ctx, "blv_b", [P, D])
        bev_b = sb(ctx, "bev_b", [P, D])
        gv_b = sb(ctx, "gv_b", [P, D])
        attc_b = sb(ctx, "attc_b", [P, D])
        nextb_b = sb(ctx, "nextb_b", [P, D])
        wes_b = sb(ctx, "wes_b", [P, D])
        wg_b = sb(ctx, "wg_b", [P, D])

        ab = ctx.enter_context(ExitStack())
        lnT_hi = sb(ab, "lnT_hi", [P, KD, N], fp32r)
        lnT_lo = sb(ab, "lnT_lo", [P, KD, N], fp32r)
        v_sp = sb(ab, "v_sp", [P, NT, 2 * D], fp32r)

        a = ab.enter_context(ExitStack())
        xg = sb(a, "xg", [P, 2, TG, D])
        lnf = sb(a, "lnf", [P, 2, TG, D])
        st6 = sb(a, "st6", [P, TG, 6])
        mv = sb(a, "mv", [P, 2, TG, 2])
        veps = sb(a, "veps", [P, TG])
        mhalf = sb(a, "mhalf", [P, TG])
        rstd = sb(a, "rstd", [P, 2, TG])
        mg = sb(a, "mg", [P, KD, CH])
        mg_hi = sb(a, "mg_hi", [P, KD, CH], fp32r)
        mg_lo = sb(a, "mg_lo", [P, KD, CH], fp32r)
        q_out = sb(a, "q_out", [P, KD, CH])
        qw_hi = sb(a, "qw_hi", [P, KD, D], fp32r)
        qw_lo = sb(a, "qw_lo", [P, KD, D], fp32r)
        qw_f = sb(a, "qw_f", [P, KD, D])
        wq_in = sb(a, "wq_in", [P, 2, KD, D])
        wgv_in = sb(a, "wgv_in", [P, KD, D])
        w_in = sb(a, "w_in", [P, 4, KD, D])
        lng = sb(a, "lng", [P, KD])
        lnb = sb(a, "lnb", [P, KD])
        xsum = sb(a, "xsum", [P, KD, NG])
        xbar = sb(a, "xbar", [P, KD])
        gk = sb(a, "gk", [P, KD])
        cols_b = sb(a, "cols_b", [P, 3, KD, P])
        ones = sb(a, "ones", [P, P])

        pa = ExitStack()
        tr_ps = [ps(pa, f"tr_ps{k}") for k in range(KD)]
        q_ps = [ps(pa, f"q_ps{k}") for k in range(KD)]
        qw_ps = ps(pa, "qw_ps", (P, CH))
        gk_ps = ps(pa, "gk_ps", (P, CH))
        row_ps = ps(pa, "row_ps", (P, CH))
        attc_ps = ps(pa, "attc_ps", (P, CH))

        x_in = [sem(f"x_in{i}") for i in range(2)]
        mg_in = sem("mg_in")
        wq_loaded, wg_loaded, w_loaded, rows_loaded = (sem(n) for n in ("wq_loaded", "wg_loaded", "w_loaded", "rows_loaded"))
        ident_ready, half_ready = sem("ident_ready"), sem("half_ready")
        stats_done, mv_ready, veps_ready, rstd_ready, ln_ready = (
            sem(n) for n in ("stats_done", "mv_ready", "veps_ready", "rstd_ready", "ln_ready"))
        vhi_ready, vlo_ready, tr_done, thi_ready, tlo_ready = (
            sem(n) for n in ("vhi_ready", "vlo_ready", "tr_done", "thi_ready", "tlo_ready"))
        mhi_ready, mlo_ready, q_done, q_copied, q_stored = (
            sem(n) for n in ("mhi_ready", "mlo_ready", "q_done", "q_copied", "q_stored"))
        qw_done, qwf_ready, qwhi_ready, qwlo_ready = (sem(n) for n in ("qw_done", "qwf_ready", "qwhi_ready", "qwlo_ready"))
        xs_ready, xbar_ready, gk_done, gk_ready, cols_ready, attcols_ready, rows_done, attc_done = (
            sem(n) for n in ("xs_ready", "xbar_ready", "gk_done", "gk_ready", "cols_ready", "attcols_ready", "rows_done", "attc_done"))
        attg_ready, whi_ready = sem("attg_ready"), sem("whi_ready")

        settled = {}

        def settle(engine):
            if engine.engine not in settled:
                settled[engine.engine] = sem(f"settled_{len(settled)}")
            engine.sem_inc(settled[engine.engine], 1)

        def kblocks(ap):
            return ap.rearrange("(k p) n -> p k n", p=P)

        def groups(eng, group):
            for pp in range(2):
                group(0, pp)
            with eng.Fori(1, NG // 2) as h:
                for pp in range(2):
                    group(h, pp)

        with nc.Block() as block:
            @block.sync
            def _(sp):
                sp.dma_start(xg[:, 0], x[0:CH].rearrange("(t p) d -> p t d", p=P)).then_inc(x_in[0], 16)
                for n, w in enumerate((wlqT, wlkT)):
                    sp.dma_start(wq_in[:, n], kblocks(w)).then_inc(wq_loaded, 16)
                sp.dma_start(xg[:, 1], x[CH:2 * CH].rearrange("(t p) d -> p t d", p=P)).then_inc(x_in[1], 16)
                sp.dma_start(mg[:, :, :], mxT[:, 0:CH].rearrange("(k p) q -> p k q", p=P)).then_inc(mg_in, 16)
                sp.dma_start(lng[:, :], ln_g).then_inc(rows_loaded, 16)
                sp.dma_start(lnb[:, :], ln_b).then_inc(rows_loaded, 16)
                for n, w in enumerate((wlv, wev, attn_wT, next_wT)):
                    sp.dma_start(w_in[:, n], kblocks(w)).then_inc(w_loaded, 16)
                sp.dma_start(wgv_in[:, :, :], kblocks(wgv)).then_inc(wg_loaded, 16)
                for dst, row in ((blv_b, blv), (bev_b, bev), (gv_b, bgv), (attc_b, attn_b), (nextb_b, next_b), (wes_b, wes)):
                    sp.dma_start(dst[:, :], row.partition_broadcast(P)).then_inc(rows_loaded, 16)

                sp.wait_ge(qw_done, 1)
                for n, w in enumerate((wgk, wgqT)):
                    sp.dma_start(wq_in[:, n], kblocks(w)).then_inc(wg_loaded, 16)

                def group(g, pp, more_x, more_m):
                    if more_x:
                        sp.wait_ge(ln_ready, g + 1)
                        settle(sp)
                        sp.dma_start(xg[:, pp], x[bass.ds((g + 2) * CH, CH)].rearrange("(t p) d -> p t d", p=P)).then_inc(x_in[pp], 16)
                    if more_m:
                        sp.wait_ge(mlo_ready, g + 1)
                        settle(sp)
                        sp.dma_start(mg[:, :, :], mxT[:, bass.ds((g + 1) * CH, CH)].rearrange("(k p) q -> p k q", p=P)).then_inc(mg_in, 16)
                    sp.wait_ge(q_copied, 2 * g + 2)
                    settle(sp)
                    for k in range(KD):
                        sp.dma_start(q_dram[bass.ds(g * TG, TG), :, k, :].rearrange("t p q -> p t q"),
                                     q_out[:, k, :].rearrange("p (t q) -> p t q", q=P)).then_inc(q_stored, 16)

                with sp.Fori(0, NG // 2 - 1) as h:
                    for pp in range(2):
                        group(2 * h + pp, pp, True, True)
                group(NG - 2, 0, False, True)
                group(NG - 1, 1, False, False)
                sp.wait_ge(q_stored, 32 * NG)

            @block.gpsimd
            def _(pool):
                nc.gpsimd.memset(ident[:, :], 0.0).then_inc(ident_ready, 1)
                nc.gpsimd.memset(mhalf[:, :], -0.5).then_inc(half_ready, 1)
                nc.gpsimd.memset(ones[:, :], 1.0).then_inc(half_ready, 1)
                pool.wait_ge(ident_ready, 1)
                nc.gpsimd.affine_select(out=ident[:, :], in_=ident[:, :], compare_op=ALU.not_equal, fill=1.0, base=0,
                                        pattern=[[-1, P]], channel_multiplier=1).then_inc(ident_ready, 1)
                pool.wait_ge(half_ready, 2)

                def group(h, pp):
                    g = 2 * h + pp
                    pool.wait_ge(mv_ready, 4 * g + 4)
                    settle(pool)
                    nc.gpsimd.tensor_scalar(veps[:, :], mv[:, pp, :, 1], EPS, 0.0, ALU.add, ALU.add).then_inc(veps_ready, 1)
                    pool.wait_ge(veps_ready, g + 1)
                    nc.gpsimd.tensor_tensor(out=rstd[:, pp, :], in0=veps[:, :], in1=mhalf[:, :], op=ALU.pow).then_inc(rstd_ready, 1)
                    pool.wait_ge(vhi_ready, g + 1)
                    nc.gpsimd.tensor_tensor(out=v_sp[:, bass.ds(g * TG, TG), D:2 * D], in0=lnf[:, pp],
                                            in1=v_sp[:, bass.ds(g * TG, TG), 0:D].bitcast(fp32), op=ALU.subtract).then_inc(vlo_ready, 1)
                groups(pool, group)

            @block.vector
            def _(dve):
                dve.wait_ge(qwhi_ready, 1)
                nc.vector.tensor_tensor(qw_lo[:, :, :], qw_f[:, :, :], qw_hi[:, :, :].bitcast(fp32), ALU.subtract).then_inc(qwlo_ready, 1)
                def group(h, pp):
                    g = 2 * h + pp
                    dve.wait_ge(x_in[pp], 16 * h + 16)
                    for j in range(TG):
                        nc.vector.bn_stats(st6[:, j], xg[:, pp, j]).then_inc(stats_done, 1)
                    dve.wait_ge(stats_done, 4 * g + 4)
                    settle(dve)
                    for j in range(TG):
                        nc.vector.bn_aggr(mv[:, pp, j], st6[:, j]).then_inc(mv_ready, 1)
                    dve.wait_ge(mhi_ready, g + 1)
                    nc.vector.tensor_tensor(mg_lo[:, :, :], mg[:, :, :], mg_hi[:, :, :].bitcast(fp32), ALU.subtract).then_inc(mlo_ready, 1)
                    dve.wait_ge(rstd_ready, g + 1)
                    for j in range(TG):
                        last = nc.vector.tensor_scalar(lnf[:, pp, j], xg[:, pp, j], mv[:, pp, j, 0:1], rstd[:, pp, j:j + 1],
                                                       ALU.subtract, ALU.mult)
                    last.then_inc(ln_ready, 1)
                    for k in range(KD):
                        dve.wait_ge(thi_ready, 2 * g + k + 1)
                        nc.vector.tensor_tensor(lnT_lo[:, k, bass.ds(g * CH, CH)], tr_ps[k][:, :],
                                                lnT_hi[:, k, bass.ds(g * CH, CH)].bitcast(fp32), ALU.subtract).then_inc(tlo_ready, 1)
                groups(dve, group)

                dve.wait_ge(thi_ready, 2 * NG)
                nc.vector.tensor_reduce(xbar[:, :], xsum[:, :, :], AX.X, ALU.add).then_inc(xs_ready, 1)
                dve.wait_ge(xs_ready, 1)
                nc.vector.tensor_scalar(xbar[:, :], xbar[:, :], 1.0 / N, None, ALU.mult).then_inc(xbar_ready, 1)
                dve.wait_ge(xbar_ready, 1)
                dve.wait_ge(half_ready, 2)
                for k in range(KD):
                    nc.vector.tensor_scalar(cols_b[:, 0, k], ones[:, :], xbar[:, k:k + 1], None, ALU.mult).then_inc(cols_ready, 1)
                dve.wait_ge(gk_done, 1)
                nc.vector.tensor_copy(gk[:, :], gk_ps[:, 0:KD]).then_inc(gk_ready, 1)
                dve.wait_ge(gk_ready, 1)
                for k in range(KD):
                    nc.vector.tensor_scalar(cols_b[:, 1, k], ones[:, :], gk[:, k:k + 1], None, ALU.mult).then_inc(cols_ready, 1)
                dve.wait_ge(rows_loaded, 16 * 8)
                dve.wait_ge(rows_done, 1)
                nc.vector.tensor_tensor(gv_b[:, :], row_ps[:, 0:D], gv_b[:, :], ALU.add)
                nc.vector.tensor_copy(wg_b[:, :], row_ps[:, D:2 * D])
                dve.wait_ge(attc_done, 1)
                nc.vector.tensor_tensor(attc_b[:, :], attc_ps[:, 0:D], attc_b[:, :], ALU.add)
                dve.wait_ge(whi_ready, 1)
                nc.vector.tensor_tensor(w_lo[:, :, :, :], w_in[:, :, :, :], w_hi[:, :, :, :].bitcast(fp32), ALU.subtract)

            @block.scalar
            def _(act):
                act.wait_ge(qw_done, 1)
                nc.scalar.activation(qw_f[:, :, :], qw_ps[:, :].rearrange("p (k n) -> p k n", k=KD), ACT.Copy).then_inc(qwf_ready, 1)
                act.wait_ge(qwf_ready, 1)
                nc.scalar.activation(qw_hi[:, :, :], qw_f[:, :, :], ACT.Copy).then_inc(qwhi_ready, 1)
                act.wait_ge(qwhi_ready, 1)
                act.wait_ge(rows_loaded, 16 * 8)
                act.wait_ge(w_loaded, 64)
                act.wait_ge(half_ready, 2)
                for k in range(KD):
                    nc.scalar.activation(cols_b[:, 2, k], ones[:, :], ACT.Copy, scale=lnb[:, k:k + 1]).then_inc(attcols_ready, 1)
                act.wait_ge(attc_done, 1)
                for k in range(KD):
                    nc.scalar.activation(w_in[:, WATT, k], w_in[:, WATT, k], ACT.Copy, scale=lng[:, k:k + 1]).then_inc(attg_ready, 1)
                act.wait_ge(attg_ready, 2)
                nc.scalar.activation(w_hi[:, :, :, :], w_in[:, :, :, :], ACT.Copy).then_inc(whi_ready, 1)

                def group(h, pp):
                    g = 2 * h + pp

                    act.wait_ge(mg_in, 16 * g + 16)
                    wait(act, q_done, 2 * g)
                    nc.scalar.activation(mg_hi[:, :, :], mg[:, :, :], ACT.Copy).then_inc(mhi_ready, 1)
                    act.wait_ge(ln_ready, g + 1)
                    nc.scalar.activation(v_sp[:, bass.ds(g * TG, TG), 0:D], lnf[:, pp], ACT.Copy).then_inc(vhi_ready, 1)
                    for k in range(KD):
                        act.wait_ge(tr_done, 2 * g + k + 1)
                        nc.scalar.activation(lnT_hi[:, k, bass.ds(g * CH, CH)], tr_ps[k][:, :], ACT.Copy,
                                             accum_out=xsum[:, k, bass.ds(g, 1)]).then_inc(thi_ready, 1)
                    wait(act, q_stored, 32 * g)
                    for k in range(KD):
                        act.wait_ge(q_done, 2 * g + k + 1)
                        nc.scalar.activation(q_out[:, k, :], q_ps[k][:, :], ACT.Copy).then_inc(q_copied, 1)
                groups(act, group)

            @block.tensor
            def _(pe):
                pe.wait_ge(wq_loaded, 32)
                for m in range(KD):
                    for k in range(KD):
                        last = nc.tensor.matmul(qw_ps[:, m * D:(m + 1) * D], wq_in[:, 0, k, m * P:(m + 1) * P], wq_in[:, 1, k, :],
                                                start=k == 0, stop=k == KD - 1)
                last.then_inc(qw_done, 1)
                pe.wait_ge(attcols_ready, 2)
                for k in range(KD):
                    last = nc.tensor.matmul(attc_ps[:, 0:D], cols_b[:, 2, k], w_in[:, WATT, k], start=k == 0, stop=k == KD - 1)
                last.then_inc(attc_done, 1)
                pe.wait_ge(qwlo_ready, 1)
                pe.wait_ge(ident_ready, 2)

                def group(h, pp):
                    g = 2 * h + pp
                    pe.wait_ge(ln_ready, g + 1)
                    wait(pe, tlo_ready, 2 * g)
                    for k in range(KD):
                        for j in range(TG):
                            last = nc.tensor.transpose(tr_ps[k][:, j * P:(j + 1) * P], lnf[:, pp, j, k * P:(k + 1) * P], ident[:, :])
                        last.then_inc(tr_done, 1)
                    pe.wait_ge(mlo_ready, g + 1)
                    wait(pe, q_copied, 2 * g)
                    for m in range(KD):
                        ms = slice(m * P, (m + 1) * P)
                        split_product(nc, q_ps[m][:, :],
                                      [(qw_hi[:, k, ms], qw_lo[:, k, ms]) for k in range(KD)],
                                      [(mg_hi[:, k], mg_lo[:, k]) for k in range(KD)]).then_inc(q_done, 1)
                groups(pe, group)

                pe.wait_ge(wg_loaded, 48)
                pe.wait_ge(xbar_ready, 1)
                for m in range(KD):
                    for k in range(KD):
                        last = nc.tensor.matmul(gk_ps[:, m:m + 1], wq_in[:, 0, k, m * P:(m + 1) * P], xbar[:, k:k + 1],
                                                start=k == 0, stop=k == KD - 1)
                last.then_inc(gk_done, 1)
                pe.wait_ge(cols_ready, 4)
                for n, w in enumerate((wgv_in, wq_in[:, 1])):
                    for k in range(KD):
                        last = nc.tensor.matmul(row_ps[:, n * D:(n + 1) * D], cols_b[:, n, k], w[:, k, :],
                                                start=k == 0, stop=k == KD - 1)
                last.then_inc(rows_done, 1)
        pa.close()
        a.close()

        b = ab.enter_context(ExitStack())
        scores = sb(b, "scores", [P, N])
        adj8 = sb(b, "adj8", [P, N], uint8)
        bias = sb(b, "bias", [P, 2, 2 * CH])
        q_in = sb(b, "q_in", [P, KD, P])
        q_hi = sb(b, "q_hi", [P, KD, P], fp32r)
        q_lo = sb(b, "q_lo", [P, KD, P], fp32r)
        mxt = sb(b, "mxt", [P, D])
        dotted = sb(b, "dotted", [P, 2, D])
        p_hi = sb(b, "p_hi", [P, 2, CH], fp32r)
        p_lo = sb(b, "p_lo", [P, 2, CH], fp32r)
        tops = sb(b, "tops", [P, NC + 2])
        neg_top = sb(b, "neg_top", [P, 1])
        sums = sb(b, "sums", [P, 6])
        den = sb(b, "den", [P, 1])
        local_sum = sb(b, "local_sum", [P, 1])
        rden = sb(b, "rden", [P, 1])
        u_part = sb(b, "u_part", [P, D])
        u_out = sb(b, "u_out", [P, ROWU])
        kt_b = sb(b, "kt_b", [P, 3, D])

        pb = ExitStack()
        s_ps = [ps(pb, f"s_ps{i}") for i in range(2)]
        pt_ps = [ps(pb, f"pt_ps{i}") for i in range(2)]
        u_ps = ps(pb, "u_ps")

        adj_in = [sem(f"adj_in{i}") for i in range(2)]
        q_loaded, mx_loaded, u_stored = sem("q_loaded"), sem("mx_loaded"), sem("u_stored")
        bias_ready, qhi_ready, qlo_ready = sem("bias_ready"), sem("qhi_ready"), sem("qlo_ready")
        score_done, score_masked, extra_dotted, extra_ready, top_ready = (
            sem(n) for n in ("score_done", "score_masked", "extra_dotted", "extra_ready", "top_ready"))
        exp_done, extra_exp, den_ready, rden_ready, coef_ready = (
            sem(n) for n in ("exp_done", "extra_exp", "den_ready", "rden_ready", "coef_ready"))
        pt_done, phi_ready, plo_ready, pv_done, upart_ready, u_ready = (
            sem(n) for n in ("pt_done", "phi_ready", "plo_ready", "pv_done", "upart_ready", "u_ready"))
        kpart_ready, ksum_ready, kt_ready = sem("kpart_ready"), sem("ksum_ready"), sem("kt_ready")

        def steps(eng, step):
            step(-1, here=False)
            step(0)
            with eng.Fori(1, NT - 2) as t:
                step(t)
            step(NT - 2, after=False)
            step(NT - 1, ahead=False, after=False)

        with nc.Block() as block:
            @block.sync
            def _(sp):
                def load_tile(n):
                    wait(sp, qlo_ready, n)
                    settle(sp)
                    sp.dma_start(q_in[:, :, :], q_dram[n]).then_inc(q_loaded, 16)
                    for h in range(2):
                        wait(sp, bias_ready, 4 * n + 2 * h - 2)
                        settle(sp)
                        sp.dma_start(adj8[:, h * (N // 2):(h + 1) * (N // 2)],
                                     adj[bass.ds(n * P, P), h * (N // 2):(h + 1) * (N // 2)]).then_inc(adj_in[h], 16)
                    wait(sp, extra_dotted, 2 * n)
                    settle(sp)
                    sp.dma_start(mxt[:, :], mx[bass.ds(n * P, P)]).then_inc(mx_loaded, 16)

                def step(t, here=True, ahead=True, after=True):
                    if after:
                        load_tile(t + 2)
                    if here:
                        sp.wait_ge(kt_ready, t + 1)
                        settle(sp)
                        sp.wait_ge(u_ready, t + 1)
                        settle(sp)
                        sp.dma_start(u_dram[t], u_out[:, :]).then_inc(u_stored, 16)

                load_tile(0)
                steps(sp, step)
                sp.wait_ge(u_stored, 16 * NT)

            @block.gpsimd
            def _(pool):
                def rank_one(t):
                    pool.wait_ge(coef_ready, 2 * t + 2)
                    wait(pool, kt_ready, t)
                    settle(pool)
                    for r, row in enumerate((blv_b, gv_b, bev_b)):
                        nc.gpsimd.tensor_scalar(kt_b[:, r], row[:, :], u_out[:, W_LOC + r:W_LOC + r + 1], 0.0,
                                                ALU.mult, ALU.add).then_inc(kpart_ready, 1)
                    pool.wait_ge(kpart_ready, 3 * t + 3)
                    nc.gpsimd.tensor_tensor(out=u_out[:, D:2 * D], in0=kt_b[:, 0], in1=kt_b[:, 1], op=ALU.add).then_inc(ksum_ready, 1)
                    pool.wait_ge(ksum_ready, t + 1)
                    nc.gpsimd.tensor_tensor(out=u_out[:, D:2 * D], in0=u_out[:, D:2 * D], in1=kt_b[:, 2], op=ALU.add).then_inc(kt_ready, 1)

                def step(t, here=True, ahead=True, after=True):
                    n = t + 1
                    for c in range(4):
                        if ahead:
                            if c % 2 == 0:
                                pool.wait_ge(adj_in[c // 2], 16 * n + 16)
                            wait(pool, score_masked, 8 * n + 2 * c - 2)
                            settle(pool)
                            nc.gpsimd.tensor_scalar(bias[:, c % 2], adj8[:, c * 2 * CH:(c + 1) * 2 * CH], -MASKED, MASKED,
                                                    ALU.mult, ALU.add).then_inc(bias_ready, 1)
                        if here and c == 2:
                            rank_one(t)
                steps(pool, step)

            @block.vector
            def _(dve):
                def q_low(n):
                    dve.wait_ge(qhi_ready, n + 1)
                    nc.vector.tensor_tensor(q_lo[:, :, :], q_in[:, :, :], q_hi[:, :, :].bitcast(fp32), ALU.subtract).then_inc(qlo_ready, 1)

                def step(t, here=True, ahead=True, after=True):
                    n = t + 1
                    for c in range(NC):
                        if here:
                            dve.wait_ge(phi_ready, 8 * t + c + 1)
                            wait(dve, pv_done, 8 * t + c - 1)
                            nc.vector.tensor_tensor(p_lo[:, c % 2], pt_ps[c % 2][:, :], p_hi[:, c % 2].bitcast(fp32),
                                                    ALU.subtract).then_inc(plo_ready, 1)
                        if ahead:
                            dve.wait_ge(score_done, 8 * n + c + 1)
                            dve.wait_ge(bias_ready, 4 * n + c // 2 + 1)
                            settle(dve)
                            nc.vector.tensor_tensor_reduce(out=scores[:, c * CH:(c + 1) * CH], in0=s_ps[c % 2][:, :],
                                                           in1=bias[:, c // 2 % 2, c % 2 * CH:(c % 2 + 1) * CH],
                                                           scale=SCALE, scalar=-3.0e38, op0=ALU.add, op1=ALU.max,
                                                           accum_out=tops[:, c:c + 1]).then_inc(score_masked, 1)
                        if here and c == 3:
                            dve.wait_ge(exp_done, 4 * t + 4)
                            dve.wait_ge(extra_exp, t + 1)
                            nc.vector.tensor_reduce(den[:, :], sums[:, 0:6], AX.X, ALU.add).then_inc(den_ready, 1)
                            nc.vector.tensor_reduce(local_sum[:, :], sums[:, 0:4], AX.X, ALU.add).then_inc(den_ready, 1)
                            dve.wait_ge(den_ready, 2 * t + 2)
                            nc.vector.reciprocal(rden[:, :], den[:, :]).then_inc(rden_ready, 1)
                            dve.wait_ge(rden_ready, t + 1)
                            wait(dve, u_stored, 16 * t)
                            nc.vector.tensor_scalar(u_out[:, W_LOC:W_LOC + 1], local_sum[:, :], rden[:, :], None, ALU.mult).then_inc(coef_ready, 1)
                            nc.vector.tensor_scalar(u_out[:, W_GLOB:W_EXT + 1], sums[:, 4:6], rden[:, :], None, ALU.mult).then_inc(coef_ready, 1)
                            if isinstance(t, int) and t == 0:
                                nc.vector.memset(u_out[:, W_EXT + 1:ROWU], 0.0)
                        if ahead and c == 5:
                            dve.wait_ge(mx_loaded, 16 * n + 16)
                            wait(dve, extra_exp, n)
                            nc.vector.tensor_tensor_reduce(out=dotted[:, 0], in0=mxt[:, :], in1=wg_b[:, :], scale=SCALE, scalar=0.0,
                                                           op0=ALU.mult, op1=ALU.add, accum_out=tops[:, NC:NC + 1]).then_inc(extra_dotted, 1)
                            nc.vector.tensor_tensor_reduce(out=dotted[:, 1], in0=mxt[:, :], in1=wes_b[:, :], scale=1.0, scalar=0.0,
                                                           op0=ALU.mult, op1=ALU.add, accum_out=tops[:, NC + 1:NC + 2]).then_inc(extra_dotted, 1)
                    if ahead:
                        dve.wait_ge(score_masked, 8 * n + 8)
                        dve.wait_ge(extra_dotted, 2 * n + 2)
                        nc.vector.tensor_reduce(neg_top[:, :], tops[:, :], AX.X, ALU.max, negate=True).then_inc(top_ready, 1)
                    if after:
                        q_low(t + 2)
                    if here:
                        dve.wait_ge(upart_ready, t + 1)
                        nc.vector.scalar_tensor_tensor(out=u_out[:, 0:D], in0=u_ps[:, 0:D], scalar=rden[:, :], in1=u_part[:, :],
                                                       op0=ALU.mult, op1=ALU.add).then_inc(u_ready, 1)
                q_low(0)
                steps(dve, step)

            @block.scalar
            def _(act):
                def q_high(n):
                    act.wait_ge(q_loaded, 16 * n + 16)
                    wait(act, score_done, 8 * n)
                    nc.scalar.activation(q_hi[:, :, :], q_in[:, :, :], ACT.Copy).then_inc(qhi_ready, 1)

                def exponentials(part):
                    span = slice(part * 2 * CH, (part + 1) * 2 * CH)
                    nc.scalar.activation(scores[:, span], scores[:, span], ACT.Exp, bias=neg_top[:, :],
                                         accum_out=sums[:, part:part + 1]).then_inc(exp_done, 1)

                def step(t, here=True, ahead=True, after=True):
                    n = t + 1
                    if here:
                        for c in range(NC):
                            act.wait_ge(pt_done, 8 * t + c + 1)
                            wait(act, pv_done, 8 * t + c - 1)
                            nc.scalar.activation(p_hi[:, c % 2], pt_ps[c % 2][:, :], ACT.Copy).then_inc(phi_ready, 1)
                            if c < 2:
                                exponentials(2 + c)
                            if c == 1:
                                nc.scalar.activation(sums[:, 4:6], tops[:, NC:NC + 2], ACT.Exp, bias=neg_top[:, :]).then_inc(extra_exp, 1)
                    if after:
                        q_high(t + 2)
                    if ahead:
                        act.wait_ge(top_ready, n + 1)
                        exponentials(0)
                    if here:
                        act.wait_ge(pv_done, 8 * t + 8)
                        act.wait_ge(rden_ready, t + 1)
                        nc.scalar.activation(u_part[:, :], u_ps[:, D:2 * D], ACT.Copy, scale=rden[:, :]).then_inc(upart_ready, 1)
                    if ahead:
                        exponentials(1)
                q_high(0)
                steps(act, step)

            @block.tensor
            def _(pe):
                def weigh(t, c):
                    pe.wait_ge(plo_ready, 8 * t + c + 1)
                    if c == 0:
                        wait(pe, u_ready, t)
                    for j in range(TG):
                        js = slice(j * P, (j + 1) * P)
                        nc.tensor.matmul(u_ps[:, :], p_hi[:, c % 2, js], v_sp[:, c * TG + j, :], start=c + j == 0, stop=False)
                        last = nc.tensor.matmul(u_ps[:, 0:D], p_lo[:, c % 2, js], v_sp[:, c * TG + j, 0:D],
                                                start=False, stop=c * TG + j == NT - 1)
                    last.then_inc(pv_done, 1)

                def step(t, here=True, ahead=True, after=True):
                    n = t + 1
                    for c in range(NC):
                        if here:
                            if c % 2 == 0:
                                pe.wait_ge(exp_done, 4 * t + c // 2 + 1)
                            wait(pe, plo_ready, 8 * t + c - 1)
                            for j in range(TG):
                                last = nc.tensor.transpose(pt_ps[c % 2][:, j * P:(j + 1) * P],
                                                           scores[:, (c * TG + j) * P:(c * TG + j + 1) * P], ident[:, :])
                            last.then_inc(pt_done, 1)
                        if ahead:
                            if c == 0:
                                pe.wait_ge(qlo_ready, n + 1)
                            wait(pe, score_masked, 8 * n + c - 1)
                            cs = slice(c * CH, (c + 1) * CH)
                            split_product(nc, s_ps[c % 2][:, :], [(q_hi[:, k], q_lo[:, k]) for k in range(KD)],
                                          [(lnT_hi[:, k, cs], lnT_lo[:, k, cs]) for k in range(KD)]).then_inc(score_done, 1)
                        if here and c > 0:
                            weigh(t, c - 1)
                    if here:
                        weigh(t, NC - 1)
                steps(pe, step)
        pb.close()
        ab.close()

        HR = 4
        raw = sb(ctx, "raw", [P, HB, 2 * D])
        e_hi = sb(ctx, "e_hi", [P, HB, 2 * D], fp32r)
        e_lo = sb(ctx, "e_lo", [P, HB, 2 * D], fp32r)
        b1_c = sb(ctx, "b1_c", [P, E * HB])
        b2_c = sb(ctx, "b2_c", [P, E * KD])
        mhalf2 = sb(ctx, "mhalf2", [P, 2])
        u4 = sb(ctx, "u4", [P, TG, ROWU])
        mx4 = sb(ctx, "mx4", [P, TG, D])
        x4 = sb(ctx, "x4", [P, TG, D])
        mT = sb(ctx, "mT", [P, KD, CH])
        mT_hi = sb(ctx, "mT_hi", [P, KD, CH], fp32r)
        mT_lo = sb(ctx, "mT_lo", [P, KD, CH], fp32r)
        uT_hi = sb(ctx, "uT_hi", [P, 2, KD, P], fp32r)
        uT_lo = sb(ctx, "uT_lo", [P, 2, KD, P], fp32r)
        comb = sb(ctx, "comb", [P, 2, D])
        res = sb(ctx, "res", [P, TG, D])
        resm = sb(ctx, "resm", [P, 2, D])
        x1_next = sb(ctx, "x1_next", [P, TG, D])
        x1_mid = sb(ctx, "x1_mid", [P, TG, D])
        x1_here = sb(ctx, "x1_here", [P, TG, D])
        cst6 = sb(ctx, "cst6", [P, 4, 2, 6])
        cmv = sb(ctx, "cmv", [P, 4, 2, 2])
        cve = sb(ctx, "cve", [P, 4, 2])
        crstd = sb(ctx, "crstd", [P, 4, 2])
        xf = sb(ctx, "xf", [P, TG, D])
        xn = sb(ctx, "xn", [P, TG, D])
        xfa = sb(ctx, "xfa", [P, TG, D])
        nT_hi = sb(ctx, "nT_hi", [P, 2, KD, P], fp32r)
        nT_lo = sb(ctx, "nT_lo", [P, 2, KD, P], fp32r)
        xa = sb(ctx, "xa", [P, TG, D])
        xT_hi = sb(ctx, "xT_hi", [P, KD, CH], fp32r)
        xT_lo = sb(ctx, "xT_lo", [P, KD, CH], fp32r)
        hf = sb(ctx, "hf", [P, HR, CH])
        h_hi = sb(ctx, "h_hi", [P, HR, CH], fp32r)
        h_lo = sb(ctx, "h_lo", [P, HR, CH], fp32r)
        yf = sb(ctx, "yf", [P, KD, CH])
        y_hi = sb(ctx, "y_hi", [P, KD, CH], fp32r)
        y_lo = sb(ctx, "y_lo", [P, KD, CH], fp32r)
        zt = sb(ctx, "zt", [P, 2, 2, D])
        zg = sb(ctx, "zg", [P, 2, 2, D])
        o4 = sb(ctx, "o4", [P, 2, 2, D])

        h_ps = [ps(ctx, f"h_ps{i}") for i in range(2)]
        y_ps = [ps(ctx, f"y_ps{i}") for i in range(KD)]
        xt_ps = ps(ctx, "xt_ps")
        vp_ps = ps(ctx, "vp_ps")
        ap_ps = ps(ctx, "ap_ps")
        zp_ps = ps(ctx, "zp_ps")

        x_loaded, b_loaded = sem("x_loaded"), sem("b_loaded")
        raw_in = [sem(f"raw_in{i}") for i in range(4)]
        out_stored = [sem(f"out_stored{i}") for i in range(2)]
        (ehi_ready, elo_ready, mthi_ready, mtlo_ready, ut_done, uthi_ready, utlo_ready,
         proj_done, comb_ready, vp_taken, resm_ready, x1_ready) = (sem(n) for n in (
             "ehi_ready", "elo_ready", "mthi_ready", "mtlo_ready", "ut_done", "uthi_ready",
             "utlo_ready", "proj_done", "comb_ready", "vp_taken", "resm_ready", "x1_ready"))
        (half2_ready, cst_done, cmv_ready, cve_ready, crstd_ready, xf_ready, xn_ready, xfa_ready, nt_done, nthi_ready, ntlo_ready,
         att_done, xa_ready, xt_done, xthi_ready, xtlo_ready) = (sem(n) for n in (
             "half2_ready", "cst_done", "cmv_ready", "cve_ready", "crstd_ready", "xf_ready", "xn_ready", "xfa_ready", "nt_done",
             "nthi_ready", "ntlo_ready", "att_done", "xa_ready", "xt_done", "xthi_ready", "xtlo_ready"))
        (fc1_done, gelu_done, hhi_ready, hlo_ready, fc2_done, y_ready, yhi_ready, ylo_ready, z_done, zt_ready, zg_ready, o_ready,
         x1_saved, x1_moved) = (sem(n) for n in (
             "fc1_done", "gelu_done", "hhi_ready", "hlo_ready", "fc2_done", "y_ready", "yhi_ready", "ylo_ready", "z_done",
             "zt_ready", "zg_ready", "o_ready", "x1_saved", "x1_moved"))

        def bodies(eng, body):
            body(-1, here=False, past=False)
            body(0, past=False)
            body(1)
            with eng.Fori(2, E - 2) as e:
                body(e)
            body(E - 2, beyond=False)
            body(E - 1, ahead=False, beyond=False)
            body(E, here=False, ahead=False, beyond=False)

        RUN = 2 * P

        with nc.Block() as block:
            @block.sync
            def _(sp):
                def load_weights(e, i):
                    wait(sp, elo_ready, 8 * e - 6 + 2 * i)
                    settle(sp)
                    sp.dma_start(raw[:, 2 * i:2 * i + 2], wffn[e, :, 2 * i:2 * i + 2]).then_inc(raw_in[i], 16)

                def load_tokens(n):
                    wait(sp, x1_ready, 2 * n)
                    settle(sp)
                    for m in range(2):
                        row = m * (N // 2) + n * RUN
                        tiles = slice(2 * m, 2 * m + 2)
                        sp.dma_start(u4[:, tiles], u_dram[bass.ds(m * (NT // 2) + 2 * n, 2)].rearrange("t p c -> p t c")).then_inc(x_loaded, 16)
                        sp.dma_start(mT[:, :, m * RUN:(m + 1) * RUN], mxT[:, bass.ds(row, RUN)].rearrange("(k p) q -> p k q", p=P)).then_inc(x_loaded, 16)
                        sp.dma_start(mx4[:, tiles], mx[bass.ds(row, RUN)].rearrange("(t p) d -> p t d", p=P)).then_inc(x_loaded, 16)
                        sp.dma_start(x4[:, tiles], x[bass.ds(row, RUN)].rearrange("(t p) d -> p t d", p=P)).then_inc(x_loaded, 16)

                def store(e):
                    for m in range(2):
                        sp.wait_ge(o_ready, 2 * e + m + 1)
                        settle(sp)
                        sp.dma_start(out[bass.ds(m * (N // 2) + e * RUN, RUN)].rearrange("(t p) d -> p t d", p=P),
                                     o4[:, m]).then_inc(out_stored[m], 16)

                def save(n):
                    sp.wait_ge(x1_ready, 2 * n + 2)
                    settle(sp)
                    wait(sp, x1_moved, 16 * n)
                    settle(sp)
                    sp.dma_start(x1_mid[:, :, :], x1_next[:, :, :]).then_inc(x1_saved, 16)

                def body(e, here=True, ahead=True, past=True, beyond=True):
                    if beyond:
                        load_tokens(e + 2)
                    if past:
                        store(e - 1)
                    if here:
                        sp.wait_ge(x1_saved, 16 * e + 16)
                        settle(sp)
                        wait(sp, o_ready, 2 * e)
                        settle(sp)
                        sp.dma_start(x1_here[:, :, :], x1_mid[:, :, :]).then_inc(x1_moved, 16)
                    if ahead:
                        save(e + 1)
                    if beyond:
                        for i in range(4):
                            load_weights(e + 2, i)

                load_tokens(0)
                for i in range(4):
                    load_weights(0, i)
                sp.dma_start(b1_c[:, :], b1).then_inc(b_loaded, 16)
                sp.dma_start(b2_c[:, :], b2).then_inc(b_loaded, 16)
                bodies(sp, body)
                for m in range(2):
                    sp.wait_ge(out_stored[m], 16 * E)

            @block.gpsimd
            def _(pool):
                nc.gpsimd.memset(mhalf2[:, :], -0.5).then_inc(half2_ready, 1)
                pool.wait_ge(half2_ready, 1)

                def reciprocal_deviation(n, r):
                    pool.wait_ge(cmv_ready, 8 * n + 2 * r + 2)
                    settle(pool)
                    nc.gpsimd.tensor_scalar(cve[:, r], cmv[:, r, :, 1], EPS, 0.0, ALU.add, ALU.add).then_inc(cve_ready, 1)
                    pool.wait_ge(cve_ready, 4 * n + r + 1)
                    nc.gpsimd.tensor_tensor(out=crstd[:, r], in0=cve[:, r], in1=mhalf2[:, :], op=ALU.pow).then_inc(crstd_ready, 1)

                def low_weights(e, j):
                    pool.wait_ge(ehi_ready, 8 * e + j + 1)
                    nc.gpsimd.tensor_tensor(out=e_lo[:, j], in0=raw[:, j], in1=e_hi[:, j].bitcast(fp32), op=ALU.subtract).then_inc(elo_ready, 1)

                def low_masked(n):
                    pool.wait_ge(mthi_ready, n + 1)
                    nc.gpsimd.tensor_tensor(out=mT_lo[:, :, :], in0=mT[:, :, :], in1=mT_hi[:, :, :].bitcast(fp32),
                                            op=ALU.subtract).then_inc(mtlo_ready, 1)

                def attention_bias(n, q):
                    pool.wait_ge(xf_ready, 4 * n + 2 * q + 2)
                    wait(pool, xa_ready, 2 * n + q - 1)
                    for s in range(2):
                        nc.gpsimd.tensor_tensor(out=xfa[:, 2 * q + s], in0=xf[:, 2 * q + s], in1=attc_b[:, :], op=ALU.add).then_inc(xfa_ready, 1)

                def output(e, m):
                    pool.wait_ge(zg_ready, 2 * e + m + 1)
                    wait(pool, out_stored[m], 16 * e)
                    pool.wait_ge(x1_moved, 16 * e + 16)
                    nc.gpsimd.tensor_tensor(out=o4[:, m], in0=zg[:, m], in1=x1_here[:, 2 * m:2 * m + 2], op=ALU.add).then_inc(o_ready, 1)

                low_masked(0)

                def body(e, here=True, ahead=True, past=True, beyond=True):
                    n = e + 1
                    if ahead:
                        reciprocal_deviation(n, 0)
                        reciprocal_deviation(n, 1)
                        reciprocal_deviation(n, 2)
                        attention_bias(n, 0)
                        reciprocal_deviation(n, 3)
                        attention_bias(n, 1)
                        low_weights(n, 0)
                    if past:
                        output(e - 1, 0)
                    if ahead:
                        low_weights(n, 1)
                        low_weights(n, 2)
                    if past:
                        output(e - 1, 1)
                    if ahead:
                        low_weights(n, 3)
                    if beyond:
                        low_masked(n + 1)
                    if ahead:
                        for j in range(4, HB):
                            low_weights(n, j)
                bodies(pool, body)

            @block.vector
            def _(dve):
                def combine(n, tt):
                    bank = (vp_ps, ap_ps)[tt % 2]
                    dve.wait_ge(proj_done, 4 * n + tt + 1)
                    nc.vector.scalar_tensor_tensor(out=comb[:, tt % 2], in0=bank[:, D:2 * D], scalar=u4[:, tt, W_EXT:W_EXT + 1],
                                                   in1=u4[:, tt, D:2 * D],
                                                   op0=ALU.mult, op1=ALU.add).then_inc(comb_ready, 1)
                    dve.wait_ge(comb_ready, 4 * n + tt + 1)
                    nc.vector.tensor_tensor(res[:, tt], bank[:, 0:D], comb[:, tt % 2], ALU.add).then_inc(vp_taken, 1)

                def residual(n, q):
                    tiles = slice(2 * q, 2 * q + 2)
                    dve.wait_ge(vp_taken, 4 * n + 2 * q + 2)
                    nc.vector.tensor_tensor(resm[:, :, :], res[:, tiles], mx4[:, tiles], ALU.max).then_inc(resm_ready, 1)
                    dve.wait_ge(resm_ready, 2 * n + q + 1)
                    wait(dve, x1_saved, 16 * n)
                    nc.vector.tensor_tensor(x1_next[:, tiles], resm[:, :, :], x4[:, tiles], ALU.add).then_inc(x1_ready, 1)

                def moments(n, r, tiles):
                    for s in range(2):
                        nc.vector.bn_stats(cst6[:, r, s], tiles[s]).then_inc(cst_done, 1)
                    dve.wait_ge(cst_done, 8 * n + 2 * r + 2)
                    settle(dve)
                    for s in range(2):
                        nc.vector.bn_aggr(cmv[:, r, s], cst6[:, r, s]).then_inc(cmv_ready, 1)

                def first_moments(n, q):
                    dve.wait_ge(x1_ready, 2 * n + q + 1)
                    moments(n, 2 * q, [x1_next[:, 2 * q + s] for s in range(2)])

                def normalise(n, r, out, tiles, done):
                    dve.wait_ge(crstd_ready, 4 * n + r + 1)
                    for s in range(2):
                        nc.vector.tensor_scalar(out[:, 2 * (r // 2) + s], tiles[:, 2 * (r // 2) + s], cmv[:, r, s, 0:1], crstd[:, r, s:s + 1],
                                                ALU.subtract, ALU.mult).then_inc(done, 1)

                def first_norm(n, q):
                    normalise(n, 2 * q, xf, x1_next, xf_ready)
                    dve.wait_ge(xf_ready, 4 * n + 2 * q + 2)
                    moments(n, 2 * q + 1, [xf[:, 2 * q + s] for s in range(2)])

                def second_norm(n, q):
                    normalise(n, 2 * q + 1, xn, xf, xn_ready)

                def low(out, whole, high, done):
                    nc.vector.tensor_tensor(out, whole, high.bitcast(fp32), ALU.subtract).then_inc(done, 1)

                def attended(n, q):
                    dve.wait_ge(att_done, 2 * n + q + 1)
                    dve.wait_ge(xfa_ready, 4 * n + 2 * q + 2)
                    nc.vector.tensor_tensor(xa[:, 2 * q:2 * q + 2], ap_ps[:, :].rearrange("p (t d) -> p t d", t=2), xfa[:, 2 * q:2 * q + 2],
                                            ALU.add).then_inc(xa_ready, 1)

                def low_attended(n, q):
                    dve.wait_ge(nthi_ready, 2 * n + q + 1)
                    low(nT_lo[:, :, :, :], xt_ps[:, :].rearrange("p (t k c) -> p t k c", t=2, k=KD), nT_hi[:, :, :, :], ntlo_ready)

                def low_result(n, q):
                    dve.wait_ge(uthi_ready, 2 * n + q + 1)
                    low(uT_lo[:, :, :, :], xt_ps[:, :].rearrange("p (t k c) -> p t k c", t=2, k=KD), uT_hi[:, :, :, :], utlo_ready)

                def last_bias(e, m):
                    dve.wait_ge(z_done, 2 * e + m + 1)
                    wait(dve, zg_ready, 2 * e + m - 1)
                    for s in range(2):
                        nc.vector.tensor_tensor(zt[:, m, s], zp_ps[:, s * D:(s + 1) * D], nextb_b[:, :], ALU.add).then_inc(zt_ready, 1)

                def body(e, here=True, ahead=True, past=True, beyond=True):
                    n = e + 1
                    for j in range(HB):
                        if here:
                            dve.wait_ge(hhi_ready, 8 * e + j + 1)
                            low(h_lo[:, j % HR], hf[:, j % HR], h_hi[:, j % HR], hlo_ready)
                        if past and j in (1, 3):
                            last_bias(e - 1, j // 2)
                        if ahead:
                            if j == 0:
                                low_result(n, 0)
                            if j == 1:
                                combine(n, 0)
                                combine(n, 1)
                                low_result(n, 1)
                                residual(n, 0)
                                first_moments(n, 0)
                            if j == 2:
                                combine(n, 2)
                                combine(n, 3)
                                residual(n, 1)
                                first_norm(n, 0)
                                first_moments(n, 1)
                            if j == 3:
                                second_norm(n, 0)
                                first_norm(n, 1)
                            if j == 4:
                                second_norm(n, 1)
                            if j == 5:
                                low_attended(n, 0)
                            if j == 6:
                                attended(n, 0)
                                low_attended(n, 1)
                            if j == 7:
                                attended(n, 1)
                    if ahead:
                        for q, bank in enumerate((xt_ps, vp_ps)):
                            dve.wait_ge(xthi_ready, 2 * n + q + 1)
                            low(xT_lo[:, :, q * RUN:(q + 1) * RUN].rearrange("p k (t c) -> p k t c", t=2),
                                bank[:, :].rearrange("p (t k c) -> p k t c", t=2, k=KD),
                                xT_hi[:, :, q * RUN:(q + 1) * RUN].rearrange("p k (t c) -> p k t c", t=2), xtlo_ready)
                    if here:
                        dve.wait_ge(yhi_ready, e + 1)
                        low(y_lo[:, :, :], yf[:, :, :], y_hi[:, :, :], ylo_ready)
                bodies(dve, body)

            @block.scalar
            def _(act):
                def high(out, whole, done):
                    nc.scalar.activation(out, whole, ACT.Copy).then_inc(done, 1)

                def high_weights(e, j):
                    act.wait_ge(raw_in[j // 2], 16 * e + 16)
                    wait(act, fc2_done, 8 * e + j - 7)
                    high(e_hi[:, j], raw[:, j], ehi_ready)

                def high_result(n, q):
                    act.wait_ge(ut_done, 2 * n + q + 1)
                    wait(act, proj_done, 4 * n + 2 * q)
                    high(uT_hi[:, :, :, :], xt_ps[:, :].rearrange("p (t k c) -> p t k c", t=2, k=KD), uthi_ready)

                def high_attended(n, q):
                    act.wait_ge(nt_done, 2 * n + q + 1)
                    wait(act, att_done, 2 * n + q)
                    high(nT_hi[:, :, :, :], xt_ps[:, :].rearrange("p (t k c) -> p t k c", t=2, k=KD), nthi_ready)

                def last_gelu(e, m):
                    act.wait_ge(zt_ready, 4 * e + 2 * m + 2)
                    wait(act, o_ready, 2 * e + m - 1)
                    nc.scalar.activation(zg[:, m], zt[:, m], ACT.Gelu).then_inc(zg_ready, 1)

                def high_masked(n):
                    act.wait_ge(x_loaded, 128 * n + 128)
                    wait(act, proj_done, 4 * n)
                    high(mT_hi[:, :, :], mT[:, :, :], mthi_ready)

                high_masked(0)

                def body(e, here=True, ahead=True, past=True, beyond=True):
                    n = e + 1
                    for j in range(HB):
                        if here:
                            act.wait_ge(fc1_done, 8 * e + j + 1)
                            wait(act, fc2_done, 8 * e + j + 1 - HR)
                            nc.scalar.activation(hf[:, j % HR], h_ps[j % 2][:, :], ACT.Gelu,
                                                 bias=b1_c[:, bass.ds(8 * e + j, 1)]).then_inc(gelu_done, 1)
                            act.wait_ge(gelu_done, 8 * e + j + 1)
                            high(h_hi[:, j % HR], hf[:, j % HR], hhi_ready)
                        if ahead:
                            if j == 0:
                                high_result(n, 0)
                            if j == 1:
                                high_result(n, 1)
                            if j == 5:
                                high_attended(n, 0)
                            if j == 6:
                                high_attended(n, 1)
                            if j >= 3:
                                high_weights(n, j - 3)
                        if past and j in (2, 4):
                            last_gelu(e - 1, j // 2 - 1)
                        if beyond and j == 6:
                            high_masked(n + 1)
                    if ahead:
                        for q, bank in enumerate((xt_ps, vp_ps)):
                            act.wait_ge(xt_done, 2 * n + q + 1)
                            wait(act, fc1_done, 8 * n)
                            high(xT_hi[:, :, q * RUN:(q + 1) * RUN].rearrange("p k (t c) -> p k t c", t=2),
                                 bank[:, :].rearrange("p (t k c) -> p k t c", t=2, k=KD), xthi_ready)
                    if here:
                        act.wait_ge(fc2_done, 8 * e + 8)
                        for k in range(KD):
                            nc.scalar.activation(yf[:, k], y_ps[k][:, :], ACT.Identity, bias=b2_c[:, bass.ds(2 * e + k, 1)]).then_inc(y_ready, 1)
                        act.wait_ge(y_ready, 2 * e + 2)
                        wait(act, z_done, 2 * e)
                        high(y_hi[:, :, :], yf[:, :, :], yhi_ready)
                    if ahead:
                        high_weights(n, 5)
                        high_weights(n, 6)
                        high_weights(n, 7)
                act.wait_ge(b_loaded, 32)
                bodies(act, body)

            @block.tensor
            def _(pe):
                def parts(hi, lo, index, what):
                    return [(hi[(slice(None), index, k, what)], lo[(slice(None), index, k, what)]) for k in range(KD)]

                def turn(bank, tile, s):
                    for k in range(KD):
                        last = nc.tensor.transpose(bank[:, (KD * s + k) * P:(KD * s + k + 1) * P], tile[:, k * P:(k + 1) * P], ident[:, :])
                    return last

                def turn_results(n, q):
                    if q == 0:
                        pe.wait_ge(x_loaded, 128 * n + 128)
                        wait(pe, xtlo_ready, 2 * n - 1)
                    else:
                        pe.wait_ge(utlo_ready, 2 * n + 1)
                    for s in range(2):
                        last = turn(xt_ps, u4[:, 2 * q + s], s)
                    last.then_inc(ut_done, 1)

                def project(n, tt):
                    if tt % 2 == 0:
                        pe.wait_ge(utlo_ready, 2 * n + tt // 2 + 1)
                    if tt == 0:
                        pe.wait_ge(mtlo_ready, n + 1)
                        wait(pe, xtlo_ready, 2 * n)
                    elif tt == 1:
                        wait(pe, xa_ready, 2 * n)
                    else:
                        pe.wait_ge(vp_taken, 4 * n + tt - 1)
                    ts = slice(tt * P, (tt + 1) * P)
                    bank = (vp_ps, ap_ps)[tt % 2]
                    split_product(nc, bank[:, 0:D], parts(uT_hi, uT_lo, tt % 2, slice(None)), parts(w_hi, w_lo, WLV, slice(None)))
                    split_product(nc, bank[:, D:2 * D], [(mT_hi[:, k, ts], mT_lo[:, k, ts]) for k in range(KD)],
                                  parts(w_hi, w_lo, WEV, slice(None))).then_inc(proj_done, 1)

                def turn_normed(n, q):
                    pe.wait_ge(xn_ready, 4 * n + 2 * q + 2)
                    if q == 0:
                        pe.wait_ge(utlo_ready, 2 * n + 2)
                    else:
                        pe.wait_ge(ntlo_ready, 2 * n + 1)
                    for s in range(2):
                        last = turn(xt_ps, xn[:, 2 * q + s], s)
                    last.then_inc(nt_done, 1)

                def attend(n, q):
                    pe.wait_ge(ntlo_ready, 2 * n + q + 1)
                    if q == 0:
                        pe.wait_ge(vp_taken, 4 * n + 4)
                    else:
                        pe.wait_ge(xa_ready, 2 * n + 1)
                    for s in range(2):
                        last = split_product(nc, ap_ps[:, s * D:(s + 1) * D], parts(nT_hi, nT_lo, s, slice(None)),
                                             parts(w_hi, w_lo, WATT, slice(None)))
                    last.then_inc(att_done, 1)

                def turn_attended(n, q):
                    pe.wait_ge(xa_ready, 2 * n + q + 1)
                    if q == 0:
                        pe.wait_ge(ntlo_ready, 2 * n + 2)
                    else:
                        pe.wait_ge(vp_taken, 4 * n + 3)
                    for s in range(2):
                        last = turn((xt_ps, vp_ps)[q], xa[:, 2 * q + s], s)
                    last.then_inc(xt_done, 1)

                def first_layer(e, j):
                    pe.wait_ge(elo_ready, 8 * e + j + 1)
                    if j == 0:
                        pe.wait_ge(xtlo_ready, 2 * e + 2)
                    wait(pe, gelu_done, 8 * e + j - 1)
                    split_product(nc, h_ps[j % 2][:, :],
                                  [(e_hi[:, j, k * P:(k + 1) * P], e_lo[:, j, k * P:(k + 1) * P]) for k in range(KD)],
                                  [(xT_hi[:, k], xT_lo[:, k]) for k in range(KD)]).then_inc(fc1_done, 1)

                def second_layer(e, j):
                    pe.wait_ge(hlo_ready, 8 * e + j + 1)
                    if j == 0:
                        wait(pe, y_ready, 2 * e)
                    for k in range(KD):
                        ks = slice(D + k * P, D + (k + 1) * P)
                        last = split_product(nc, y_ps[k][:, :], [(e_hi[:, j, ks], e_lo[:, j, ks])],
                                             [(h_hi[:, j % HR], h_lo[:, j % HR])], start=j == 0, stop=j == HB - 1)
                    last.then_inc(fc2_done, 1)

                def last_layer(e, m):
                    if m == 0:
                        pe.wait_ge(ylo_ready, e + 1)
                    wait(pe, zt_ready, 4 * e + 2 * m)
                    for s in range(2):
                        ts = slice((2 * m + s) * P, (2 * m + s + 1) * P)
                        last = split_product(nc, zp_ps[:, s * D:(s + 1) * D],
                                             [(y_hi[:, k, ts], y_lo[:, k, ts]) for k in range(KD)],
                                             parts(w_hi, w_lo, WNEXT, slice(None)))
                    last.then_inc(z_done, 1)

                def body(e, here=True, ahead=True, past=True, beyond=True):
                    n = e + 1
                    for j in range(HB):
                        if here:
                            first_layer(e, j)
                            if j > 1:
                                second_layer(e, j - 2)
                        if past and j in (1, 3):
                            last_layer(e - 1, j // 2)
                        if ahead:
                            if j == 0:
                                turn_results(n, 0)
                            if j == 1:
                                project(n, 0)
                                project(n, 1)
                                turn_results(n, 1)
                            if j == 2:
                                project(n, 2)
                                project(n, 3)
                            if j == 5:
                                turn_normed(n, 0)
                            if j == 6:
                                attend(n, 0)
                                turn_normed(n, 1)
                            if j == 7:
                                attend(n, 1)
                                turn_attended(n, 0)
                    if here:
                        second_layer(e, HB - 2)
                    if ahead:
                        turn_attended(n, 1)
                    if here:
                        second_layer(e, HB - 1)
                bodies(pe, body)


def kernel(**inputs):
    import numpy as np
    import concourse.bacc as bacc
    from concourse.bass_utils import run_bass_kernel_spmd

    def g(name):
        return np.asarray(inputs[name])

    def rows_to_columns(a, blocks):
        return a.reshape(-1, blocks, P).transpose(2, 0, 1).reshape(P, -1)

    fc1 = g("L0_ffn_fc1_w").reshape(E, HB, P, KD, P).transpose(0, 4, 1, 3, 2).reshape(E, P, HB, D)
    fc2 = g("L0_ffn_fc2_w").reshape(E, D, HB, P).transpose(0, 3, 2, 1)
    arrays = {
        "x": g("x"), "mx": g("L0_gnn_masked_x"), "mxT": g("L0_gnn_masked_x").T, "adj": g("adj"),
        "wlqT": g("L0_gnn_Wlq").T, "wlkT": g("L0_gnn_Wlk").T, "wgk": g("L0_gnn_Wgk"), "wgqT": g("L0_gnn_Wgq").T,
        "wgv": g("L0_gnn_Wgv"), "bgv": g("L0_gnn_bgv"), "wes": g("L0_gnn_Wes").reshape(D), "wlv": g("L0_gnn_Wlv"),
        "blv": g("L0_gnn_blv"), "wev": g("L0_gnn_Wev"), "bev": g("L0_gnn_bev"),
        "ln_g": rows_to_columns(g("L0_ffn_ln_g")[None], KD), "ln_b": rows_to_columns(g("L0_ffn_ln_b")[None], KD),
        "attn_wT": g("L0_ffn_attn_w").T, "attn_b": g("L0_ffn_attn_b"), "next_wT": g("L0_ffn_next_w").T, "next_b": g("L0_ffn_next_b"),
        "b1": rows_to_columns(g("L0_ffn_fc1_b"), HB), "b2": rows_to_columns(g("L0_ffn_fc2_b"), KD),
        "wffn": np.concatenate([fc1, fc2], axis=3),
    }
    nc = bacc.Bacc("TRN2", target_bir_lowering=False, num_devices=1)
    fed, args = {}, []
    for name, a in arrays.items():
        fed[f"in_{name}"] = np.ascontiguousarray(a)
        args.append(nc.dram_tensor(f"in_{name}", a.shape, mybir.dt.from_np(a.dtype), kind="ExternalInput").ap())
    args.append(nc.dram_tensor("result", (N, D), fp32, kind="ExternalOutput").ap())
    gnn_moe_kernel(nc, *args)
    r = run_bass_kernel_spmd(nc, [fed], core_ids=[0])
    return r.results[0]["result"]
```

```python
import concourse.bass as bass
from concourse import mybir
from contextlib import ExitStack

fp32 = mybir.dt.float32
fp32r = mybir.dt.float32r
uint8 = mybir.dt.uint8
ALU = mybir.AluOpType
ACT = mybir.ActivationFunctionType
AX = mybir.AxisListType

N, D, E, HID = 4096, 256, 8, 1024
P = 128
KD = D // P
NT = N // P
CH = 512
NC = N // CH
TG = CH // P
NG = N // CH
HB = HID // P
ROWU = 2 * D + 4
W_LOC, W_GLOB, W_EXT = 2 * D, 2 * D + 1, 2 * D + 2
SCALE = 1.0 / 16.0
MASKED = -1.0e9 / SCALE
EPS = 1e-5
WLV, WEV, WATT, WNEXT = range(4)


def wait(engine, semaphore, value):
    if isinstance(value, int) and value <= 0:
        return
    engine.wait_ge(semaphore, value)


def split_product(nc, out, lhs, rhs, start=True, stop=True):
    pairs = [(lh, rh, k, len(lhs)) for k, (lh, rh) in enumerate(zip(lhs, rhs))]
    for (l_hi, l_lo), (r_hi, r_lo), k, n in pairs:
        nc.tensor.matmul(out, l_hi, r_hi, start=start and k == 0, stop=False)
        nc.tensor.matmul(out, l_hi, r_lo, start=False, stop=False)
        last = nc.tensor.matmul(out, l_lo, r_hi, start=False, stop=stop and k == n - 1)
    return last


def gnn_moe_kernel(nc, x, mx, mxT, adj, wlqT, wlkT, wgkT, wgqT, wgv, bgv, wes, wlv, blv, wev, bev,
                   ln_g, ln_b, attn_wT, attn_b, next_wT, next_b, b1, b2, wffn, out):
    u_dram = nc.dram_tensor("u_scratch", (NT, P, ROWU), fp32, kind="Internal").ap()
    q_dram = nc.dram_tensor("q_scratch", (NT, P, KD, P), fp32, kind="Internal").ap()

    ctx = ExitStack()
    with ctx:
        starts = {}

        def sb(stack, name, shape, dt=fp32):
            buffer = stack.enter_context(nc.sbuf_tensor(name, shape, dt))
            size = mybir.dt.size(dt)
            for n in shape[1:]:
                size *= n
            starts[name] = nc.sbuf_base - size
            return buffer

        def over(buffer, name, shape, dt=fp32):
            return nc.alloc_sbuf_tensor_at(name, shape, dt, offset=starts[buffer.name])

        def ps(stack, name, shape=(P, CH)):
            return stack.enter_context(nc.psum_tensor(name, list(shape), fp32))

        def sem(name):
            return ctx.enter_context(nc.semaphore(name))

        ident = sb(ctx, "ident", [P, P])
        w_hi = sb(ctx, "w_hi", [P, 4, KD, D], fp32r)
        w_lo = sb(ctx, "w_lo", [P, 4, KD, D], fp32r)
        blv_b = sb(ctx, "blv_b", [P, D])
        bev_b = sb(ctx, "bev_b", [P, D])
        gv_b = sb(ctx, "gv_b", [P, D])
        attc_b = sb(ctx, "attc_b", [P, D])
        nextb_b = sb(ctx, "nextb_b", [P, D])
        wes_b = sb(ctx, "wes_b", [P, D])
        wg_b = sb(ctx, "wg_b", [P, D])

        ab = ctx.enter_context(ExitStack())
        lnT_hi = sb(ab, "lnT_hi", [P, KD, N], fp32r)
        lnT_lo = sb(ab, "lnT_lo", [P, KD, N], fp32r)
        v_sp = sb(ab, "v_sp", [P, NT, 2 * D], fp32r)

        adj8 = sb(ab, "adj8", [P, N], uint8)
        q_in = sb(ab, "q_in", [P, KD, P])
        mxt = sb(ab, "mxt", [P, D])
        adj_in = [sem(f"adj_in{i}") for i in range(2)]
        q_loaded, mx_loaded = sem("q_loaded"), sem("mx_loaded")

        a = ab.enter_context(ExitStack())
        xg = sb(a, "xg", [P, 2, TG, D])
        lnf = sb(a, "lnf", [P, 2, TG, D])
        st6 = sb(a, "st6", [P, TG, 6])
        mv = sb(a, "mv", [P, 2, TG, 2])
        veps = sb(a, "veps", [P, TG])
        mhalf = sb(a, "mhalf", [P, TG])
        rstd = sb(a, "rstd", [P, 2, TG])
        mg_hi = sb(a, "mg_hi", [P, 2, KD, CH], fp32r)
        mg_lo = sb(a, "mg_lo", [P, 2, KD, CH], fp32r)
        mg_raw = over(mg_lo, "mg_raw", [P, 2, KD, CH])
        qw_hi = sb(a, "qw_hi", [P, KD, D], fp32r)
        qw_lo = sb(a, "qw_lo", [P, KD, D], fp32r)
        wq_in = sb(a, "wq_in", [P, 2, KD, D])
        wgv_in = sb(a, "wgv_in", [P, KD, D])
        w_raw = over(w_lo, "w_raw", [P, 4, KD, D])
        lng = sb(a, "lng", [P, KD])
        lnb = sb(a, "lnb", [P, KD])
        xsum = sb(a, "xsum", [P, KD, NG])
        xtotal = sb(a, "xtotal", [P, KD])
        xbar_c = sb(a, "xbar_c", [P, KD, P])
        lnb_c = sb(a, "lnb_c", [P, KD, P])
        ones = sb(a, "ones", [P, P])
        share = sb(a, "share", [P, P])
        q_out = sb(a, "q_out", [P, KD, CH])
        bias = over(xg, "bias", [P, 2, 2 * CH])
        q_hi = over(lnf, "q_hi", [P, KD, P], fp32r)
        q_lo = nc.alloc_sbuf_tensor_at("q_lo", [P, KD, P], fp32r, offset=starts["lnf"] + KD * P * 4)
        bias_ready, qhi_ready, qlo_ready = sem("bias_ready"), sem("qhi_ready"), sem("qlo_ready")

        pa = ExitStack()
        tr_ps = [ps(pa, f"tr_ps{k}") for k in range(KD)]
        q_ps = [ps(pa, f"q_ps{k}") for k in range(KD)]
        qw_ps = ps(pa, "qw_ps", (P, CH))
        gw_ps = ps(pa, "gw_ps", (P, CH))
        row_ps = ps(pa, "row_ps", (P, CH))
        attc_ps = ps(pa, "attc_ps", (P, CH))

        x_in = [sem(f"x_in{i}") for i in range(2)]
        mg_in = [sem(f"mg_in{i}") for i in range(2)]
        wq_loaded, wg_loaded, w_loaded, rows_loaded = (sem(n) for n in ("wq_loaded", "wg_loaded", "w_loaded", "rows_loaded"))
        ident_ready, consts_ready = sem("ident_ready"), sem("consts_ready")
        stats_done, mv_ready, veps_ready, rstd_ready, ln_ready = (
            sem(n) for n in ("stats_done", "mv_ready", "veps_ready", "rstd_ready", "ln_ready"))
        vhi_ready, vlo_ready, tr_done, thi_ready, tlo_ready = (
            sem(n) for n in ("vhi_ready", "vlo_ready", "tr_done", "thi_ready", "tlo_ready"))
        mhi_ready, mlo_ready, q_done, q_copied, q_stored = (
            sem(n) for n in ("mhi_ready", "mlo_ready", "q_done", "q_copied", "q_stored"))
        qw_done, qwhi_ready, qwlo_ready, gw_done, gw_ready = (
            sem(n) for n in ("qw_done", "qwhi_ready", "qwlo_ready", "gw_done", "gw_ready"))
        xtotal_ready, xbar_ready, lnb_ready, rows_done, attc_done, attg_ready, whi_ready = (
            sem(n) for n in ("xtotal_ready", "xbar_ready", "lnb_ready", "rows_done", "attc_done", "attg_ready", "whi_ready"))
        mlo_0_ready = sem("mlo_0_ready")
        wlo_ready, late_rows_loaded = sem("wlo_ready"), sem("late_rows_loaded")

        settled = {}

        def settle(engine):
            if engine.engine not in settled:
                settled[engine.engine] = sem(f"settled_{len(settled)}")
            engine.sem_inc(settled[engine.engine], 1)

        def is_tile(t, which):
            return isinstance(t, int) and t == which

        def kblocks(ap):
            return ap.rearrange("(k p) n -> p k n", p=P)

        def groups(eng, group):
            for g in range(2):
                group(g, g % 2)
            with eng.Fori(1, NG // 2 - 1) as h:
                for pp in range(2):
                    group(2 * h + pp, pp, h=h)
            for g in range(NG - 2, NG):
                group(g, g % 2)

        def is_group(g, *which):
            return isinstance(g, int) and g in which

        with nc.Block() as block:
            @block.sync
            def _(sp):
                def load_x(g, pp):
                    sp.dma_start(xg[:, pp], x[bass.ds(g * CH, CH)].rearrange("(t p) d -> p t d", p=P)).then_inc(x_in[pp], 16)

                def load_masked(g, pp):
                    sp.dma_start(mg_raw[:, pp], mxT[:, bass.ds(g * CH, CH)].rearrange("(k p) q -> p k q", p=P)).then_inc(mg_in[pp], 16)

                load_x(0, 0)
                for n, w in enumerate((wlqT, wlkT)):
                    sp.dma_start(wq_in[:, n], kblocks(w)).then_inc(wq_loaded, 16)
                load_masked(0, 0)
                load_x(1, 1)
                load_masked(1, 1)
                sp.dma_start(lng[:, :], ln_g).then_inc(rows_loaded, 16)
                sp.dma_start(lnb[:, :], ln_b).then_inc(rows_loaded, 16)
                for n, w in enumerate((wlv, wev, attn_wT, next_wT)):
                    sp.dma_start(w_raw[:, n], kblocks(w)).then_inc(w_loaded, 16)

                def group(g, pp, h=None):
                    if not is_group(g, NG - 2, NG - 1):
                        sp.wait_ge(ln_ready, g + 1)
                        settle(sp)
                        load_x(g + 2, pp)
                    if is_group(g, 0):
                        sp.wait_ge(qw_done, 1)
                        for n, w in enumerate((wgkT, wgqT)):
                            sp.dma_start(wq_in[:, n], kblocks(w)).then_inc(wg_loaded, 16)
                    if not is_group(g, NG - 2, NG - 1):
                        sp.wait_ge(q_done, 2 * g + 2)
                        settle(sp)
                        load_masked(g + 2, pp)
                    if is_group(g, NG - 2):
                        sp.dma_start(wgv_in[:, :, :], kblocks(wgv)).then_inc(wg_loaded, 16)
                        sp.wait_ge(q_stored, 32 * (NG - 2))
                        sp.dma_start(q_in[:, :, :], q_dram[0]).then_inc(q_loaded, 16)
                        sp.dma_start(adj8[:, 0:N // 2], adj[0:P, 0:N // 2]).then_inc(adj_in[0], 16)
                        for dst, row in ((gv_b, bgv), (attc_b, attn_b)):
                            sp.dma_start(dst[:, :], row.partition_broadcast(P)).then_inc(rows_loaded, 16)
                    sp.wait_ge(q_copied, 2 * g + 2)
                    settle(sp)
                    for k in range(KD):
                        sp.dma_start(q_dram[bass.ds(g * TG, TG), :, k, :].rearrange("t p q -> p t q"),
                                     q_out[:, k, :].rearrange("p (t q) -> p t q", q=P)).then_inc(q_stored, 16)
                    if is_group(g, NG - 2):
                        for dst, row in ((blv_b, blv), (bev_b, bev), (nextb_b, next_b), (wes_b, wes)):
                            sp.dma_start(dst[:, :], row.partition_broadcast(P)).then_inc(late_rows_loaded, 16)
                        sp.dma_start(adj8[:, N // 2:N], adj[0:P, N // 2:N]).then_inc(adj_in[1], 16)
                        sp.dma_start(mxt[:, :], mx[0:P]).then_inc(mx_loaded, 16)
                groups(sp, group)

            @block.gpsimd
            def _(pool):
                nc.gpsimd.memset(mhalf[:, :], -0.5).then_inc(consts_ready, 1)
                nc.gpsimd.memset(ones[:, :], 1.0).then_inc(consts_ready, 1)
                nc.gpsimd.memset(share[:, :], 1.0 / N).then_inc(consts_ready, 1)
                nc.gpsimd.memset(ident[:, :], 0.0).then_inc(ident_ready, 1)
                pool.wait_ge(ident_ready, 1)
                nc.gpsimd.affine_select(out=ident[:, :], in_=ident[:, :], compare_op=ALU.not_equal, fill=1.0, base=0,
                                        pattern=[[-1, P]], channel_multiplier=1).then_inc(ident_ready, 1)
                pool.wait_ge(consts_ready, 3)

                def reciprocal_deviation(g, pp):
                    pool.wait_ge(mv_ready, 4 * g + 4)
                    settle(pool)
                    nc.gpsimd.tensor_scalar(veps[:, :], mv[:, pp, :, 1], EPS, 0.0, ALU.add, ALU.add).then_inc(veps_ready, 1)
                    pool.wait_ge(veps_ready, g + 1)
                    nc.gpsimd.tensor_tensor(out=rstd[:, pp, :], in0=veps[:, :], in1=mhalf[:, :], op=ALU.pow).then_inc(rstd_ready, 1)

                def low_masked(g, pp):
                    pool.wait_ge(mhi_ready, g + 1)
                    nc.gpsimd.tensor_tensor(out=mg_lo[:, pp, 0], in0=mg_raw[:, pp, 0], in1=mg_hi[:, pp, 0].bitcast(fp32),
                                            op=ALU.subtract).then_inc(mlo_0_ready, 1)

                def group(g, pp, h=None):
                    if not is_group(g, NG - 1):
                        reciprocal_deviation(g + 1, 1 - pp)
                        low_masked(g + 1, 1 - pp)
                    pool.wait_ge(vhi_ready, g + 1)
                    nc.gpsimd.tensor_tensor(out=v_sp[:, bass.ds(g * TG, TG), D:2 * D], in0=lnf[:, pp],
                                            in1=v_sp[:, bass.ds(g * TG, TG), 0:D].bitcast(fp32), op=ALU.subtract).then_inc(vlo_ready, 1)
                reciprocal_deviation(0, 0)
                low_masked(0, 0)
                groups(pool, group)
                pool.wait_ge(ln_ready, NG)
                pool.wait_ge(adj_in[0], 16)
                for c in range(2):
                    nc.gpsimd.tensor_scalar(bias[:, c], adj8[:, c * 2 * CH:(c + 1) * 2 * CH], -MASKED, MASKED,
                                            ALU.mult, ALU.add).then_inc(bias_ready, 1)

            @block.vector
            def _(dve):
                def moments(g, pp, h):
                    dve.wait_ge(x_in[pp], 16 * h + 16)
                    for j in range(TG):
                        nc.vector.bn_stats(st6[:, j], xg[:, pp, j]).then_inc(stats_done, 1)
                    dve.wait_ge(stats_done, 4 * g + 4)
                    settle(dve)
                    for j in range(TG):
                        nc.vector.bn_aggr(mv[:, pp, j], st6[:, j]).then_inc(mv_ready, 1)

                def low_masked(g, pp):
                    dve.wait_ge(mhi_ready, g + 1)
                    nc.vector.tensor_tensor(mg_lo[:, pp, 1], mg_raw[:, pp, 1], mg_hi[:, pp, 1].bitcast(fp32),
                                            ALU.subtract).then_inc(mlo_ready, 1)

                def group(g, pp, h=None):
                    h = g // 2 if h is None else h
                    dve.wait_ge(rstd_ready, g + 1)
                    for j in range(TG):
                        last = nc.vector.tensor_scalar(lnf[:, pp, j], xg[:, pp, j], mv[:, pp, j, 0:1], rstd[:, pp, j:j + 1],
                                                       ALU.subtract, ALU.mult)
                    last.then_inc(ln_ready, 1)
                    if not is_group(g, NG - 1):
                        moments(g + 1, 1 - pp, h + pp)
                    if is_group(g, 0):
                        dve.wait_ge(qwhi_ready, 1)
                        nc.vector.tensor_tensor(qw_lo[:, :, :], qw_ps[:, :].rearrange("p (k n) -> p k n", k=KD),
                                                qw_hi[:, :, :].bitcast(fp32), ALU.subtract).then_inc(qwlo_ready, 1)
                        low_masked(0, 0)
                    for k in range(KD):
                        dve.wait_ge(thi_ready, 2 * g + k + 1)
                        nc.vector.tensor_tensor(lnT_lo[:, k, bass.ds(g * CH, CH)], tr_ps[k][:, :],
                                                lnT_hi[:, k, bass.ds(g * CH, CH)].bitcast(fp32), ALU.subtract).then_inc(tlo_ready, 1)
                    if not is_group(g, NG - 1):
                        low_masked(g + 1, 1 - pp)
                moments(0, 0, 0)
                groups(dve, group)

                dve.wait_ge(thi_ready, 2 * NG)
                nc.vector.tensor_reduce(xtotal[:, :], xsum[:, :, :], AX.X, ALU.add).then_inc(xtotal_ready, 1)
                dve.wait_ge(xtotal_ready, 1)
                dve.wait_ge(consts_ready, 3)
                for k in range(KD):
                    nc.vector.tensor_scalar(xbar_c[:, k], share[:, :], xtotal[:, k:k + 1], None, ALU.mult).then_inc(xbar_ready, 1)
                dve.wait_ge(qhi_ready, 1)
                nc.vector.tensor_tensor(q_lo[:, :, :], q_in[:, :, :], q_hi[:, :, :].bitcast(fp32), ALU.subtract).then_inc(qlo_ready, 1)
                dve.wait_ge(rows_loaded, 16 * 4)
                dve.wait_ge(attc_done, 1)
                nc.vector.tensor_tensor(attc_b[:, :], attc_ps[:, 0:D], attc_b[:, :], ALU.add)
                dve.wait_ge(rows_done, 1)
                nc.vector.tensor_tensor(gv_b[:, :], row_ps[:, 0:D], gv_b[:, :], ALU.add)
                nc.vector.tensor_copy(wg_b[:, :], row_ps[:, D:2 * D])

            @block.scalar
            def _(act):
                def high_masked(g, pp, h):
                    act.wait_ge(mg_in[pp], 16 * h + 16)
                    wait(act, q_done, 2 * g - 2)
                    nc.scalar.activation(mg_hi[:, pp], mg_raw[:, pp], ACT.Copy).then_inc(mhi_ready, 1)

                def group(g, pp, h=None):
                    h = g // 2 if h is None else h
                    act.wait_ge(ln_ready, g + 1)
                    nc.scalar.activation(v_sp[:, bass.ds(g * TG, TG), 0:D], lnf[:, pp], ACT.Copy).then_inc(vhi_ready, 1)
                    if is_group(g, 0):
                        high_masked(0, 0, 0)
                    for k in range(KD):
                        act.wait_ge(tr_done, 2 * g + k + 1)
                        nc.scalar.activation(lnT_hi[:, k, bass.ds(g * CH, CH)], tr_ps[k][:, :], ACT.Copy,
                                             accum_out=xsum[:, k, bass.ds(g, 1)]).then_inc(thi_ready, 1)
                    if not is_group(g, NG - 1):
                        high_masked(g + 1, 1 - pp, h + pp)
                    if is_group(g, 0):
                        act.wait_ge(rows_loaded, 16 * 2)
                        act.wait_ge(consts_ready, 3)
                        for k in range(KD):
                            nc.scalar.activation(lnb_c[:, k], ones[:, :], ACT.Copy, scale=lnb[:, k:k + 1]).then_inc(lnb_ready, 1)
                    if is_group(g, NG - 1):
                        act.wait_ge(tr_done, 2 * NG)
                        act.wait_ge(vlo_ready, NG)
                        act.wait_ge(q_loaded, 16)
                        nc.scalar.activation(q_hi[:, :, :], q_in[:, :, :], ACT.Copy).then_inc(qhi_ready, 1)
                    wait(act, q_stored, 32 * g)
                    for k in range(KD):
                        act.wait_ge(q_done, 2 * g + k + 1)
                        nc.scalar.activation(q_out[:, k, :], q_ps[k][:, :], ACT.Copy).then_inc(q_copied, 1)
                    if is_group(g, 1):
                        act.wait_ge(w_loaded, 64)
                        act.wait_ge(attc_done, 1)
                        for k in range(KD):
                            nc.scalar.activation(w_raw[:, WATT, k], w_raw[:, WATT, k], ACT.Copy,
                                                 scale=lng[:, k:k + 1]).then_inc(attg_ready, 1)
                    if is_group(g, NG - 2):
                        act.wait_ge(gw_done, 1)
                        nc.scalar.activation(wq_in[:, 0], gw_ps[:, :].rearrange("p (k n) -> p k n", k=KD), ACT.Copy).then_inc(gw_ready, 1)
                act.wait_ge(qw_done, 1)
                nc.scalar.activation(qw_hi[:, :, :], qw_ps[:, :].rearrange("p (k n) -> p k n", k=KD), ACT.Copy).then_inc(qwhi_ready, 1)
                groups(act, group)

            @block.tensor
            def _(pe):
                def fold(out, done):
                    for m in range(KD):
                        for k in range(KD):
                            last = nc.tensor.matmul(out[:, m * D:(m + 1) * D], wq_in[:, 0, k, m * P:(m + 1) * P], wq_in[:, 1, k, :],
                                                    start=k == 0, stop=k == KD - 1)
                    last.then_inc(done, 1)

                def group(g, pp, h=None):
                    def queries(m):
                        pe.wait_ge(mlo_ready, g + 1)
                        pe.wait_ge(mlo_0_ready, g + 1)
                        if m == 0:
                            wait(pe, q_copied, 2 * g)
                        ms = slice(m * P, (m + 1) * P)
                        split_product(nc, q_ps[m][:, :],
                                      [(qw_hi[:, k, ms], qw_lo[:, k, ms]) for k in range(KD)],
                                      [(mg_hi[:, pp, k], mg_lo[:, pp, k]) for k in range(KD)]).then_inc(q_done, 1)

                    if is_group(g, NG - 1):
                        queries(0)
                    pe.wait_ge(ln_ready, g + 1)
                    wait(pe, tlo_ready, 2 * g)
                    for k in range(KD):
                        for j in range(TG):
                            last = nc.tensor.transpose(tr_ps[k][:, j * P:(j + 1) * P], lnf[:, pp, j, k * P:(k + 1) * P], ident[:, :])
                        last.then_inc(tr_done, 1)
                    if is_group(g, 0):
                        pe.wait_ge(qwlo_ready, 1)
                    if not is_group(g, NG - 1):
                        queries(0)
                    queries(1)
                    if is_group(g, 1):
                        pe.wait_ge(lnb_ready, 2)
                        pe.wait_ge(w_loaded, 64)
                        for k in range(KD):
                            last = nc.tensor.matmul(attc_ps[:, 0:D], lnb_c[:, k], w_raw[:, WATT, k], start=k == 0, stop=k == KD - 1)
                        last.then_inc(attc_done, 1)
                    if is_group(g, NG - 2):
                        pe.wait_ge(wg_loaded, 32)
                        fold(gw_ps, gw_done)
                pe.wait_ge(wq_loaded, 32)
                fold(qw_ps, qw_done)
                pe.wait_ge(ident_ready, 2)
                groups(pe, group)

                pe.wait_ge(wg_loaded, 48)
                pe.wait_ge(gw_ready, 1)
                pe.wait_ge(xbar_ready, 2)
                for n, w in enumerate((wgv_in, wq_in[:, 0])):
                    for k in range(KD):
                        last = nc.tensor.matmul(row_ps[:, n * D:(n + 1) * D], xbar_c[:, k], w[:, k, :],
                                                start=k == 0, stop=k == KD - 1)
                last.then_inc(rows_done, 1)
        pa.close()
        a.close()

        b = ab.enter_context(ExitStack())
        sb(b, "held", [P, 2 * 2 * CH + 2 * KD * P])
        scores = sb(b, "scores", [P, N])
        dotted = sb(b, "dotted", [P, 2, D])
        p_hi = sb(b, "p_hi", [P, 2, CH], fp32r)
        p_lo = sb(b, "p_lo", [P, 2, CH], fp32r)
        tops = sb(b, "tops", [P, NC + 2])
        neg_top = sb(b, "neg_top", [P, 1])
        sums = sb(b, "sums", [P, 6])
        den = sb(b, "den", [P, 1])
        local_sum = sb(b, "local_sum", [P, 1])
        rden = sb(b, "rden", [P, 1])
        table_in = sb(b, "table_in", [P, 1])
        u_part = sb(b, "u_part", [P, D])
        u_out = sb(b, "u_out", [P, ROWU])
        kt_b = sb(b, "kt_b", [P, 3, D])

        attention_end = nc.sbuf_base
        assert starts["xg"] == starts["held"] and starts["lnf"] == starts["xg"] + 2 * 2 * CH * 4
        assert attention_end <= starts["q_out"]

        xt_ps = ps(ctx, "xt_ps")
        vp_ps = ps(ctx, "vp_ps")
        ap_ps = ps(ctx, "ap_ps")

        pb = ExitStack()
        s_ps = [ps(pb, f"s_ps{i}") for i in range(2)]
        pt_ps = [ps(pb, f"pt_ps{i}") for i in range(2)]
        u_ps = ps(pb, "u_ps")

        u_stored = sem("u_stored")
        score_done, score_masked, extra_dotted, top_ready = (
            sem(n) for n in ("score_done", "score_masked", "extra_dotted", "top_ready"))
        exp_done, extra_exp, den_ready, rden_ready, coef_ready = (
            sem(n) for n in ("exp_done", "extra_exp", "den_ready", "rden_ready", "coef_ready"))
        pt_done, phi_ready, plo_ready, pv_done, upart_ready, u_ready = (
            sem(n) for n in ("pt_done", "phi_ready", "plo_ready", "pv_done", "upart_ready", "u_ready"))
        kpart_ready, ksum_ready, kt_ready = sem("kpart_ready"), sem("ksum_ready"), sem("kt_ready")

        def steps(eng, step):
            step(-1, here=False)
            step(0)
            with eng.Fori(1, NT - 2) as t:
                step(t)
            step(NT - 2, after=False)
            step(NT - 1, ahead=False, after=False)

        pb.close()

        HR = 4

        def region(start, end):
            position = [start]

            def place(name, shape, dt=fp32):
                size = mybir.dt.size(dt)
                for n in shape[1:]:
                    size *= n
                buffer = nc.alloc_sbuf_tensor_at(name, shape, dt, offset=position[0])
                position[0] += size + -size % 32
                assert position[0] <= end, name
                return buffer
            return place

        HALF = N // 2 * 4
        halves = [starts[name] + k * 2 * HALF for name in ("lnT_hi", "lnT_lo") for k in range(KD)]
        first = [region(at, at + HALF) for at in halves]
        second = [region(at + HALF, at + 2 * HALF) for at in halves]
        mT = first[0]("mT", [P, KD, CH])
        mx4 = first[0]("mx4", [P, TG, D])
        x4 = first[1]("x4", [P, TG, D])
        mT_lo = first[1]("mT_lo", [P, KD, CH], fp32r)
        mT_hi = first[2]("mT_hi", [P, KD, CH], fp32r)
        uT_hi = first[2]("uT_hi", [P, 2, KD, P], fp32r)
        uT_lo = first[2]("uT_lo", [P, 2, KD, P], fp32r)
        comb = first[3]("comb", [P, 2, D])
        res = first[3]("res", [P, TG, D])
        resm = first[3]("resm", [P, 2, D])
        x1_next = second[0]("x1_next", [P, TG, D])
        xT_lo = second[0]("xT_lo", [P, KD, CH], fp32r)
        xf = second[1]("xf", [P, TG, D])
        xn = second[1]("xn", [P, TG, D])
        xfa = second[2]("xfa", [P, TG, D])
        nT_hi = second[2]("nT_hi", [P, 2, KD, P], fp32r)
        nT_lo = second[2]("nT_lo", [P, 2, KD, P], fp32r)
        xa = second[3]("xa", [P, TG, D])
        cst6 = second[3]("cst6", [P, 4, 2, 6])
        cmv = second[3]("cmv", [P, 4, 2, 2])
        cve = second[3]("cve", [P, 4, 2])
        crstd = second[3]("crstd", [P, 4, 2])
        mhalf2 = second[3]("mhalf2", [P, 2])
        b1_c = second[3]("b1_c", [P, E * HB])
        b2_c = second[3]("b2_c", [P, E * KD])

        tokens = region(starts["v_sp"], starts["v_sp"] + N * 2 * D * 4 // P)
        raw = tokens("raw", [P, HB, 2 * D])
        e_hi = tokens("e_hi", [P, HB, 2 * D], fp32r)
        e_lo = tokens("e_lo", [P, HB, 2 * D], fp32r)
        yf = tokens("yf", [P, KD, CH])
        y_hi = tokens("y_hi", [P, KD, CH], fp32r)
        y_lo = tokens("y_lo", [P, KD, CH], fp32r)
        x1_here = tokens("x1_here", [P, TG, D])

        rest = region(starts["adj8"], attention_end)
        xT_hi = rest("xT_hi", [P, KD, CH], fp32r)
        x1_mid = rest("x1_mid", [P, TG, D])
        hf = rest("hf", [P, HR, CH])
        h_hi = rest("h_hi", [P, HR, CH], fp32r)
        h_lo = rest("h_lo", [P, HR, CH], fp32r)
        zt = rest("zt", [P, 2, 2, D])
        zg = rest("zg", [P, 2, 2, D])
        o4 = rest("o4", [P, 2, 2, D])

        free = region(attention_end, nc.sbuf_usable_end)
        u4 = free("u4", [P, TG, ROWU])

        h_ps = [ps(ctx, f"h_ps{i}") for i in range(2)]
        y_ps = [ps(ctx, f"y_ps{i}") for i in range(KD)]
        zp_ps = ps(ctx, "zp_ps")

        u_loaded, mt_loaded, x_loaded, b_loaded = (sem(n) for n in ("u_loaded", "mt_loaded", "x_loaded", "b_loaded"))
        raw_in = [sem(f"raw_in{i}") for i in range(4)]
        out_stored = [sem(f"out_stored{i}") for i in range(2)]
        (ehi_ready, elo_ready, mthi_ready, mtlo_ready, ut_done, uthi_ready, utlo_ready,
         proj_done, comb_ready, vp_taken, resm_ready, x1_ready) = (sem(n) for n in (
             "ehi_ready", "elo_ready", "mthi_ready", "mtlo_ready", "ut_done", "uthi_ready",
             "utlo_ready", "proj_done", "comb_ready", "vp_taken", "resm_ready", "x1_ready"))
        (half2_ready, cst_done, cmv_ready, cve_ready, crstd_ready, xf_ready, xn_ready, xfa_ready, nt_done, nthi_ready, ntlo_ready,
         att_done, xa_ready, xt_done, xthi_ready, xtlo_ready) = (sem(n) for n in (
             "half2_ready", "cst_done", "cmv_ready", "cve_ready", "crstd_ready", "xf_ready", "xn_ready", "xfa_ready", "nt_done",
             "nthi_ready", "ntlo_ready", "att_done", "xa_ready", "xt_done", "xthi_ready", "xtlo_ready"))
        (fc1_done, gelu_done, hhi_ready, hlo_ready, fc2_done, y_ready, yhi_ready, ylo_ready, z_done, zt_ready, zg_ready, o_ready,
         x1_saved, x1_moved) = (sem(n) for n in (
             "fc1_done", "gelu_done", "hhi_ready", "hlo_ready", "fc2_done", "y_ready", "yhi_ready", "ylo_ready", "z_done",
             "zt_ready", "zg_ready", "o_ready", "x1_saved", "x1_moved"))

        def bodies(eng, body):
            body(0, past=False)
            body(1)
            with eng.Fori(2, E - 2) as e:
                body(e)
            body(E - 2, beyond=False)
            body(E - 1, ahead=False, beyond=False)
            body(E, here=False, ahead=False, beyond=False)

        WLEFT = 3
        y_half_done = sem("y_half_done")
        RUN = 2 * P


        def last_layer_bank(e, m):
            return h_ps[0] if is_tile(e, E - 1) and m == 1 else zp_ps

        with nc.Block() as block:
            @block.sync
            def _(sp):
                def load_tile(n):
                    wait(sp, qlo_ready, n)
                    settle(sp)
                    sp.dma_start(q_in[:, :, :], q_dram[n]).then_inc(q_loaded, 16)
                    for h in range(2):
                        wait(sp, bias_ready, 4 * n + 2 * h - 2)
                        settle(sp)
                        sp.dma_start(adj8[:, h * (N // 2):(h + 1) * (N // 2)],
                                     adj[bass.ds(n * P, P), h * (N // 2):(h + 1) * (N // 2)]).then_inc(adj_in[h], 16)
                    wait(sp, extra_dotted, 2 * n)
                    settle(sp)
                    sp.dma_start(mxt[:, :], mx[bass.ds(n * P, P)]).then_inc(mx_loaded, 16)

                def step(t, here=True, ahead=True, after=True):
                    if after:
                        load_tile(t + 2)
                    if is_tile(t, NT - 2):
                        first_tokens()
                    if is_tile(t, NT - 1):
                        sp.wait_ge(pv_done, 8 * t + 2)
                        for i in range(4):
                            load_weights(0, i)
                        sp.dma_start(b1_c[:, :], b1).then_inc(b_loaded, 16)
                        sp.dma_start(b2_c[:, :], b2).then_inc(b_loaded, 16)
                        load_tokens(1)
                    if here:
                        sp.wait_ge(kt_ready, t + 1)
                        settle(sp)
                        sp.wait_ge(u_ready, t + 1)
                        settle(sp)
                        sp.dma_start(u_dram[t], u_out[:, :]).then_inc(u_stored, 16)

                def load_weights(e, i):
                    wait(sp, elo_ready, 8 * e - 6 + 2 * i)
                    settle(sp)
                    sp.dma_start(raw[:, 2 * i:2 * i + 2], wffn[e, :, 2 * i:2 * i + 2]).then_inc(raw_in[i], 16)

                def load_results(n):
                    for m in range(2):
                        sp.dma_start(u4[:, 2 * m:2 * m + 2],
                                     u_dram[bass.ds(m * (NT // 2) + 2 * n, 2)].rearrange("t p c -> p t c")).then_inc(u_loaded, 16)

                def load_inputs(n):
                    for m in range(2):
                        row = m * (N // 2) + n * RUN
                        sp.dma_start(mT[:, :, m * RUN:(m + 1) * RUN], mxT[:, bass.ds(row, RUN)].rearrange("(k p) q -> p k q", p=P)).then_inc(mt_loaded, 16)
                    for m in range(2):
                        row = m * (N // 2) + n * RUN
                        tiles = slice(2 * m, 2 * m + 2)
                        sp.dma_start(mx4[:, tiles], mx[bass.ds(row, RUN)].rearrange("(t p) d -> p t d", p=P)).then_inc(x_loaded, 16)
                        sp.dma_start(x4[:, tiles], x[bass.ds(row, RUN)].rearrange("(t p) d -> p t d", p=P)).then_inc(x_loaded, 16)

                def load_tokens(n):
                    wait(sp, x1_ready, 2 * n)
                    settle(sp)
                    load_results(n)
                    load_inputs(n)

                def first_tokens():
                    sp.wait_ge(u_stored, 16 * (NT - 2))
                    load_results(0)
                    sp.wait_ge(score_done, 8 * NT - 4)
                    load_inputs(0)

                def store(e):
                    for m in range(2):
                        sp.wait_ge(o_ready, 2 * e + m + 1)
                        settle(sp)
                        sp.dma_start(out[bass.ds(m * (N // 2) + e * RUN, RUN)].rearrange("(t p) d -> p t d", p=P),
                                     o4[:, m]).then_inc(out_stored[m], 16)

                def save(n):
                    sp.wait_ge(x1_ready, 2 * n + 2)
                    settle(sp)
                    wait(sp, x1_moved, 16 * n)
                    settle(sp)
                    sp.dma_start(x1_mid[:, :, :], x1_next[:, :, :]).then_inc(x1_saved, 16)

                def body(e, here=True, ahead=True, past=True, beyond=True):
                    if beyond:
                        load_tokens(e + 2)
                    if past:
                        store(e - 1)
                    if here:
                        sp.wait_ge(x1_saved, 16 * e + 16)
                        settle(sp)
                        wait(sp, o_ready, 2 * e)
                        settle(sp)
                        sp.dma_start(x1_here[:, :, :], x1_mid[:, :, :]).then_inc(x1_moved, 16)
                    if ahead:
                        save(e + 1)
                    if beyond:
                        for i in range(4):
                            load_weights(e + 2, i)

                sp.wait_ge(q_stored, 32 * NG)
                steps(sp, step)
                sp.wait_ge(u_stored, 16 * NT)
                save(0)
                for i in range(4):
                    load_weights(1, i)
                bodies(sp, body)
                for m in range(2):
                    sp.wait_ge(out_stored[m], 16 * E)

            @block.gpsimd
            def _(pool):
                def rank_one(t):
                    if is_tile(t, 0):
                        pool.wait_ge(late_rows_loaded, 64)
                    pool.wait_ge(coef_ready, 2 * t + 2)
                    wait(pool, kt_ready, t)
                    settle(pool)
                    for r, row in enumerate((blv_b, gv_b, bev_b)):
                        nc.gpsimd.tensor_scalar(kt_b[:, r], row[:, :], u_out[:, W_LOC + r:W_LOC + r + 1], 0.0,
                                                ALU.mult, ALU.add).then_inc(kpart_ready, 1)
                    pool.wait_ge(kpart_ready, 3 * t + 3)
                    nc.gpsimd.tensor_tensor(out=u_out[:, D:2 * D], in0=kt_b[:, 0], in1=kt_b[:, 1], op=ALU.add).then_inc(ksum_ready, 1)
                    pool.wait_ge(ksum_ready, t + 1)
                    nc.gpsimd.tensor_tensor(out=u_out[:, D:2 * D], in0=u_out[:, D:2 * D], in1=kt_b[:, 2], op=ALU.add).then_inc(kt_ready, 1)

                def step(t, here=True, ahead=True, after=True):
                    n = t + 1
                    for c in range(4):
                        if ahead and not (is_tile(t, -1) and c < 2):
                            if c % 2 == 0:
                                pool.wait_ge(adj_in[c // 2], 16 * n + 16)
                            wait(pool, score_masked, 8 * n + 2 * c - 2)
                            settle(pool)
                            nc.gpsimd.tensor_scalar(bias[:, c % 2], adj8[:, c * 2 * CH:(c + 1) * 2 * CH], -MASKED, MASKED,
                                                    ALU.mult, ALU.add).then_inc(bias_ready, 1)
                        if here and c == 2:
                            if is_tile(t, NT - 1):
                                low_masked(0)
                                pool.wait_ge(score_done, 8 * NT)
                                nc.gpsimd.memset(mhalf2[:, :], -0.5).then_inc(half2_ready, 1)
                                pool.wait_ge(half2_ready, 1)
                                for r in range(3):
                                    reciprocal_deviation(0, r)
                                attention_bias(0, 0)
                                reciprocal_deviation(0, 3)
                                attention_bias(0, 1)
                            rank_one(t)

                def reciprocal_deviation(n, r):
                    pool.wait_ge(cmv_ready, 8 * n + 2 * r + 2)
                    settle(pool)
                    nc.gpsimd.tensor_scalar(cve[:, r], cmv[:, r, :, 1], EPS, 0.0, ALU.add, ALU.add).then_inc(cve_ready, 1)
                    pool.wait_ge(cve_ready, 4 * n + r + 1)
                    nc.gpsimd.tensor_tensor(out=crstd[:, r], in0=cve[:, r], in1=mhalf2[:, :], op=ALU.pow).then_inc(crstd_ready, 1)

                def low_weights(e, j):
                    pool.wait_ge(ehi_ready, 8 * e + j + 1)
                    nc.gpsimd.tensor_tensor(out=e_lo[:, j], in0=raw[:, j], in1=e_hi[:, j].bitcast(fp32), op=ALU.subtract).then_inc(elo_ready, 1)

                def low_masked(n):
                    pool.wait_ge(mthi_ready, n + 1)
                    nc.gpsimd.tensor_tensor(out=mT_lo[:, :, :], in0=mT[:, :, :], in1=mT_hi[:, :, :].bitcast(fp32),
                                            op=ALU.subtract).then_inc(mtlo_ready, 1)

                def attention_bias(n, q):
                    pool.wait_ge(xf_ready, 4 * n + 2 * q + 2)
                    wait(pool, xa_ready, 2 * n + q - 1)
                    for s in range(2):
                        nc.gpsimd.tensor_tensor(out=xfa[:, 2 * q + s], in0=xf[:, 2 * q + s], in1=attc_b[:, :], op=ALU.add).then_inc(xfa_ready, 1)

                def output(e, m):
                    pool.wait_ge(zg_ready, 2 * e + m + 1)
                    wait(pool, out_stored[m], 16 * e)
                    pool.wait_ge(x1_moved, 16 * e + 16)
                    nc.gpsimd.tensor_tensor(out=o4[:, m], in0=zg[:, m], in1=x1_here[:, 2 * m:2 * m + 2], op=ALU.add).then_inc(o_ready, 1)

                def body(e, here=True, ahead=True, past=True, beyond=True):
                    n = e + 1
                    if here:
                        for j in range(HB - WLEFT, HB):
                            low_weights(e, j)
                    if ahead:
                        for r in range(3):
                            reciprocal_deviation(n, r)
                        attention_bias(n, 0)
                        reciprocal_deviation(n, 3)
                        attention_bias(n, 1)
                        low_weights(n, 0)
                    if past and not is_tile(e, E):
                        output(e - 1, 0)
                    if ahead:
                        low_weights(n, 1)
                        low_weights(n, 2)
                    if past and not is_tile(e, E):
                        output(e - 1, 1)
                    if ahead:
                        low_weights(n, 3)
                    if beyond:
                        low_masked(n + 1)
                    if ahead:
                        low_weights(n, 4)
                steps(pool, step)
                pool.wait_ge(pv_done, 8 * NT - 2)
                for j in range(HB - WLEFT):
                    low_weights(0, j)
                    if j == 1:
                        low_masked(1)
                bodies(pool, body)

            @block.vector
            def _(dve):
                def q_low(n):
                    dve.wait_ge(qhi_ready, n + 1)
                    nc.vector.tensor_tensor(q_lo[:, :, :], q_in[:, :, :], q_hi[:, :, :].bitcast(fp32), ALU.subtract).then_inc(qlo_ready, 1)

                def step(t, here=True, ahead=True, after=True):
                    n = t + 1
                    beside(t, -1)
                    for c in range(NC):
                        if here:
                            dve.wait_ge(phi_ready, 8 * t + c + 1)
                            wait(dve, pv_done, 8 * t + c - 1)
                            nc.vector.tensor_tensor(p_lo[:, c % 2], pt_ps[c % 2][:, :], p_hi[:, c % 2].bitcast(fp32),
                                                    ALU.subtract).then_inc(plo_ready, 1)
                        if ahead:
                            dve.wait_ge(score_done, 8 * n + c + 1)
                            dve.wait_ge(bias_ready, 4 * n + c // 2 + 1)
                            settle(dve)
                            nc.vector.tensor_tensor_reduce(out=scores[:, c * CH:(c + 1) * CH], in0=s_ps[c % 2][:, :],
                                                           in1=bias[:, c // 2 % 2, c % 2 * CH:(c % 2 + 1) * CH],
                                                           scale=SCALE, scalar=-3.0e38, op0=ALU.add, op1=ALU.max,
                                                           accum_out=tops[:, c:c + 1]).then_inc(score_masked, 1)
                        if here and c == 3:
                            dve.wait_ge(exp_done, 4 * t + 4)
                            dve.wait_ge(extra_exp, t + 1)
                            nc.vector.tensor_reduce(den[:, :], sums[:, 0:6], AX.X, ALU.add).then_inc(den_ready, 1)
                            nc.vector.tensor_reduce(local_sum[:, :], sums[:, 0:4], AX.X, ALU.add).then_inc(den_ready, 1)
                            dve.wait_ge(den_ready, 2 * t + 2)
                            nc.vector.reciprocal(rden[:, :], den[:, :]).then_inc(rden_ready, 1)
                            dve.wait_ge(rden_ready, t + 1)
                            wait(dve, u_stored, 16 * t)
                            nc.vector.tensor_scalar(u_out[:, W_LOC:W_LOC + 1], local_sum[:, :], rden[:, :], None, ALU.mult).then_inc(coef_ready, 1)
                            nc.vector.tensor_scalar(u_out[:, W_GLOB:W_EXT + 1], sums[:, 4:6], rden[:, :], None, ALU.mult).then_inc(coef_ready, 1)
                            if isinstance(t, int) and t == 0:
                                nc.vector.memset(u_out[:, W_EXT + 1:ROWU], 0.0)
                        if is_tile(t, -1) and c < 4:
                            dve.wait_ge(whi_ready, c + 1)
                            nc.vector.tensor_tensor(w_lo[:, c], w_raw[:, c], w_hi[:, c].bitcast(fp32), ALU.subtract).then_inc(wlo_ready, 1)
                        if ahead and c == 5:
                            if is_tile(t, -1):
                                dve.wait_ge(late_rows_loaded, 64)
                            dve.wait_ge(mx_loaded, 16 * n + 16)
                            wait(dve, extra_exp, n)
                            nc.vector.tensor_tensor_reduce(out=dotted[:, 0], in0=mxt[:, :], in1=wg_b[:, :], scale=SCALE, scalar=0.0,
                                                           op0=ALU.mult, op1=ALU.add, accum_out=tops[:, NC:NC + 1]).then_inc(extra_dotted, 1)
                            nc.vector.tensor_tensor_reduce(out=dotted[:, 1], in0=mxt[:, :], in1=wes_b[:, :], scale=1.0, scalar=0.0,
                                                           op0=ALU.mult, op1=ALU.add, accum_out=tops[:, NC + 1:NC + 2]).then_inc(extra_dotted, 1)
                        beside(t, c)
                    if ahead:
                        dve.wait_ge(score_masked, 8 * n + 8)
                        dve.wait_ge(extra_dotted, 2 * n + 2)
                        nc.vector.tensor_reduce(neg_top[:, :], tops[:, :], AX.X, ALU.max, negate=True).then_inc(top_ready, 1)
                    if after:
                        q_low(t + 2)
                    if here:
                        dve.wait_ge(upart_ready, t + 1)
                        nc.vector.scalar_tensor_tensor(out=u_out[:, 0:D], in0=u_ps[:, 0:D], scalar=rden[:, :], in1=u_part[:, :],
                                                       op0=ALU.mult, op1=ALU.add).then_inc(u_ready, 1)

                def combine(n, tt):
                    bank = (vp_ps, ap_ps)[tt % 2]
                    dve.wait_ge(proj_done, 4 * n + tt + 1)
                    nc.vector.scalar_tensor_tensor(out=comb[:, tt % 2], in0=bank[:, D:2 * D], scalar=u4[:, tt, W_EXT:W_EXT + 1],
                                                   in1=u4[:, tt, D:2 * D],
                                                   op0=ALU.mult, op1=ALU.add).then_inc(comb_ready, 1)
                    dve.wait_ge(comb_ready, 4 * n + tt + 1)
                    nc.vector.tensor_tensor(res[:, tt], bank[:, 0:D], comb[:, tt % 2], ALU.add).then_inc(vp_taken, 1)

                def residual(n, q):
                    tiles = slice(2 * q, 2 * q + 2)
                    dve.wait_ge(vp_taken, 4 * n + 2 * q + 2)
                    dve.wait_ge(x_loaded, 64 * n + 64)
                    nc.vector.tensor_tensor(resm[:, :, :], res[:, tiles], mx4[:, tiles], ALU.max).then_inc(resm_ready, 1)
                    dve.wait_ge(resm_ready, 2 * n + q + 1)
                    if is_tile(n, 0):
                        dve.wait_ge(score_done, 8 * NT)
                    wait(dve, x1_saved, 16 * n)
                    nc.vector.tensor_tensor(x1_next[:, tiles], resm[:, :, :], x4[:, tiles], ALU.add).then_inc(x1_ready, 1)

                def moments(n, r, tiles):
                    for s in range(2):
                        nc.vector.bn_stats(cst6[:, r, s], tiles[s]).then_inc(cst_done, 1)
                    dve.wait_ge(cst_done, 8 * n + 2 * r + 2)
                    settle(dve)
                    for s in range(2):
                        nc.vector.bn_aggr(cmv[:, r, s], cst6[:, r, s]).then_inc(cmv_ready, 1)

                def first_moments(n, q):
                    dve.wait_ge(x1_ready, 2 * n + q + 1)
                    moments(n, 2 * q, [x1_next[:, 2 * q + s] for s in range(2)])

                def normalise(n, r, out, tiles, done):
                    dve.wait_ge(crstd_ready, 4 * n + r + 1)
                    for s in range(2):
                        nc.vector.tensor_scalar(out[:, 2 * (r // 2) + s], tiles[:, 2 * (r // 2) + s], cmv[:, r, s, 0:1], crstd[:, r, s:s + 1],
                                                ALU.subtract, ALU.mult).then_inc(done, 1)

                def first_norm(n, q):
                    normalise(n, 2 * q, xf, x1_next, xf_ready)
                    dve.wait_ge(xf_ready, 4 * n + 2 * q + 2)
                    moments(n, 2 * q + 1, [xf[:, 2 * q + s] for s in range(2)])

                def second_norm(n, q):
                    normalise(n, 2 * q + 1, xn, xf, xn_ready)

                def low(out, whole, high, done):
                    nc.vector.tensor_tensor(out, whole, high.bitcast(fp32), ALU.subtract).then_inc(done, 1)

                def attended(n, q):
                    dve.wait_ge(att_done, 2 * n + q + 1)
                    dve.wait_ge(xfa_ready, 4 * n + 2 * q + 2)
                    nc.vector.tensor_tensor(xa[:, 2 * q:2 * q + 2], ap_ps[:, :].rearrange("p (t d) -> p t d", t=2), xfa[:, 2 * q:2 * q + 2],
                                            ALU.add).then_inc(xa_ready, 1)

                def low_attended(n, q):
                    dve.wait_ge(nthi_ready, 2 * n + q + 1)
                    low(nT_lo[:, :, :, :], xt_ps[:, :].rearrange("p (t k c) -> p t k c", t=2, k=KD), nT_hi[:, :, :, :], ntlo_ready)

                def low_result(n, q):
                    dve.wait_ge(uthi_ready, 2 * n + q + 1)
                    low(uT_lo[:, :, :, :], xt_ps[:, :].rearrange("p (t k c) -> p t k c", t=2, k=KD), uT_hi[:, :, :, :], utlo_ready)

                def low_input(n, q):
                    dve.wait_ge(xthi_ready, 2 * n + q + 1)
                    low(xT_lo[:, :, q * RUN:(q + 1) * RUN].rearrange("p k (t c) -> p k t c", t=2),
                        (xt_ps, vp_ps)[q][:, :].rearrange("p (t k c) -> p k t c", t=2, k=KD),
                        xT_hi[:, :, q * RUN:(q + 1) * RUN].rearrange("p k (t c) -> p k t c", t=2), xtlo_ready)

                def last_bias(e, m):
                    dve.wait_ge(z_done, 2 * e + m + 1)
                    wait(dve, zg_ready, 2 * e + m - 1)
                    for s in range(2):
                        nc.vector.tensor_tensor(zt[:, m, s], last_layer_bank(e, m)[:, s * D:(s + 1) * D], nextb_b[:, :], ALU.add).then_inc(zt_ready, 1)

                def part(e, j, here=True, ahead=True, past=True, beyond=True):
                    n = e + 1
                    if ahead and j == 0:
                        low_result(n, 0)
                    if ahead and j == 5:
                        low_attended(n, 0)
                    if here:
                        dve.wait_ge(hhi_ready, 8 * e + j + 1)
                        low(h_lo[:, j % HR], hf[:, j % HR], h_hi[:, j % HR], hlo_ready)
                    if past and j in (1, 3):
                        last_bias(e - 1, j // 2)
                    if ahead:
                        if j == 1:
                            combine(n, 0)
                            combine(n, 1)
                            low_result(n, 1)
                            residual(n, 0)
                            first_moments(n, 0)
                        if j == 2:
                            combine(n, 2)
                            combine(n, 3)
                            residual(n, 1)
                            first_norm(n, 0)
                            first_moments(n, 1)
                        if j == 3:
                            second_norm(n, 0)
                            first_norm(n, 1)
                        if j == 4:
                            second_norm(n, 1)
                        if j == 6:
                            attended(n, 0)
                            low_attended(n, 1)
                        if j == 7:
                            attended(n, 1)

                def finish(e, here=True, ahead=True, past=True, beyond=True):
                    n = e + 1
                    if ahead:
                        low_input(n, 0)
                        low_input(n, 1)
                    if here:
                        for k in range(KD):
                            dve.wait_ge(yhi_ready, 2 * e + k + 1)
                            low(y_lo[:, k], yf[:, k], y_hi[:, k], ylo_ready)
                    if is_tile(e, E):
                        for m in range(2):
                            dve.wait_ge(zg_ready, 2 * (E - 1) + m + 1)
                            dve.wait_ge(out_stored[m], 16 * (E - 1))
                            dve.wait_ge(x1_moved, 16 * E)
                            nc.vector.tensor_tensor(o4[:, m], zg[:, m], x1_here[:, 2 * m:2 * m + 2], ALU.add).then_inc(o_ready, 1)

                def beside(t, c):
                    if is_tile(t, NT - 2) and c == 6:
                        low_result(0, 0)
                    if not is_tile(t, NT - 1):
                        return
                    if c == -1:
                        combine(0, 0)
                        combine(0, 1)
                        low_result(0, 1)
                    if c == 0:
                        residual(0, 0)
                        first_moments(0, 0)
                        combine(0, 2)
                        combine(0, 3)
                    if c == 1:
                        first_norm(0, 0)
                    if c == 2:
                        residual(0, 1)
                        first_moments(0, 1)
                    if c == 3:
                        second_norm(0, 0)
                        first_norm(0, 1)
                    if c == 4:
                        low_attended(0, 0)
                        second_norm(0, 1)
                    if c == 5:
                        attended(0, 0)
                        low_attended(0, 1)
                    if c == 6:
                        low_input(0, 0)
                        attended(0, 1)
                    if c == 7:
                        low_input(0, 1)

                def body(e, here=True, ahead=True, past=True, beyond=True):
                    for j in range(HB):
                        part(e, j, here, ahead, past, beyond)
                    finish(e, here, ahead, past, beyond)
                steps(dve, step)
                bodies(dve, body)

            @block.scalar
            def _(act):
                def q_high(n):
                    act.wait_ge(q_loaded, 16 * n + 16)
                    wait(act, score_done, 8 * n)
                    nc.scalar.activation(q_hi[:, :, :], q_in[:, :, :], ACT.Copy).then_inc(qhi_ready, 1)

                def exponentials(part):
                    span = slice(part * 2 * CH, (part + 1) * 2 * CH)
                    nc.scalar.activation(scores[:, span], scores[:, span], ACT.Exp, bias=neg_top[:, :],
                                         accum_out=sums[:, part:part + 1]).then_inc(exp_done, 1)

                def step(t, here=True, ahead=True, after=True):
                    n = t + 1
                    beside(t, -1)
                    if here:
                        for c in range(NC):
                            act.wait_ge(pt_done, 8 * t + c + 1)
                            wait(act, pv_done, 8 * t + c - 1)
                            nc.scalar.activation(p_hi[:, c % 2], pt_ps[c % 2][:, :], ACT.Copy).then_inc(phi_ready, 1)
                            if c < 2:
                                exponentials(2 + c)
                            if c == 1:
                                nc.scalar.activation(sums[:, 4:6], tops[:, NC:NC + 2], ACT.Exp, bias=neg_top[:, :]).then_inc(extra_exp, 1)
                            beside(t, c)
                    if after:
                        q_high(t + 2)
                    if ahead:
                        act.wait_ge(top_ready, n + 1)
                        exponentials(0)
                    if here:
                        act.wait_ge(pv_done, 8 * t + 8)
                        act.wait_ge(rden_ready, t + 1)
                        nc.scalar.activation(u_part[:, :], u_ps[:, D:2 * D], ACT.Copy, scale=rden[:, :]).then_inc(upart_ready, 1)
                    if ahead:
                        exponentials(1)

                def high(out, whole, done):
                    nc.scalar.activation(out, whole, ACT.Copy).then_inc(done, 1)

                def high_weights(e, j):
                    act.wait_ge(raw_in[j // 2], 16 * e + 16)
                    wait(act, fc2_done, 8 * e + j - 7)
                    high(e_hi[:, j], raw[:, j], ehi_ready)

                def high_result(n, q):
                    act.wait_ge(ut_done, 2 * n + q + 1)
                    wait(act, proj_done, 4 * n + 2 * q)
                    high(uT_hi[:, :, :, :], xt_ps[:, :].rearrange("p (t k c) -> p t k c", t=2, k=KD), uthi_ready)

                def high_attended(n, q):
                    act.wait_ge(nt_done, 2 * n + q + 1)
                    wait(act, att_done, 2 * n + q)
                    high(nT_hi[:, :, :, :], xt_ps[:, :].rearrange("p (t k c) -> p t k c", t=2, k=KD), nthi_ready)

                def high_input(n, q):
                    act.wait_ge(xt_done, 2 * n + q + 1)
                    wait(act, fc1_done, 8 * n)
                    high(xT_hi[:, :, q * RUN:(q + 1) * RUN].rearrange("p k (t c) -> p k t c", t=2),
                         (xt_ps, vp_ps)[q][:, :].rearrange("p (t k c) -> p k t c", t=2, k=KD), xthi_ready)

                def last_gelu(e, m):
                    act.wait_ge(zt_ready, 4 * e + 2 * m + 2)
                    wait(act, o_ready, 2 * e + m - 1)
                    nc.scalar.activation(zg[:, m], zt[:, m], ACT.Gelu).then_inc(zg_ready, 1)

                def high_masked(n):
                    act.wait_ge(mt_loaded, 32 * n + 32)
                    wait(act, proj_done, 4 * n)
                    high(mT_hi[:, :, :], mT[:, :, :], mthi_ready)

                def part(e, j, here=True, ahead=True, past=True, beyond=True):
                    n = e + 1
                    if ahead and j == 0:
                        high_result(n, 0)
                    if here:
                        if isinstance(e, int) and e == j == 0:
                            act.wait_ge(u_stored, 16 * NT)
                        act.wait_ge(fc1_done, 8 * e + j + 1)
                        wait(act, fc2_done, 8 * e + j + 1 - HR)
                        nc.scalar.activation(hf[:, j % HR], h_ps[j % 2][:, :], ACT.Gelu,
                                             bias=b1_c[:, bass.ds(8 * e + j, 1)]).then_inc(gelu_done, 1)
                        act.wait_ge(gelu_done, 8 * e + j + 1)
                        high(h_hi[:, j % HR], hf[:, j % HR], hhi_ready)
                        if j < WLEFT:
                            high_weights(e, HB - WLEFT + j)
                    if ahead:
                        if j == 1:
                            high_result(n, 1)
                        if j == 5:
                            high_attended(n, 0)
                        if j == 6:
                            high_attended(n, 1)
                        if j >= WLEFT:
                            high_weights(n, j - WLEFT)
                    if past and j in (2, 4):
                        last_gelu(e - 1, j // 2 - 1)
                    if beyond and j == 6:
                        high_masked(n + 1)

                def finish(e, here=True, ahead=True, past=True, beyond=True):
                    n = e + 1
                    if ahead:
                        high_input(n, 0)
                        high_input(n, 1)
                    if here:
                        for k in range(KD):
                            if k == 0:
                                act.wait_ge(y_half_done, e + 1)
                            else:
                                act.wait_ge(fc2_done, 8 * e + 8)
                            nc.scalar.activation(yf[:, k], y_ps[k][:, :], ACT.Identity, bias=b2_c[:, bass.ds(2 * e + k, 1)]).then_inc(y_ready, 1)
                        wait(act, z_done, 2 * e)
                        for k in range(KD):
                            act.wait_ge(y_ready, 2 * e + k + 1)
                            high(y_hi[:, k], yf[:, k], yhi_ready)

                def beside(t, c):
                    if is_tile(t, NT - 2) and c == 6:
                        high_masked(0)
                        high_result(0, 0)
                    if not is_tile(t, NT - 1):
                        return
                    if c == -1:
                        high_result(0, 1)
                    if c == 2:
                        nc.scalar.activation(table_in[:, :], neg_top[:, :], ACT.Gelu)
                    if c == 4:
                        high_attended(0, 0)
                    if c == 5:
                        high_attended(0, 1)
                    if c == 6:
                        act.wait_ge(bias_ready, 4 * NT)
                        high_input(0, 0)
                        act.wait_ge(pv_done, 8 * t + 4)
                        high_weights(0, 0)
                    if c == 7:
                        high_input(0, 1)
                        high_weights(0, 1)

                def body(e, here=True, ahead=True, past=True, beyond=True):
                    for j in range(HB):
                        part(e, j, here, ahead, past, beyond)
                    finish(e, here, ahead, past, beyond)
                act.wait_ge(attg_ready, 2)
                for n in range(4):
                    nc.scalar.activation(w_hi[:, n], w_raw[:, n], ACT.Copy).then_inc(whi_ready, 1)
                steps(act, step)
                high_masked(1)
                for j in range(2, HB - WLEFT):
                    high_weights(0, j)
                act.wait_ge(b_loaded, 32)
                bodies(act, body)

            @block.tensor
            def _(pe):
                def weigh(t, c):
                    pe.wait_ge(plo_ready, 8 * t + c + 1)
                    if c == 0:
                        wait(pe, u_ready, t)
                    for j in range(TG):
                        js = slice(j * P, (j + 1) * P)
                        nc.tensor.matmul(u_ps[:, :], p_hi[:, c % 2, js], v_sp[:, c * TG + j, :], start=c + j == 0, stop=False)
                        last = nc.tensor.matmul(u_ps[:, 0:D], p_lo[:, c % 2, js], v_sp[:, c * TG + j, 0:D],
                                                start=False, stop=c * TG + j == NT - 1)
                    last.then_inc(pv_done, 1)

                def step(t, here=True, ahead=True, after=True):
                    n = t + 1
                    beside(t, -1)
                    for c in range(NC):
                        if here:
                            if c % 2 == 0:
                                pe.wait_ge(exp_done, 4 * t + c // 2 + 1)
                            wait(pe, plo_ready, 8 * t + c - 1)
                            for j in range(TG):
                                last = nc.tensor.transpose(pt_ps[c % 2][:, j * P:(j + 1) * P],
                                                           scores[:, (c * TG + j) * P:(c * TG + j + 1) * P], ident[:, :])
                            last.then_inc(pt_done, 1)
                        if ahead:
                            if c == 0:
                                pe.wait_ge(qlo_ready, n + 1)
                            wait(pe, score_masked, 8 * n + c - 1)
                            cs = slice(c * CH, (c + 1) * CH)
                            split_product(nc, s_ps[c % 2][:, :], [(q_hi[:, k], q_lo[:, k]) for k in range(KD)],
                                          [(lnT_hi[:, k, cs], lnT_lo[:, k, cs]) for k in range(KD)]).then_inc(score_done, 1)
                        if here and c > 0:
                            weigh(t, c - 1)
                        beside(t, c)
                    if here:
                        weigh(t, NC - 1)

                def parts(hi, lo, index, what):
                    return [(hi[(slice(None), index, k, what)], lo[(slice(None), index, k, what)]) for k in range(KD)]

                def turn(bank, tile, s):
                    for k in range(KD):
                        last = nc.tensor.transpose(bank[:, (KD * s + k) * P:(KD * s + k + 1) * P], tile[:, k * P:(k + 1) * P], ident[:, :])
                    return last

                def turn_results(n, q):
                    if q == 0:
                        pe.wait_ge(u_loaded, 32 * n + 32)
                        wait(pe, xtlo_ready, 2 * n - 1)
                    else:
                        pe.wait_ge(utlo_ready, 2 * n + 1)
                    for s in range(2):
                        last = turn(xt_ps, u4[:, 2 * q + s], s)
                    last.then_inc(ut_done, 1)

                def project(n, tt):
                    if tt % 2 == 0:
                        pe.wait_ge(utlo_ready, 2 * n + tt // 2 + 1)
                    if tt == 0:
                        pe.wait_ge(mtlo_ready, n + 1)
                        wait(pe, xtlo_ready, 2 * n)
                    elif tt == 1:
                        wait(pe, xa_ready, 2 * n)
                    else:
                        pe.wait_ge(vp_taken, 4 * n + tt - 1)
                    ts = slice(tt * P, (tt + 1) * P)
                    bank = (vp_ps, ap_ps)[tt % 2]
                    split_product(nc, bank[:, 0:D], parts(uT_hi, uT_lo, tt % 2, slice(None)), parts(w_hi, w_lo, WLV, slice(None)))
                    split_product(nc, bank[:, D:2 * D], [(mT_hi[:, k, ts], mT_lo[:, k, ts]) for k in range(KD)],
                                  parts(w_hi, w_lo, WEV, slice(None))).then_inc(proj_done, 1)

                def turn_normed(n, q):
                    pe.wait_ge(xn_ready, 4 * n + 2 * q + 2)
                    if q == 0:
                        pe.wait_ge(utlo_ready, 2 * n + 2)
                    else:
                        pe.wait_ge(ntlo_ready, 2 * n + 1)
                    for s in range(2):
                        last = turn(xt_ps, xn[:, 2 * q + s], s)
                    last.then_inc(nt_done, 1)

                def attend(n, q):
                    pe.wait_ge(ntlo_ready, 2 * n + q + 1)
                    if q == 0:
                        pe.wait_ge(vp_taken, 4 * n + 4)
                    else:
                        pe.wait_ge(xa_ready, 2 * n + 1)
                    for s in range(2):
                        last = split_product(nc, ap_ps[:, s * D:(s + 1) * D], parts(nT_hi, nT_lo, s, slice(None)),
                                             parts(w_hi, w_lo, WATT, slice(None)))
                    last.then_inc(att_done, 1)

                def turn_attended(n, q):
                    pe.wait_ge(xa_ready, 2 * n + q + 1)
                    if q == 0:
                        pe.wait_ge(ntlo_ready, 2 * n + 2)
                    else:
                        pe.wait_ge(vp_taken, 4 * n + 3)
                    for s in range(2):
                        last = turn((xt_ps, vp_ps)[q], xa[:, 2 * q + s], s)
                    last.then_inc(xt_done, 1)

                def first_layer(e, j):
                    pe.wait_ge(elo_ready, 8 * e + j + 1)
                    if j == 0:
                        pe.wait_ge(xtlo_ready, 2 * e + 2)
                    wait(pe, gelu_done, 8 * e + j - 1)
                    split_product(nc, h_ps[j % 2][:, :],
                                  [(e_hi[:, j, k * P:(k + 1) * P], e_lo[:, j, k * P:(k + 1) * P]) for k in range(KD)],
                                  [(xT_hi[:, k], xT_lo[:, k]) for k in range(KD)]).then_inc(fc1_done, 1)

                def second_layer(e, j):
                    pe.wait_ge(hlo_ready, 8 * e + j + 1)
                    if j == 0:
                        wait(pe, y_ready, 2 * e)
                    for k in range(KD):
                        ks = slice(D + k * P, D + (k + 1) * P)
                        last = split_product(nc, y_ps[k][:, :], [(e_hi[:, j, ks], e_lo[:, j, ks])],
                                             [(h_hi[:, j % HR], h_lo[:, j % HR])], start=j == 0, stop=j == HB - 1)
                        if j == HB - 1 and k == 0:
                            last.then_inc(y_half_done, 1)
                    last.then_inc(fc2_done, 1)

                def last_layer(e, m):
                    if m == 0:
                        pe.wait_ge(ylo_ready, 2 * e + 2)
                    bank = last_layer_bank(e, m)
                    if bank is zp_ps:
                        wait(pe, zt_ready, 4 * e + 2 * m)
                    for s in range(2):
                        ts = slice((2 * m + s) * P, (2 * m + s + 1) * P)
                        last = split_product(nc, bank[:, s * D:(s + 1) * D],
                                             [(y_hi[:, k, ts], y_lo[:, k, ts]) for k in range(KD)],
                                             parts(w_hi, w_lo, WNEXT, slice(None)))
                    last.then_inc(z_done, 1)

                def part(e, j, here=True, ahead=True, past=True, beyond=True):
                    n = e + 1
                    if here:
                        first_layer(e, j)
                        if 1 < j < HB - 1:
                            second_layer(e, j - 2)
                    if past and j in (1, 3):
                        last_layer(e - 1, j // 2)
                    if ahead:
                        if j == 0:
                            turn_results(n, 0)
                        if j == 1:
                            project(n, 0)
                            project(n, 1)
                            turn_results(n, 1)
                        if j == 2:
                            project(n, 2)
                            project(n, 3)
                        if j == 5:
                            turn_normed(n, 0)
                        if j == 6:
                            attend(n, 0)
                            turn_normed(n, 1)
                        if j == 7:
                            attend(n, 1)
                    if here and j == HB - 1:
                        second_layer(e, HB - 3)
                    if ahead and j == HB - 1:
                        turn_attended(n, 0)
                        turn_attended(n, 1)

                def finish(e, here=True, ahead=True, past=True, beyond=True):
                    n = e + 1
                    if here:
                        second_layer(e, HB - 2)
                        second_layer(e, HB - 1)

                def beside(t, c):
                    if is_tile(t, NT - 2) and c == 6:
                        turn_results(0, 0)
                    if not is_tile(t, NT - 1):
                        return
                    if c == -1:
                        pe.wait_ge(wlo_ready, 4)
                        project(0, 0)
                        project(0, 1)
                        turn_results(0, 1)
                    if c == 0:
                        project(0, 2)
                        project(0, 3)
                    if c == 4:
                        turn_normed(0, 0)
                    if c == 5:
                        attend(0, 0)
                        turn_normed(0, 1)
                    if c == 6:
                        turn_attended(0, 0)
                        attend(0, 1)
                    if c == 7:
                        turn_attended(0, 1)

                def body(e, here=True, ahead=True, past=True, beyond=True):
                    for j in range(HB):
                        part(e, j, here, ahead, past, beyond)
                    finish(e, here, ahead, past, beyond)
                steps(pe, step)
                bodies(pe, body)


def kernel(**inputs):
    import numpy as np
    import concourse.bacc as bacc
    from concourse.bass_utils import run_bass_kernel_spmd

    def g(name):
        return np.asarray(inputs[name])

    def rows_to_columns(a, blocks):
        return a.reshape(-1, blocks, P).transpose(2, 0, 1).reshape(P, -1)

    fc1 = g("L0_ffn_fc1_w").reshape(E, HB, P, KD, P).transpose(0, 4, 1, 3, 2).reshape(E, P, HB, D)
    fc2 = g("L0_ffn_fc2_w").reshape(E, D, HB, P).transpose(0, 3, 2, 1)
    arrays = {
        "x": g("x"), "mx": g("L0_gnn_masked_x"), "mxT": g("L0_gnn_masked_x").T, "adj": g("adj"),
        "wlqT": g("L0_gnn_Wlq").T, "wlkT": g("L0_gnn_Wlk").T, "wgkT": g("L0_gnn_Wgk").T, "wgqT": g("L0_gnn_Wgq").T,
        "wgv": g("L0_gnn_Wgv"), "bgv": g("L0_gnn_bgv"), "wes": g("L0_gnn_Wes").reshape(D), "wlv": g("L0_gnn_Wlv"),
        "blv": g("L0_gnn_blv"), "wev": g("L0_gnn_Wev"), "bev": g("L0_gnn_bev"),
        "ln_g": rows_to_columns(g("L0_ffn_ln_g")[None], KD), "ln_b": rows_to_columns(g("L0_ffn_ln_b")[None], KD),
        "attn_wT": g("L0_ffn_attn_w").T, "attn_b": g("L0_ffn_attn_b"), "next_wT": g("L0_ffn_next_w").T, "next_b": g("L0_ffn_next_b"),
        "b1": rows_to_columns(g("L0_ffn_fc1_b"), HB), "b2": rows_to_columns(g("L0_ffn_fc2_b"), KD),
        "wffn": np.concatenate([fc1, fc2], axis=3),
    }
    nc = bacc.Bacc("TRN2", target_bir_lowering=False, num_devices=1)
    fed, args = {}, []
    for name, a in arrays.items():
        fed[f"in_{name}"] = np.ascontiguousarray(a)
        args.append(nc.dram_tensor(f"in_{name}", a.shape, mybir.dt.from_np(a.dtype), kind="ExternalInput").ap())
    args.append(nc.dram_tensor("result", (N, D), fp32, kind="ExternalOutput").ap())
    gnn_moe_kernel(nc, *args)
    r = run_bass_kernel_spmd(nc, [fed], core_ids=[0])
    return r.results[0]["result"]
```
